# Optimizing a Trainium2 kernel written in Bass

```python
import numpy as np
import jax
import jax.numpy as jnp

def _softmax(x, axis=-1):
    return jax.nn.softmax(x, axis=axis)

def _gelu(x):
    return jax.nn.gelu(x, approximate=True)

def _silu(x):
    return jax.nn.silu(x)

def _sigmoid(x):
    return jax.nn.sigmoid(x)

def _layernorm(x, axis=-1, eps=1e-05):
    m = jnp.mean(x, axis=axis, keepdims=True)
    v = jnp.var(x, axis=axis, keepdims=True)
    return (x - m) / jnp.sqrt(v + eps)

def _scatter_add(tgt, idx, src, axis=0):
    return tgt.at[idx].add(src)

def _segment_sum(src, seg, n):
    return jax.ops.segment_sum(src, seg, n)
kernel_name = 'mk_adaln_attn_ffn_d1_seqx_r8_1b65b6'

def setup_inputs(seed: int=0):
    np.random.seed(seed)
    _w = jnp.asarray

    def _rec_inputs():
        import jax
        import jax.numpy as jnp
        _rk = jax.random.key(seed)
        x = -5.13e-06 + 0.01765 * jax.random.normal(jax.random.fold_in(_rk, 1), (4, 256, 128), jnp.float32)
        _lenS = 256 - jax.random.randint(jax.random.fold_in(_rk, 7), (4,), 0, max(1, 256 // 4) + 1, jnp.int32)
        _lenS2 = 256 - jax.random.randint(jax.random.fold_in(_rk, 8), (4,), 0, max(1, 256 // 4) + 1, jnp.int32)
        cond_1024 = 0.0061147 + 1.02565 * jax.random.normal(jax.random.fold_in(_rk, 11), (4, 128), jnp.float32)
        return (x, cond_1024)
    x, cond_1024 = _rec_inputs()

    def _L0_cond_setup():
        import math
        import jax, jax.numpy as jnp
        import numpy as np
        EPS = 1e-07
        MAX_TANH_ARG = 1.0 - 1e-05

        def _norm(x):
            return jnp.sqrt(jnp.sum(x * x, axis=-1, keepdims=True)).clip(EPS)

        def logmap0(x):
            n = _norm(x)
            return jnp.arctanh(jnp.clip(n, EPS, MAX_TANH_ARG)) * x / n

        def expmap0(v):
            n = _norm(v)
            return jnp.tanh(n) * v / n

        def mobius_add(x, y):
            x2 = jnp.sum(x * x, -1, keepdims=True)
            y2 = jnp.sum(y * y, -1, keepdims=True)
            xy = jnp.sum(x * y, -1, keepdims=True)
            num = (1 + 2 * xy + y2) * x + (1 - x2) * y
            den = (1 + 2 * xy + x2 * y2).clip(EPS)
            return num / den

        def plin(x, w, b):
            return expmap0(logmap0(x) @ w + b)

        def layer_norm(x, eps=1e-06):
            m = x.mean(-1, keepdims=True)
            v = ((x - m) ** 2).mean(-1, keepdims=True)
            return (x - m) / jnp.sqrt(v + eps)

        def _beta(a, b):
            return math.exp(math.lgamma(a) + math.lgamma(b) - math.lgamma(a + b))
        D, H, FF = (128, 16, 512)
        HD = D // H
        BETA_N = _beta(D / 2, 0.5)
        BETA_H = _beta(HD / 2, 0.5)

        def _to_heads(p):
            B, S, _ = p.shape
            t = logmap0(p).reshape(B, S, H, HD) * (BETA_H / BETA_N)
            return expmap0(jnp.transpose(t, (0, 2, 1, 3)))

        def _from_heads(ph):
            B, _, S, _ = ph.shape
            t = logmap0(ph) * (BETA_N / BETA_H)
            t = jnp.transpose(t, (0, 2, 1, 3)).reshape(B, S, D)
            return expmap0(t)
        key = jax.random.key(seed)
        ks = jax.random.split(key, 20)
        B, S = (4, 128)
        x = expmap0(0.02 * jax.random.normal(ks[0], (B, S, D), jnp.float32))
        t_emb = jax.random.normal(ks[1], (B, 1, D), jnp.float32)
        g = lambda k, sh: 0.02 * jax.random.normal(k, sh, jnp.float32)
        return {'x': x, 't_emb': t_emb, 'w_q': g(ks[2], (D, D)), 'b_q': jnp.zeros((D,), jnp.float32), 'w_k': g(ks[3], (D, D)), 'b_k': jnp.zeros((D,), jnp.float32), 'w_v': g(ks[4], (D, D)), 'b_v': jnp.zeros((D,), jnp.float32), 'w_o': g(ks[5], (D, D)), 'b_o': jnp.zeros((D,), jnp.float32), 'w_f1': g(ks[6], (D, FF)), 'b_f1': jnp.zeros((FF,), jnp.float32), 'w_f2': g(ks[7], (FF, D)), 'b_f2': jnp.zeros((D,), jnp.float32), 'w_ada': g(ks[8], (D, 6 * D)), 'b_ada': jnp.zeros((6 * D,), jnp.float32)}
    _L0_cond_all = _L0_cond_setup()
    _L0_cond_in = {k: v for k, v in _L0_cond_all.items() if k in ('w_q', 'b_q', 'w_k', 'b_k', 'w_v', 'b_v', 'w_o', 'b_o', 'w_f1', 'b_f1', 'w_f2', 'b_f2', 'w_ada', 'b_ada')}
    del _L0_cond_all

    def _L0_attn_setup():
        import math
        import jax, jax.numpy as jnp
        import numpy as np
        D_MODEL = 128
        N_HEADS = 16
        D_K = D_MODEL // N_HEADS
        D_C = 32
        B, S = (2, 256)
        key = jax.random.key(seed)
        ks = jax.random.split(key, 7)
        sd = lambda fan_in: 1.0 / math.sqrt(fan_in)
        return {'x': jax.random.normal(ks[0], (B, S, D_MODEL), dtype=jnp.float32), 'W_dq': jax.random.uniform(ks[1], (D_MODEL, D_C), minval=-sd(D_MODEL), maxval=sd(D_MODEL), dtype=jnp.float32), 'W_uq': jax.random.uniform(ks[2], (D_C, N_HEADS * D_K), minval=-sd(D_C), maxval=sd(D_C), dtype=jnp.float32), 'W_dkv': jax.random.uniform(ks[3], (D_MODEL, D_C), minval=-sd(D_MODEL), maxval=sd(D_MODEL), dtype=jnp.float32), 'W_uk': jax.random.uniform(ks[4], (D_C, N_HEADS * D_K), minval=-sd(D_C), maxval=sd(D_C), dtype=jnp.float32), 'W_uv': jax.random.uniform(ks[5], (D_C, N_HEADS * D_K), minval=-sd(D_C), maxval=sd(D_C), dtype=jnp.float32), 'W_o': jax.random.uniform(ks[6], (N_HEADS * D_K, D_MODEL), minval=-sd(N_HEADS * D_K), maxval=sd(N_HEADS * D_K), dtype=jnp.float32)}
    _L0_attn_all = _L0_attn_setup()
    _L0_attn_in = {k: v for k, v in _L0_attn_all.items() if k in ('W_dq', 'W_uq', 'W_dkv', 'W_uk', 'W_uv', 'W_o')}
    del _L0_attn_all

    def _L0_cond2_setup():
        import jax, jax.numpy as jnp
        import numpy as np
        import math
        N, T, D, H = (64, 64, 128, 128)
        key = jax.random.key(seed)
        k1, k2, k3, k4 = jax.random.split(key, 4)
        x = jax.random.normal(k1, (N, T, D), dtype=jnp.float32)
        h0 = jax.random.normal(k2, (N, H), dtype=jnp.float32)
        Wx = jax.random.normal(k3, (D, 4 * H), dtype=jnp.float32) / math.sqrt(D)
        Wh = jax.random.normal(k4, (H, 4 * H), dtype=jnp.float32) / math.sqrt(H)
        b = jnp.zeros((4 * H,), dtype=jnp.float32)
        return {'x': x, 'h0': h0, 'Wx': Wx, 'Wh': Wh, 'b': b}
    _L0_cond2_all = _L0_cond2_setup()
    _L0_cond2_in = {k: v for k, v in _L0_cond2_all.items() if k in ('Wx', 'Wh', 'b')}
    del _L0_cond2_all

    def _L0_ffn_setup():
        import jax, jax.numpy as jnp
        import numpy as np
        N_EMBD = 128
        N_STATE = 512
        key = jax.random.key(seed)
        k_x, k_w1, k_b1, k_w2, k_b2 = jax.random.split(key, 5)
        x = jax.random.normal(k_x, (4, 256, N_EMBD), dtype=jnp.float32)
        w1 = jax.random.normal(k_w1, (N_EMBD, N_STATE), dtype=jnp.float32) * (1.0 / np.sqrt(N_EMBD))
        b1 = jax.random.normal(k_b1, (N_STATE,), dtype=jnp.float32) * 0.02
        w2 = jax.random.normal(k_w2, (N_STATE, N_EMBD), dtype=jnp.float32) * (1.0 / np.sqrt(N_STATE))
        b2 = jax.random.normal(k_b2, (N_EMBD,), dtype=jnp.float32) * 0.02
        return {'x': x, 'w1': w1, 'b1': b1, 'w2': w2, 'b2': b2}
    _L0_ffn_all = _L0_ffn_setup()
    _L0_ffn_in = {k: v for k, v in _L0_ffn_all.items() if k in ('w1', 'b1', 'w2', 'b2')}
    del _L0_ffn_all
    return {'x': x, 'cond_1024': cond_1024, 'L0_cond_w_q': _L0_cond_in['w_q'], 'L0_cond_b_q': _L0_cond_in['b_q'], 'L0_cond_w_k': _L0_cond_in['w_k'], 'L0_cond_b_k': _L0_cond_in['b_k'], 'L0_cond_w_v': _L0_cond_in['w_v'], 'L0_cond_b_v': _L0_cond_in['b_v'], 'L0_cond_w_o': _L0_cond_in['w_o'], 'L0_cond_b_o': _L0_cond_in['b_o'], 'L0_cond_w_f1': _L0_cond_in['w_f1'], 'L0_cond_b_f1': _L0_cond_in['b_f1'], 'L0_cond_w_f2': _L0_cond_in['w_f2'], 'L0_cond_b_f2': _L0_cond_in['b_f2'], 'L0_cond_w_ada': _L0_cond_in['w_ada'], 'L0_cond_b_ada': _L0_cond_in['b_ada'], 'L0_attn_W_dq': _L0_attn_in['W_dq'], 'L0_attn_W_uq': _L0_attn_in['W_uq'], 'L0_attn_W_dkv': _L0_attn_in['W_dkv'], 'L0_attn_W_uk': _L0_attn_in['W_uk'], 'L0_attn_W_uv': _L0_attn_in['W_uv'], 'L0_attn_W_o': _L0_attn_in['W_o'], 'L0_cond2_Wx': _L0_cond2_in['Wx'], 'L0_cond2_Wh': _L0_cond2_in['Wh'], 'L0_cond2_b': _L0_cond2_in['b'], 'L0_ffn_w1': _L0_ffn_in['w1'], 'L0_ffn_b1': _L0_ffn_in['b1'], 'L0_ffn_w2': _L0_ffn_in['w2'], 'L0_ffn_b2': _L0_ffn_in['b2']}

def reference(x, cond_1024, L0_cond_w_q, L0_cond_b_q, L0_cond_w_k, L0_cond_b_k, L0_cond_w_v, L0_cond_b_v, L0_cond_w_o, L0_cond_b_o, L0_cond_w_f1, L0_cond_b_f1, L0_cond_w_f2, L0_cond_b_f2, L0_cond_w_ada, L0_cond_b_ada, L0_attn_W_dq, L0_attn_W_uq, L0_attn_W_dkv, L0_attn_W_uk, L0_attn_W_uv, L0_attn_W_o, L0_cond2_Wx, L0_cond2_Wh, L0_cond2_b, L0_ffn_w1, L0_ffn_b1, L0_ffn_w2, L0_ffn_b2):
    import jax
    import jax.numpy as jnp

    def _L0_cond_ref(x, t_emb, w_q, b_q, w_k, b_k, w_v, b_v, w_o, b_o, w_f1, b_f1, w_f2, b_f2, w_ada, b_ada):
        import math
        import jax, jax.numpy as jnp
        import numpy as np
        EPS = 1e-07
        MAX_TANH_ARG = 1.0 - 1e-05

        def _norm(x):
            return jnp.sqrt(jnp.sum(x * x, axis=-1, keepdims=True)).clip(EPS)

        def logmap0(x):
            n = _norm(x)
            return jnp.arctanh(jnp.clip(n, EPS, MAX_TANH_ARG)) * x / n

        def expmap0(v):
            n = _norm(v)
            return jnp.tanh(n) * v / n

        def mobius_add(x, y):
            x2 = jnp.sum(x * x, -1, keepdims=True)
            y2 = jnp.sum(y * y, -1, keepdims=True)
            xy = jnp.sum(x * y, -1, keepdims=True)
            num = (1 + 2 * xy + y2) * x + (1 - x2) * y
            den = (1 + 2 * xy + x2 * y2).clip(EPS)
            return num / den

        def plin(x, w, b):
            return expmap0(logmap0(x) @ w + b)

        def layer_norm(x, eps=1e-06):
            m = x.mean(-1, keepdims=True)
            v = ((x - m) ** 2).mean(-1, keepdims=True)
            return (x - m) / jnp.sqrt(v + eps)

        def _beta(a, b):
            return math.exp(math.lgamma(a) + math.lgamma(b) - math.lgamma(a + b))
        D, H, FF = (128, 16, 512)
        HD = D // H
        BETA_N = _beta(D / 2, 0.5)
        BETA_H = _beta(HD / 2, 0.5)

        def _to_heads(p):
            B, S, _ = p.shape
            t = logmap0(p).reshape(B, S, H, HD) * (BETA_H / BETA_N)
            return expmap0(jnp.transpose(t, (0, 2, 1, 3)))

        def _from_heads(ph):
            B, _, S, _ = ph.shape
            t = logmap0(ph) * (BETA_N / BETA_H)
            t = jnp.transpose(t, (0, 2, 1, 3)).reshape(B, S, D)
            return expmap0(t)
        ada = t_emb @ w_ada + b_ada
        sh_msa, sc_msa, g_msa, sh_mlp, sc_mlp, g_mlp = jnp.split(ada, 6, axis=-1)
        residual = x
        xn = layer_norm(logmap0(x))
        xm = expmap0(xn * (1 + sc_msa) + sh_msa)
        q = _to_heads(plin(xm, w_q, b_q))
        k = _to_heads(plin(xm, w_k, b_k))
        v = _to_heads(plin(xm, w_v, b_v))
        qt, kt, vt = (logmap0(q), logmap0(k), logmap0(v))
        scores = jnp.einsum('bhqd,bhkd->bhqk', qt, kt) / math.sqrt(HD)
        attn = jax.nn.softmax(scores, axis=-1)
        out_h = expmap0(jnp.einsum('bhqk,bhkd->bhqd', attn, vt))
        attn_out = plin(_from_heads(out_h), w_o, b_o)
        attn_t = g_msa * logmap0(attn_out)
        x = mobius_add(residual, expmap0(attn_t))
        residual = x
        xn = layer_norm(logmap0(x))
        xm = expmap0(xn * (1 + sc_mlp) + sh_mlp)
        ff = plin(plin(xm, w_f1, b_f1), w_f2, b_f2)
        ff_t = g_mlp * logmap0(ff)
        return mobius_add(residual, expmap0(ff_t))

    def _L0_attn_ref(x, W_dq, W_uq, W_dkv, W_uk, W_uv, W_o):
        import math
        import jax, jax.numpy as jnp
        import numpy as np
        D_MODEL = 128
        N_HEADS = 16
        D_K = D_MODEL // N_HEADS
        D_C = 32
        B, S = (2, 256)
        Bx, Sx, _ = x.shape
        c_q = x @ W_dq
        Q = (c_q @ W_uq).reshape(Bx, Sx, N_HEADS, D_K)
        c_kv = x @ W_dkv
        K = (c_kv @ W_uk).reshape(Bx, Sx, N_HEADS, D_K)
        V = (c_kv @ W_uv).reshape(Bx, Sx, N_HEADS, D_K)
        scores = jnp.einsum('bqhd,bkhd->bhqk', Q, K) / math.sqrt(D_K)
        causal = jnp.tril(jnp.ones((Sx, Sx), dtype=bool))
        scores = jnp.where(causal, scores, -jnp.inf)
        attn = jax.nn.softmax(scores, axis=-1)
        out = jnp.einsum('bhqk,bkhd->bqhd', attn, V).reshape(Bx, Sx, N_HEADS * D_K)
        return out @ W_o

    def _L0_cond2_ref(x, h0, Wx, Wh, b):
        import jax, jax.numpy as jnp
        import numpy as np
        import math
        N, T, D, H = (64, 64, 128, 128)
        Hdim = h0.shape[1]
        xW = jnp.einsum('ntd,dg->ntg', x, Wx) + b

        def step(carry, xw_t):
            prev_h, prev_c = carry
            a = xw_t + prev_h @ Wh
            i = jax.nn.sigmoid(a[:, :Hdim])
            f = jax.nn.sigmoid(a[:, Hdim:2 * Hdim])
            o = jax.nn.sigmoid(a[:, 2 * Hdim:3 * Hdim])
            g = jnp.tanh(a[:, 3 * Hdim:])
            next_c = f * prev_c + i * g
            next_h = o * jnp.tanh(next_c)
            return ((next_h, next_c), next_h)
        c0 = jnp.zeros_like(h0)
        _, hs = jax.lax.scan(step, (h0, c0), jnp.swapaxes(xW, 0, 1))
        return jnp.swapaxes(hs, 0, 1)

    def _L0_ffn_ref(x, w1, b1, w2, b2):
        import jax, jax.numpy as jnp
        import numpy as np
        N_EMBD = 128
        N_STATE = 512
        h = jax.nn.gelu(jnp.einsum('bse,eh->bsh', x, w1) + b1, approximate=False)
        return jnp.einsum('bsh,he->bse', h, w2) + b2
    x = x + _L0_attn_ref(_L0_cond_ref(x, cond_1024[:, None, :], L0_cond_w_q, L0_cond_b_q, L0_cond_w_k, L0_cond_b_k, L0_cond_w_v, L0_cond_b_v, L0_cond_w_o, L0_cond_b_o, L0_cond_w_f1, L0_cond_b_f1, L0_cond_w_f2, L0_cond_b_f2, L0_cond_w_ada, L0_cond_b_ada), L0_attn_W_dq, L0_attn_W_uq, L0_attn_W_dkv, L0_attn_W_uk, L0_attn_W_uv, L0_attn_W_o)
    x = x + _L0_ffn_ref(_L0_cond2_ref(x, cond_1024, L0_cond2_Wx, L0_cond2_Wh, L0_cond2_b), L0_ffn_w1, L0_ffn_b1, L0_ffn_w2, L0_ffn_b2)
    return x

_drawn_inputs = setup_inputs


def setup_inputs(seed=0):
    import zlib

    import numpy as np

    out = dict(_drawn_inputs(seed))
    spreads = {'L0_cond_b_q': (0.0, 2.0),
     'L0_cond_b_k': (0.0, 2.0),
     'L0_cond_b_v': (0.0, 0.312),
     'L0_cond_b_o': (0.0, 0.1),
     'L0_cond_b_f1': (0.0, 0.1),
     'L0_cond_b_f2': (0.0, 0.1),
     'L0_cond_b_ada': (0.0, 0.1),
     'L0_cond2_b': (0.0, 0.1)}
    factors = {'L0_cond_w_q': 43.429,
     'L0_cond_w_k': 8.0,
     'L0_cond_w_v': 6.6,
     'L0_attn_W_dq': 64.0,
     'L0_attn_W_uq': 64.0,
     'L0_attn_W_uk': 64.0}
    for name, (base, spread) in spreads.items():
        noise = np.random.default_rng([zlib.crc32(name.encode()), seed]).standard_normal(out[name].shape)
        drawn = base * np.exp(spread * noise) if base else spread * noise
        out[name] = jnp.asarray(drawn.astype(out[name].dtype))
    for name, factor in factors.items():
        out[name] = (out[name] * factor).astype(out[name].dtype)
    return out
```

```python
import math
from contextlib import ExitStack

import concourse.bass as bass
from concourse import mybir

ALU = mybir.AluOpType
ACT = mybir.ActivationFunctionType
AX = mybir.AxisListType
F32 = mybir.dt.float32
F16 = mybir.dt.float16
BF16 = mybir.dt.bfloat16

B, S, D, H = 4, 256, 128, 16
HD = D // H
FF = 512
P = 128
HALVES = S // P
TILES = B * HALVES
GROUP = 4
NG = H // GROUP
FC = FF // P
VP = 32

EPS = 1e-7
MAX_TANH_ARG = 1.0 - 1e-5
CLIP = math.atanh(0.9999899864196777)
LN_EPS = 1e-6
TINY = EPS * EPS
SERIES_TO = 0.25


def _beta(a, b):
    return math.exp(math.lgamma(a) + math.lgamma(b) - math.lgamma(a + b))


HEADS_UP = _beta(HD / 2, 0.5) / _beta(D / 2, 0.5)
SCALE = 1.0 / math.sqrt(HD)
MASKED = -1e30

STEPS = 32
CHUNKS = S // STEPS
GW = 4 * B
H_SCALE = 4096.0
W_SCALE = 16.0
A_SCALE = H_SCALE * W_SCALE


def adaln_attention_lstm_ffn(nc, x, cond, w_q, b_q, w_k, b_k, w_v, b_v, w_o, b_o, w_f1, b_f1, w_f2, b_f2,
                             w_ada, b_ada, W_dq, W_uq, W_dkv, W_uk, W_uv, W_o, Wx, Wh, b_g, w1, b1, w2, b2, out):
    with ExitStack() as ctx:
        def sb(name, shape, dt=F32):
            return ctx.enter_context(nc.sbuf_tensor(name, shape, dt))

        def ps(name, shape, dt=F32):
            return ctx.enter_context(nc.psum_tensor(name, shape, dt))

        def sem(name):
            return ctx.enter_context(nc.semaphore(name))

        ident = sb("ident", [P, P])
        identb = sb("identb", [P, P], BF16)
        mask0 = sb("mask0", [P, GROUP, P], BF16)
        mask1 = sb("mask1", [P, 2, S], BF16)
        ones = sb("ones", [1, P])
        cond4 = sb("cond4", [B, D])
        condT = sb("condT", [P, B])
        condB = sb("condB", [P, B, P])
        ada_w = sb("ada_w", [P, 6 * D])
        ada_b = sb("ada_b", [1, 6 * D])
        ada = sb("ada", [P, B, 6, D])
        wqkv = sb("wqkv", [P, 3, D])
        bqkv = sb("bqkv", [P, 3, D])
        wo_c = sb("wo_c", [P, D])
        bo_c = sb("bo_c", [P, D])
        wf1 = sb("wf1", [P, FF])
        bf1_col = sb("bf1_col", [P, FC])
        bf1_row = sb("bf1_row", [1, FF])
        wf2 = sb("wf2", [P, FC, D])
        bf2 = sb("bf2", [P, D])
        wd = sb("wd", [P, 2, 32])
        wu = sb("wu", [32, 3, D])
        wo_m = sb("wo_m", [P, D])
        wx = sb("wx", [P, 4, D])
        wh = sb("wh", [P, 4, D])
        bg = sb("bg", [1, 4, D])
        wha = sb("wha", [P, 4, D], F16)
        whb = sb("whb", [P, 4, D], F16)
        w1s = sb("w1s", [P, FF])
        b1s = sb("b1s", [P, FC])
        w2s = sb("w2s", [P, FC, D])
        b2s = sb("b2s", [1, D])
        x_tb = sb("x_tb", [P, CHUNKS, D])

        x_tm = sb("x_tm", [P, TILES, D])
        ta = sb("ta", [P, TILES, D])
        tb = sb("tb", [P, TILES, D])
        v_tm = sb("v_tm", [P, TILES, D])
        x1_tm = sb("x1_tm", [P, TILES, D])
        o_tm = sb("o_tm", [P, TILES, D])
        vT = sb("vT", [P, TILES, P])
        q_tm = sb("q_tm", [P, 3, TILES, H, HD])
        q_sq = sb("q_sq", [P, 3, TILES, H, HD])
        qT = sb("qT", [P, TILES, P])
        kT = sb("kT", [P, TILES, P])
        qz = sb("qz", [P, H, B * S])
        vaug = sb("vaug", [P, TILES, H, VP])
        hn = sb("hn", [P, 3, TILES, H])
        pT = sb("pT", [P, 2, GROUP * S])
        oTs = sb("oTs", [P, 2, S])
        rd = sb("rd", [P, 2, HALVES, GROUP])
        sm = sb("sm", [P, 24, TILES])
        nq = sb("nq", [P, 3, 3 * TILES])
        hn_x = tb[:].rearrange("p t n -> p (t n)")[:, 0:3 * TILES * H]
        hn_t = tb[:].rearrange("p t n -> p (t n)")[:, 512:512 + 3 * TILES * H]
        cT = q_sq[:].rearrange("p a t h d -> p (a t h d)")[0:32, 0:2 * B * S].rearrange("p (a n) -> p a n", a=2)
        mx = sb("mx", [P, 2, GROUP])

        gates = sb("gates", [P, 2, 5 * B])
        so = sb("so", [P, 2, B])
        pr = sb("pr", [P, 2, 2 * B])
        th = sb("th", [P, 2, B])
        ha = sb("ha", [P, 2, B], F16)
        hb = sb("hb", [P, 2, B], F16)
        h0 = sb("h0", [P, B])
        hist = sb("hist", [P, 2, STEPS, B])
        gel = ta[:].rearrange("p (a f) n -> p a f n", a=2)
        o_sb = tb[:, 0:2, :]

        x1T = vT[:].rearrange("p t n -> p (t n)")
        oT = kT[:].rearrange("p t n -> p (t n)")

        bank = ps("bank", [P, 8, 512])

        ld_x = sem("ld_x")
        ld_ada = sem("ld_ada")
        ld_qkv = sem("ld_qkv")
        ld_cff = sem("ld_cff")
        ld_mla = sem("ld_mla")
        ld_rnn = sem("ld_rnn")
        ld_xtb = sem("ld_xtb")
        consts = sem("consts")
        zeros = sem("zeros")
        dve = sem("dve_chain")
        act_ch = sem("act_chain")
        squares = sem("squares")
        cond_t = sem("cond_t")
        cond_bc = sem("cond_bc")
        ada_mm = sem("ada_mm")
        ada_ready = sem("ada_ready")
        roots_in = sem("roots_in")
        roots_out = sem("roots_out")
        ratio_ready = sem("ratio_ready")
        ln_ready = sem("ln_ready")
        v_ready = sem("v_ready")
        v_turned = sem("v_turned")
        vT_ready = sem("vT_ready")
        qkv_mm = sem("qkv_mm")
        qkv_ready = sem("qkv_ready")
        qk_scaled = sem("qk_scaled")
        q_turned = sem("q_turned")
        qT_ready = sem("qT_ready")
        k_turned = sem("k_turned")
        kT_ready = sem("kT_ready")
        qz_ready = sem("qz_ready")
        vaug_ready = sem("vaug_ready")
        score_mm = sem("score_mm")
        exp_done = sem("exp_done")
        pv_mm = sem("pv_mm")
        o_copied = sem("o_copied")
        o_turned = sem("o_turned")
        o_normed = sem("o_normed")
        oT_mm = sem("oT_mm")
        oT_ready = sem("oT_ready")
        attn_mm = sem("attn_mm")
        tanh_in = sem("tanh_in")
        tanh_out = sem("tanh_out")
        f1_mm = sem("f1_mm")
        f1n_mm = sem("f1n_mm")
        f1_ready = sem("f1_ready")
        f1_norm = sem("f1_norm")
        f2_mm = sem("f2_mm")
        cond_out = sem("cond_out")
        co_turned = sem("co_turned")
        co_ready = sem("co_ready")
        c_mm = sem("c_mm")
        c_ready = sem("c_ready")
        u_mm = sem("u_mm")
        mq_ready = sem("mq_ready")
        mv_mm = sem("mv_mm")
        mv_ready = sem("mv_ready")
        ms_mm = sem("ms_mm")
        mx_ready = sem("mx_ready")
        mp_ready = sem("mp_ready")
        mt_mm = sem("mt_mm")
        mt_ready = sem("mt_ready")
        mpv_mm = sem("mpv_mm")
        mo_copied = sem("mo_copied")
        mo_turned = sem("mo_turned")
        mo_normed = sem("mo_normed")
        moT_mm = sem("moT_mm")
        moT_ready = sem("moT_ready")
        x1_mm = sem("x1_mm")
        x1_ready = sem("x1_ready")
        w_ready = sem("w_ready")
        h_ready = sem("h_ready")
        hb_ready = sem("hb_ready")
        hist_ready = sem("hist_ready")
        xw_ready = sem("xw_ready")
        gates_mm = sem("gates_mm")
        gates_act = sem("gates_act")
        c_new = sem("c_new")
        th_act = sem("th_act")
        ff_mm = sem("ff_mm")
        gel_ready = sem("gel_ready")
        y_mm = sem("y_mm")
        y_ready = sem("y_ready")
        stored = [sem("stored_even"), sem("stored_odd")]

        block = ctx.enter_context(nc.Block())

        x_tiles = x.rearrange("b (h p) d -> p (b h) d", p=P)
        x_steps = x.rearrange("b (c t) d -> b t c d", t=STEPS)
        out_steps = out.rearrange("b (c t) d -> c t b d", t=STEPS)

        def row(a):
            return a.rearrange("(a n) -> a n", a=1)

        def spread(a):
            return row(a).partition_broadcast(P).rearrange("p a n -> p (a n)") if len(row(a).partition_broadcast(P).shape) == 3 else row(a).partition_broadcast(P)

        def column(a, c):
            return a.rearrange("(c p) -> p c", c=c)

        def f1_slot(f, k):
            base = (q_tm if f < 3 else q_sq)
            v = base[:].rearrange("p a t h d -> p (a t h d)")
            o = (f % 3) * B * S + 512 * k + (FF if f == 3 else 0)
            return v[:, o:o + 512]

        @block.sync
        def _(sp):
            sp.dma_start(cond4[:], cond).then_inc(ld_ada, 16)
            sp.dma_start(ada_w[:], w_ada).then_inc(ld_ada, 16)
            sp.dma_start(ada_b[:], row(b_ada)).then_inc(ld_ada, 16)
            sp.dma_start(wqkv[:, 0, :], w_q).then_inc(ld_qkv, 16)
            sp.dma_start(wqkv[:, 1, :], w_k).then_inc(ld_qkv, 16)
            sp.dma_start(wqkv[:, 2, :], w_v).then_inc(ld_qkv, 16)
            sp.dma_start(bqkv[:, 0, :], spread(b_q)).then_inc(ld_qkv, 16)
            sp.dma_start(bqkv[:, 1, :], spread(b_k)).then_inc(ld_qkv, 16)
            sp.dma_start(bqkv[:, 2, :], spread(b_v)).then_inc(ld_qkv, 16)
            sp.dma_start(wo_c[:], w_o).then_inc(ld_cff, 16)
            sp.dma_start(bo_c[:], spread(b_o)).then_inc(ld_cff, 16)
            sp.dma_start(wf1[:], w_f1).then_inc(ld_cff, 16)
            sp.dma_start(bf1_row[:], row(b_f1)).then_inc(ld_cff, 16)
            sp.dma_start(bf1_col[:], column(b_f1, FC), allow_slow_non_contiguous=True).then_inc(ld_cff, 16)
            sp.dma_start(wf2[:], w_f2.rearrange("(c p) d -> p c d", p=P)).then_inc(ld_cff, 16)
            sp.dma_start(bf2[:], spread(b_f2)).then_inc(ld_cff, 16)
            sp.dma_start(wd[:, 0, :], W_dq).then_inc(ld_mla, 16)
            sp.dma_start(wd[:, 1, :], W_dkv).then_inc(ld_mla, 16)
            sp.dma_start(wu[:, 0, :], W_uq).then_inc(ld_mla, 16)
            sp.dma_start(wu[:, 1, :], W_uk).then_inc(ld_mla, 16)
            sp.dma_start(wu[:, 2, :], W_uv).then_inc(ld_mla, 16)
            sp.dma_start(wo_m[:], W_o).then_inc(ld_mla, 16)
            for w_s, w_d in ((wx, Wx), (wh, Wh)):
                src = w_d.rearrange("k (g n) -> k g n", g=4)
                sp.dma_start(w_s[:, 0, :], src[:, 2, :]).then_inc(ld_rnn, 16)
                sp.dma_start(w_s[:, 1:3, :], src[:, 0:2, :]).then_inc(ld_rnn, 16)
                sp.dma_start(w_s[:, 3, :], src[:, 3, :]).then_inc(ld_rnn, 16)
            bsrc = row(b_g).rearrange("a (g n) -> a g n", g=4)
            sp.dma_start(bg[:, 0, :], bsrc[:, 2, :]).then_inc(ld_rnn, 16)
            sp.dma_start(bg[:, 1:3, :], bsrc[:, 0:2, :]).then_inc(ld_rnn, 16)
            sp.dma_start(bg[:, 3, :], bsrc[:, 3, :]).then_inc(ld_rnn, 16)
            sp.dma_start(w1s[:], w1).then_inc(ld_rnn, 16)
            sp.dma_start(b1s[:], column(b1, FC), allow_slow_non_contiguous=True).then_inc(ld_rnn, 16)
            sp.dma_start(w2s[:], w2.rearrange("(c p) d -> p c d", p=P)).then_inc(ld_rnn, 16)
            sp.dma_start(b2s[:], row(b2)).then_inc(ld_rnn, 16)
            for bb in range(B):
                sp.dma_start(x_tb[bb:P:B, :, :], x_steps[bb]).then_inc(ld_xtb, 16)

            sp.wait_ge(zeros, 2)
            sp.wait_ge(qT_ready, 2)
            for h in range(H):
                sp.dma_start(qz[h * HD:(h + 1) * HD, h, :], qT[h * HD:(h + 1) * HD].rearrange("p t n -> p (t n)")).then_inc(qz_ready, 16)
            sp.wait_ge(mq_ready, 4)
            sp.wait_ge(score_mm, 2 * B * NG)
            for h in range(H):
                sp.dma_start(qz[h * HD:(h + 1) * HD, h, :], qT[h * HD:(h + 1) * HD].rearrange("p t n -> p (t n)")).then_inc(qz_ready, 16)
            for c in range(CHUNKS):
                sp.wait_ge(y_ready, c + 1)
                sp.dma_start(out_steps[c], o_sb[:, c % 2, :]).then_inc(stored[c % 2], 16)
            for k in range(2):
                sp.wait_ge(stored[k], 8 * CHUNKS)

        @block.gpsimd
        def _(pool):
            nc.gpsimd.memset(ident[:], 0.0).then_inc(consts, 1)
            nc.gpsimd.memset(mask0[:], 0.0).then_inc(consts, 1)
            nc.gpsimd.memset(mask1[:], 0.0).then_inc(consts, 1)
            nc.gpsimd.memset(ones[:], 1.0).then_inc(consts, 1)
            pool.wait_ge(consts, 4)
            nc.gpsimd.affine_select(out=ident[:], in_=ident[:], compare_op=ALU.not_equal, fill=1.0, base=0,
                                    pattern=[[-1, P]], channel_multiplier=1).then_inc(consts, 1)
            nc.gpsimd.affine_select(out=mask0[:], in_=mask0[:], compare_op=ALU.is_ge, fill=MASKED, base=0,
                                    pattern=[[0, GROUP], [-1, P]], channel_multiplier=1).then_inc(consts, 1)
            nc.gpsimd.affine_select(out=mask1[:], in_=mask1[:], compare_op=ALU.is_ge, fill=MASKED, base=P,
                                    pattern=[[0, 2], [-1, S]], channel_multiplier=1).then_inc(consts, 1)
            pool.wait_ge(consts, 7)
            nc.gpsimd.tensor_copy(identb[:], ident[:]).then_inc(consts, 1)
            nc.gpsimd.memset(vaug[:], 0.0).then_inc(zeros, 1)
            nc.gpsimd.memset(qz[:], 0.0).then_inc(zeros, 1)

        @block.scalar
        def _(act):
            act.dma_start(x_tm[:], x_tiles).then_inc(ld_x, 16)

            taken = [0, 0]

            def col(k):
                return sm[:, k, :]

            def root(a, y):
                taken[0] += 1
                act.wait_ge(roots_in, taken[0])
                nc.scalar.activation(y, a, ACT.Ln).then_inc(act_ch, 1)
                taken[1] += 1
                act.wait_ge(act_ch, taken[1])
                nc.scalar.activation(y, y, ACT.Exp, scale=-0.5).then_inc(roots_out, 1)

            def front_roots(k):
                root(col(4), col(21))
                act.wait_ge(ratio_ready, k)
                nc.scalar.activation(col(7), col(6), ACT.Ln).then_inc(ln_ready, 1)
                root(col(4), col(21))
                root(col(23), col(10))

            def join_roots(k):
                root(col(23), col(11))
                root(col(23), col(15))
                act.wait_ge(tanh_in, k)
                nc.scalar.activation(col(14), col(12), ACT.Tanh).then_inc(tanh_out, 1)

            for bb in range(B):
                act.wait_ge(ada_mm, bb + 1)
                ins = nc.scalar.activation(ada[:, bb].rearrange("p s d -> p (s d)"),
                                           bank[:, 2 * bb:2 * bb + 2, :].rearrange("p k n -> p (k n)")[:, 0:6 * D], ACT.Copy)
                ins.then_inc(ada_ready, 1)
            front_roots(1)
            for k in range(2):
                act.wait_ge(v_turned, k + 1)
                nc.scalar.activation(vT[:, 4 * k:4 * k + 4, :].rearrange("p t n -> p (t n)"), bank[:, k, :], ACT.Copy).then_inc(vT_ready, 1)
            act.wait_ge(qkv_ready, TILES)
            nc.scalar.activation(q_sq[:].rearrange("p a t h d -> p (a t h d)"),
                                 q_tm[:].rearrange("p a t h d -> p (a t h d)"), ACT.Square).then_inc(squares, 1)
            root(nq[:, 1, :], nq[:, 0, :])
            root(hn_x, hn[:].rearrange("p a t h -> p (a t h)"))
            for k in range(2):
                act.wait_ge(q_turned, k + 1)
                nc.scalar.activation(qT[:, 4 * k:4 * k + 4, :].rearrange("p t n -> p (t n)"), bank[:, k, :], ACT.Copy).then_inc(qT_ready, 1)
            for w in range(2 * B * NG):
                act.wait_ge(score_mm, w + 1)
                if w >= 2:
                    act.wait_ge(pv_mm, w - 1)
                pair = w % 2
                nc.scalar.activation(pT[:, pair, :], bank[:, 2 * pair:2 * pair + 2, :].rearrange("p k n -> p (k n)"),
                                     ACT.Exp, scale=SCALE).then_inc(exp_done, 1)
            for k in range(2):
                act.wait_ge(oT_mm, k + 1)
                nc.scalar.activation(vT[:, 4 * k:4 * k + 4, :].rearrange("p t n -> p (t n)"), bank[:, k, :], ACT.Copy).then_inc(oT_ready, 1)
            join_roots(1)
            front_roots(2)
            for k in range(2):
                act.wait_ge(v_turned, 3 + k)
                nc.scalar.activation(vT[:, 4 * k:4 * k + 4, :].rearrange("p t n -> p (t n)"), bank[:, k, :], ACT.Copy).then_inc(vT_ready, 1)
            for t in range(TILES):
                act.wait_ge(f1n_mm, t + 1)
                nc.scalar.activation(q_sq[:].rearrange("p a t h d -> p (a t h d)")[:, 0:FF], bank[:, 4 + t % 2, :], ACT.Square,
                                     accum_out=sm[:, 20, t:t + 1]).then_inc(f1_norm, 1)
                act.wait_ge(f1_norm, t + 1)
            root(col(23), col(20))
            join_roots(2)
            for k in range(2):
                act.wait_ge(co_turned, k + 1)
                nc.scalar.activation(vT[:, 4 * k:4 * k + 4, :].rearrange("p t n -> p (t n)"), bank[:, k, :], ACT.Copy).then_inc(co_ready, 1)
            for j in range(2):
                for k in range(2):
                    act.wait_ge(c_mm, 2 * j + k + 1)
                    nc.scalar.activation(cT[:, j, 512 * k:512 * k + 512], bank[0:32, 2 + 2 * j + k, :], ACT.Copy).then_inc(c_ready, 1)
            for j, dst in ((0, qT), (1, kT)):
                for k in range(2):
                    act.wait_ge(u_mm, 2 * j + k + 1)
                    nc.scalar.activation(dst[:, 4 * k:4 * k + 4, :].rearrange("p t n -> p (t n)"), bank[:, 2 * j + k, :], ACT.Copy).then_inc(mq_ready, 1)
            m = 0
            for half in range(HALVES):
                keys = P * (half + 1)
                for u in range(B * NG):
                    act.wait_ge(mx_ready, m + 1)
                    if m >= 2:
                        act.wait_ge(mt_mm, m - 1)
                    for j in range(GROUP):
                        ins = nc.scalar.activation(pT[:, m % 2, j * keys:(j + 1) * keys],
                                                   bank[:, 0:2, :].rearrange("p k n -> p (k n)")[:, j * keys:(j + 1) * keys],
                                                   ACT.Exp, scale=SCALE, bias=mx[:, m % 2, j:j + 1])
                    ins.then_inc(mp_ready, 1)
                    m += 1
            act.wait_ge(ld_rnn, 16 * 13)
            for w in (wx, bg):
                for g0, g1, f in ((0, 3, .5), (3, 4, 1.)):
                    nc.scalar.mul(w[:, g0:g1, :], w[:, g0:g1, :], A_SCALE * f).then_inc(w_ready, 1)
            for g0, g1, f in ((0, 3, .5), (3, 4, 1.)):
                nc.scalar.mul(wh[:, g0:g1, :], wh[:, g0:g1, :], W_SCALE * f).then_inc(w_ready, 1)
            act.wait_ge(w_ready, 6)
            nc.scalar.activation(wha[:].rearrange("p g n -> p (g n)"), wh[:].rearrange("p g n -> p (g n)"), ACT.Copy).then_inc(w_ready, 1)
            nc.scalar.mul(h0[:], condT[:], H_SCALE).then_inc(w_ready, 1)

            def gelu(c):
                act.wait_ge(ff_mm, c + 1)
                if c >= 2:
                    act.wait_ge(y_mm, c - 1)
                for f in range(FC):
                    ins = nc.scalar.activation(gel[:, c % 2, f, :], bank[:, 4 + c % 2, f * P:(f + 1) * P], ACT.Gelu,
                                               scale=1.0 / H_SCALE, bias=b1s[:, f:f + 1])
                ins.then_inc(gel_ready, 1)

            for t in range(S):
                k = t % 2
                src = bank[:, 6 + (t // STEPS) % 2, (t % STEPS) * GW:(t % STEPS + 1) * GW]
                act.wait_ge(gates_mm, t + 1)
                if t >= 1:
                    act.wait_ge(hist_ready, t)
                if t == 0:
                    act.wait_ge(c_new, 1)
                nc.scalar.activation(gates[:, k, 0:GW], src, ACT.Tanh, scale=1.0 / A_SCALE).then_inc(gates_act, 1)
                act.wait_ge(c_new, t + 2)
                nc.scalar.activation(th[:, k, :], gates[:, 1 - k, 4 * B:5 * B], ACT.Tanh, scale=0.5).then_inc(th_act, 1)
                if t % STEPS == 8 and t > STEPS:
                    gelu(t // STEPS - 1)
            gelu(CHUNKS - 1)

        @block.vector
        def _(vec):
            counts = {}

            def step(ins, signal=None):
                s = dve if signal is None else signal
                ins.then_inc(s, 1)
                counts[id(s)] = counts.get(id(s), 0) + 1
                vec.wait_ge(s, counts[id(s)])

            V = nc.vector

            def wide(a):
                return a.unsqueeze(2).to_broadcast([P, TILES, D])

            def flat(a):
                return a.rearrange("p t n -> p (t n)")

            vec.wait_ge(ld_ada, 48)
            step(V.tensor_scalar(ada_b[:, D:2 * D], ada_b[:, D:2 * D], 1.0, None, ALU.add))
            step(V.tensor_scalar(ada_b[:, 4 * D:5 * D], ada_b[:, 4 * D:5 * D], 1.0, None, ALU.add))
            vec.wait_ge(cond_t, 1)
            step(V.tensor_copy(condT[:], bank[:, 0, 0:B]))
            step(V.tensor_copy(condB[:], condT[:].unsqueeze(2).to_broadcast([P, B, P])), cond_bc)

            def col(k):
                return sm[:, k, :]

            def rsqrt(a, y, t):
                vec.wait_ge(roots_out, counts[id(roots_in)])
                step(V.tensor_tensor(t, y, y, ALU.mult))
                step(V.scalar_tensor_tensor(t, t, -0.5, a, ALU.mult, ALU.mult))
                step(V.scalar_tensor_tensor(y, t, 1.5, y, ALU.add, ALU.mult))

            def front(src, part):
                step(V.tensor_reduce(col(0), src[:], AX.X, ALU.add))
                step(V.tensor_scalar(col(2), col(0), 1.0 / D, None, ALU.mult))
                step(V.tensor_tensor(ta[:], src[:], wide(col(2)), ALU.subtract))
                step(V.tensor_tensor(tb[:], ta[:], ta[:], ALU.mult))
                step(V.tensor_reduce(col(3), tb[:], AX.X, ALU.add))
                step(V.tensor_tensor(col(4), col(2), col(0), ALU.mult))
                step(V.tensor_tensor(col(1), col(4), col(3), ALU.add))
                step(V.tensor_scalar(col(4), col(1), TINY, None, ALU.max), roots_in)
                rsqrt(col(4), col(21), col(22))
                step(V.tensor_tensor(col(4), col(4), col(21), ALU.mult))
                step(V.tensor_scalar(col(4), col(4), MAX_TANH_ARG, None, ALU.min))
                step(V.tensor_scalar(col(5), col(4), -1.0, 1.0, ALU.mult, ALU.add))
                step(V.reciprocal(col(6), col(5)))
                step(V.scalar_tensor_tensor(col(6), col(4), 1.0, col(6), ALU.add, ALU.mult), ratio_ready)
                step(V.tensor_tensor(col(8), col(4), col(4), ALU.mult))
                step(V.tensor_scalar(col(9), col(8), 1.0 / 13, None, ALU.mult))
                for k in (11, 9, 7, 5, 3):
                    step(V.scalar_tensor_tensor(col(9), col(9), 1.0 / k, col(8), ALU.add, ALU.mult))
                step(V.tensor_scalar(col(9), col(9), 1.0, None, ALU.add))
                step(V.tensor_scalar(col(5), col(4), SERIES_TO, None, ALU.is_lt))
                vec.wait_ge(ln_ready, counts[id(ratio_ready)])
                step(V.scalar_tensor_tensor(col(7), col(7), 0.5, col(21), ALU.mult, ALU.mult))
                step(V.tensor_tensor(col(9), col(9), col(7), ALU.subtract))
                step(V.tensor_tensor(col(9), col(9), col(5), ALU.mult))
                step(V.tensor_tensor(col(9), col(9), col(7), ALU.add))
                step(V.tensor_tensor(col(4), col(9), col(9), ALU.mult))
                step(V.scalar_tensor_tensor(col(4), col(4), 1.0 / D, col(3), ALU.mult, ALU.mult))
                step(V.tensor_scalar(col(4), col(4), LN_EPS, None, ALU.add), roots_in)
                rsqrt(col(4), col(21), col(22))
                step(V.tensor_tensor(col(4), col(21), col(9), ALU.mult))
                vec.wait_ge(ada_ready, B)
                step(V.tensor_tensor(ta[:], ta[:], wide(col(4)), ALU.mult))
                step(V.tensor_tensor(ta[:].rearrange("p (b h) d -> p b h d", b=B), ta[:].rearrange("p (b h) d -> p b h d", b=B),
                                     ada[:, :, part + 1, :].unsqueeze(2).to_broadcast([P, B, HALVES, D]), ALU.mult))
                step(V.tensor_tensor(v_tm[:].rearrange("p (b h) d -> p b h d", b=B), ta[:].rearrange("p (b h) d -> p b h d", b=B),
                                     ada[:, :, part, :].unsqueeze(2).to_broadcast([P, B, HALVES, D]), ALU.add))
                step(V.tensor_tensor(tb[:], v_tm[:], v_tm[:], ALU.mult))
                step(V.tensor_reduce(col(10), tb[:], AX.X, ALU.add))
                step(V.tensor_scalar(col(23), col(10), TINY, None, ALU.max), roots_in)
                rsqrt(col(23), col(10), col(22))
                step(V.tensor_scalar(col(10), col(10), CLIP, 1.0, ALU.mult, ALU.min))

            def join(src, part, dst, signal):
                step(V.tensor_tensor(tb[:], ta[:], ta[:], ALU.mult))
                step(V.tensor_reduce(col(11), tb[:], AX.X, ALU.add))
                step(V.tensor_scalar(col(23), col(11), TINY, None, ALU.max), roots_in)
                rsqrt(col(23), col(11), col(22))
                step(V.tensor_scalar(col(11), col(11), CLIP, 1.0, ALU.mult, ALU.min))
                step(V.tensor_tensor(ta[:], ta[:], wide(col(11)), ALU.mult))
                step(V.tensor_tensor(ta[:].rearrange("p (b h) d -> p b h d", b=B), ta[:].rearrange("p (b h) d -> p b h d", b=B),
                                     ada[:, :, part, :].unsqueeze(2).to_broadcast([P, B, HALVES, D]), ALU.mult))
                step(V.tensor_tensor(tb[:], ta[:], ta[:], ALU.mult))
                step(V.tensor_reduce(col(11), tb[:], AX.X, ALU.add))
                step(V.tensor_scalar(col(23), col(11), TINY, None, ALU.max), roots_in)
                rsqrt(col(23), col(15), col(22))
                step(V.tensor_tensor(col(12), col(23), col(15), ALU.mult), tanh_in)
                step(V.tensor_tensor(tb[:], ta[:], src[:], ALU.mult))
                step(V.tensor_reduce(col(13), tb[:], AX.X, ALU.add))
                vec.wait_ge(tanh_out, counts[id(tanh_in)])
                step(V.tensor_tensor(col(15), col(15), col(14), ALU.mult))
                step(V.tensor_tensor(col(13), col(13), col(15), ALU.mult))
                step(V.tensor_scalar(col(13), col(13), 2.0, 1.0, ALU.mult, ALU.add))
                step(V.tensor_tensor(col(16), col(15), col(15), ALU.mult))
                step(V.tensor_tensor(col(16), col(16), col(11), ALU.mult))
                step(V.tensor_tensor(col(17), col(13), col(16), ALU.add))
                step(V.tensor_tensor(col(16), col(16), col(1), ALU.mult))
                step(V.tensor_tensor(col(16), col(16), col(13), ALU.add))
                step(V.tensor_scalar(col(16), col(16), EPS, None, ALU.max))
                step(V.reciprocal(col(16), col(16)))
                step(V.tensor_scalar(col(18), col(1), -1.0, 1.0, ALU.mult, ALU.add))
                step(V.tensor_tensor(col(18), col(18), col(15), ALU.mult))
                step(V.tensor_tensor(col(18), col(18), col(16), ALU.mult))
                step(V.tensor_tensor(col(17), col(17), col(16), ALU.mult))
                step(V.tensor_tensor(ta[:], ta[:], wide(col(18)), ALU.mult))
                step(V.tensor_tensor(tb[:], src[:], wide(col(17)), ALU.mult))
                step(V.tensor_tensor(dst[:], ta[:], tb[:], ALU.add), signal)

            vec.wait_ge(ld_x, 16)
            front(x_tm, 0)
            step(V.tensor_copy(col(19), col(10)), v_ready)
            vec.wait_ge(ld_qkv, 96)
            for t in range(TILES):
                vec.wait_ge(qkv_mm, t + 1)
                V.scalar_tensor_tensor(q_tm[:, :, t].rearrange("p a h d -> p a (h d)"),
                                       bank[:, 2 + t % 4, 0:3 * D].rearrange("p (a n) -> p a n", a=3), sm[:, 10, t:t + 1],
                                       bqkv[:], ALU.mult, ALU.add).then_inc(qkv_ready, 1)
            vec.wait_ge(squares, 1)
            hn_f = hn[:].rearrange("p a t h -> p (a t) h")
            hn_g = hn[:].rearrange("p a t h -> p (a t h)")
            q_f = q_tm[:].rearrange("p a t h d -> p (a t h) d")
            step(V.tensor_reduce(hn_g, q_sq[:].rearrange("p a t h d -> p (a t h) d"), AX.X, ALU.add))
            step(V.tensor_reduce(nq[:, 0, :], hn_f, AX.X, ALU.add))
            step(V.tensor_scalar(nq[:, 1, :], nq[:, 0, :], TINY, None, ALU.max), roots_in)
            rsqrt(nq[:, 1, :], nq[:, 0, :], nq[:, 2, :])
            step(V.tensor_scalar(nq[:, 0, :], nq[:, 0, :], CLIP, 1.0, ALU.mult, ALU.min))
            step(V.tensor_scalar(nq[:, 0, :], nq[:, 0, :], HEADS_UP, None, ALU.mult))
            step(V.tensor_scalar(hn_x, hn_g, TINY, None, ALU.max), roots_in)
            rsqrt(hn_x, hn_g, hn_t)
            step(V.tensor_scalar(hn_g, hn_g, CLIP, None, ALU.mult))
            step(V.tensor_tensor(hn_f, hn_f, nq[:, 0, :].unsqueeze(2).to_broadcast([P, 3 * TILES, H]), ALU.min))
            n = 2 * TILES * H
            step(V.tensor_tensor(q_f[:, 0:n, :], q_f[:, 0:n, :], hn_g[:, 0:n].unsqueeze(2).to_broadcast([P, n, HD]), ALU.mult), qk_scaled)
            vec.wait_ge(zeros, 2)
            step(V.tensor_tensor(vaug[:].rearrange("p t h v -> p (t h) v")[:, :, 0:HD], q_f[:, n:n + TILES * H, :],
                                 hn_g[:, n:n + TILES * H].unsqueeze(2).to_broadcast([P, TILES * H, HD]), ALU.mult))
            step(V.memset(vaug[:, :, :, HD:HD + 1], HEADS_UP), vaug_ready)
            for k in range(2):
                vec.wait_ge(k_turned, k + 1)
                V.tensor_copy(flat(kT[:, 4 * k:4 * k + 4, :]), bank[:, 2 + k, :]).then_inc(kT_ready, 1)

            def o_copy(u):
                vec.wait_ge(pv_mm, 2 * u + 2)
                if u >= 2:
                    vec.wait_ge(o_turned, u - 1)
                V.tensor_copy(oTs[:, u % 2, :], bank[:, 4 + u % 2, 0:S]).then_inc(o_copied, 1)

            def o_norm(u):
                vec.wait_ge(o_turned, u + 1)
                bb, g = divmod(u, NG)
                tr = bank[:, 6 + u % 2, 0:S].rearrange("p (h j v) -> p h j v", h=HALVES, j=GROUP)
                step(V.reciprocal(rd[:, u % 2], tr[:, :, :, HD]))
                o4 = o_tm[:].rearrange("p t (g j d) -> p t g j d", g=NG, d=HD)
                V.tensor_tensor(o4[:, HALVES * bb:HALVES * bb + HALVES, g], tr[:, :, :, 0:HD],
                                rd[:, u % 2].unsqueeze(3).to_broadcast([P, HALVES, GROUP, HD]), ALU.mult).then_inc(o_normed, 1)

            for u in range(B * NG):
                o_copy(u)
                if u:
                    o_norm(u - 1)
            o_norm(B * NG - 1)
            vec.wait_ge(ld_cff, 16 * 7)
            vec.wait_ge(attn_mm, 1)
            step(V.tensor_tensor(ta[:], bank[:, 2:4, :].rearrange("p k (t n) -> p (k t) n", n=D),
                                 bo_c[:].unsqueeze(1).to_broadcast([P, TILES, D]), ALU.add))
            join(x_tm, 2, x1_tm, dve)
            front(x1_tm, 3)
            step(V.tensor_tensor(v_tm[:], v_tm[:], wide(col(10)), ALU.mult), v_ready)
            for f in range(FC):
                for k in range(2):
                    i = 2 * f + k
                    vec.wait_ge(f1_mm, i + 1)
                    V.tensor_scalar(f1_slot(f, k),
                                    bank[:, 2 + i % 2, :], bf1_col[:, f:f + 1], None, ALU.add).then_inc(f1_ready, 1)
            vec.wait_ge(f1_norm, TILES)
            step(V.tensor_scalar(col(23), col(20), TINY, None, ALU.max), roots_in)
            rsqrt(col(23), col(20), col(22))
            step(V.tensor_scalar(col(20), col(20), CLIP, 1.0, ALU.mult, ALU.min))
            vec.wait_ge(f2_mm, 1)
            step(V.tensor_tensor(ta[:], bank[:, 6:8, :].rearrange("p k (t n) -> p (k t) n", n=D), wide(col(20)), ALU.mult))
            step(V.tensor_tensor(ta[:], ta[:], bf2[:].unsqueeze(1).to_broadcast([P, TILES, D]), ALU.add))
            join(x1_tm, 5, v_tm, cond_out)

            step(V.memset(vaug[:, :, :, HD:HD + 1], 1.0))
            for t in range(TILES):
                vec.wait_ge(mv_mm, t + 1)
                V.tensor_copy(vaug[:, t, :, 0:HD], bank[:, 4 + t % 2, 0:D].rearrange("p (h d) -> p h d", h=H)).then_inc(mv_ready, 1)

            def m_max(m, half):
                keys = P * (half + 1)
                vec.wait_ge(ms_mm, m + 1)
                if m >= 2:
                    vec.wait_ge(mp_ready, m - 1)
                src = bank[:, 0:2, :].rearrange("p k n -> p (k n)")[:, 0:GROUP * keys].rearrange("p (j n) -> p j n", j=GROUP)
                step(V.tensor_reduce(mx[:, m % 2, :], src, AX.X, ALU.max))
                V.tensor_scalar(mx[:, m % 2, :], mx[:, m % 2, :], -SCALE, None, ALU.mult).then_inc(mx_ready, 1)

            def m_tail(m, half, u):
                n = GROUP * P
                for kc in range(half + 1):
                    vec.wait_ge(mt_mm, m + 1)
                    if m >= 1 and kc == 0:
                        vec.wait_ge(mpv_mm, m)
                    ins = V.tensor_copy(q_sq[:].rearrange("p a t h d -> p (a t h d)")[:, kc * n:(kc + 1) * n], bank[:, 2 + kc, :])
                ins.then_inc(mt_ready, 1)
                vec.wait_ge(mpv_mm, m + 1)
                step(V.tensor_copy(oTs[:, 0, 0:P], bank[:, 4, 0:P]), mo_copied)
                vec.wait_ge(mo_turned, m + 1)
                bb, g = divmod(u, NG)
                tr = bank[:, 5, 0:P].rearrange("p (j v) -> p j v", j=GROUP)
                step(V.reciprocal(rd[:, 0, 0], tr[:, :, HD]))
                o4 = o_tm[:].rearrange("p t (g j d) -> p t g j d", g=NG, d=HD)
                V.tensor_tensor(o4[:, HALVES * bb + half, g], tr[:, :, 0:HD],
                                rd[:, 0, 0].unsqueeze(2).to_broadcast([P, GROUP, HD]), ALU.mult).then_inc(mo_normed, 1)

            m = 0
            for half in range(HALVES):
                for u in range(B * NG):
                    m_max(m, half)
                    m_tail(m, half, u)
                    m += 1
            for k in range(2):
                vec.wait_ge(moT_mm, k + 1)
                V.tensor_copy(oT[:].rearrange("p (t b) -> p t b", b=B)[:, :, 2 * k:2 * k + 2],
                              bank[:, k, :].rearrange("p (b t) -> p t b", b=2)).then_inc(moT_ready, 1)
            for k in range(2):
                vec.wait_ge(x1_mm, k + 1)
                V.tensor_copy(flat(vT[:, 4 * k:4 * k + 4, :]), bank[:, 2 + k, :]).then_inc(x1_ready, 1)

            vec.wait_ge(w_ready, 8)
            step(V.tensor_tensor(whb[:], wh[:], wha[:], ALU.subtract), h_ready)
            step(V.memset(gates[:], 0.0), c_new)

            def result(c):
                vec.wait_ge(y_mm, c + 1)
                vec.wait_ge(ld_xtb, 64)
                if c >= 2:
                    vec.wait_ge(stored[c % 2], 16 * (c // 2))
                V.tensor_tensor(o_sb[:, c % 2, :], bank[:, 2 + c % 2, 0:D], x_tb[:, c, :], ALU.add).then_inc(y_ready, 1)

            for t in range(S):
                k = t % 2
                vec.wait_ge(gates_act, t + 1)
                step(V.scalar_tensor_tensor(pr[:, k, :], gates[:, k, B:3 * B], 1.0, gates[:, k, 3 * B:5 * B], ALU.add, ALU.mult))
                V.scalar_tensor_tensor(gates[:, 1 - k, 4 * B:5 * B], pr[:, k, B:2 * B], 0.5, pr[:, k, 0:B], ALU.mult, ALU.add).then_inc(c_new, 1)
                step(V.tensor_scalar(so[:, k, :], gates[:, k, 0:B], 1.0, 0.5 * H_SCALE, ALU.add, ALU.mult))
                vec.wait_ge(th_act, t + 1)
                V.tensor_tensor(ha[:, k, :], so[:, k, :], th[:, k, :], ALU.mult).then_inc(h_ready, 1)
                if t % STEPS == 0 and t >= 2 * STEPS:
                    vec.wait_ge(ff_mm, t // STEPS - 1)
                hs = hist[:, (t // STEPS) % 2, t % STEPS, :]
                V.tensor_tensor(hs, so[:, k, :], th[:, k, :], ALU.mult).then_inc(hist_ready, 1)
                vec.wait_ge(hist_ready, t + 1)
                vec.wait_ge(h_ready, t + 2)
                V.tensor_tensor(hb[:, k, :], hs, ha[:, k, :], ALU.subtract).then_inc(hb_ready, 1)
                if t % STEPS == 16 and t > STEPS:
                    result(t // STEPS - 1)
            result(CHUNKS - 1)

        @block.tensor
        def _(pe):
            T = nc.tensor
            pe.wait_ge(consts, 8)
            pe.wait_ge(ld_ada, 48)
            T.transpose(bank[:, 0, 0:B], cond4[:], ident[0:B, 0:B]).then_inc(cond_t, 1)
            pe.wait_ge(cond_bc, 1)
            pe.wait_ge(dve, 2)
            for bb in range(B):
                for k, (a, z) in enumerate(((0, 512), (512, 6 * D))):
                    T.matmul(bank[:, 2 * bb + k, 0:z - a], condB[:, bb, :], ada_w[:, a:z], start=True, stop=False)
                    ins = T.matmul(bank[:, 2 * bb + k, 0:z - a], ones[:], ada_b[:, a:z], start=False, stop=True)
                ins.then_inc(ada_mm, 1)

            def turn8(src, base, signal):
                for k in range(2):
                    for t in range(4):
                        ins = T.transpose(bank[:, base + k, t * P:(t + 1) * P], src(4 * k + t), ident[:])
                    ins.then_inc(signal, 1)

            pe.wait_ge(v_ready, 1)
            pe.wait_ge(ada_ready, B)
            turn8(lambda t: v_tm[:, t, :], 0, v_turned)
            pe.wait_ge(ld_qkv, 96)
            for t in range(TILES):
                pe.wait_ge(vT_ready, 1 + t // 4)
                if t >= 4:
                    pe.wait_ge(qkv_ready, t - 3)
                T.matmul(bank[:, 2 + t % 4, 0:3 * D], vT[:, t, :], wqkv[:].rearrange("p a n -> p (a n)"), start=True, stop=True).then_inc(qkv_mm, 1)
            pe.wait_ge(qk_scaled, 1)
            turn8(lambda t: q_tm[:, 0, t].rearrange("p h d -> p (h d)"), 0, q_turned)
            turn8(lambda t: q_tm[:, 1, t].rearrange("p h d -> p (h d)"), 2, k_turned)

            def scores(w):
                u, kc = divmod(w, 2)
                bb, g = divmod(u, NG)
                if w >= 2:
                    pe.wait_ge(exp_done, w - 1)
                for j in range(2):
                    h = GROUP * g + 2 * j
                    ins = T.matmul(bank[:, 2 * (w % 2) + j, :], kT[:, HALVES * bb + kc, :], qz[:, h:h + 2, bb * S:(bb + 1) * S],
                                   start=True, stop=True)
                ins.then_inc(score_mm, 1)

            def values(w):
                u, kc = divmod(w, 2)
                bb, g = divmod(u, NG)
                pe.wait_ge(exp_done, w + 1)
                if kc == 0 and u >= 2:
                    pe.wait_ge(o_copied, u - 1)
                for j in range(GROUP):
                    ins = T.matmul(bank[VP * j:VP * j + VP, 4 + u % 2, 0:S], vaug[:, HALVES * bb + kc, GROUP * g + j, :],
                                   pT[:, w % 2, j * S:(j + 1) * S], start=(kc == 0), stop=(kc == 1), tile_position=(0, VP * j))
                ins.then_inc(pv_mm, 1)

            def o_turn(u):
                pe.wait_ge(o_copied, u + 1)
                if u >= 2:
                    pe.wait_ge(o_normed, u - 1)
                for half in range(HALVES):
                    ins = T.transpose(bank[:, 6 + u % 2, half * P:(half + 1) * P], oTs[:, u % 2, half * P:(half + 1) * P], ident[:])
                ins.then_inc(o_turned, 1)

            pe.wait_ge(qT_ready, 2)
            pe.wait_ge(kT_ready, 2)
            pe.wait_ge(qz_ready, 16 * H)
            pe.wait_ge(vaug_ready, 1)
            N = 2 * B * NG
            scores(0)
            for w in range(N):
                if w + 1 < N:
                    scores(w + 1)
                values(w)
                if w % 2 == 0 and w >= 2:
                    o_turn(w // 2 - 1)
            o_turn(B * NG - 1)
            pe.wait_ge(o_normed, B * NG)
            turn8(lambda t: o_tm[:, t, :], 0, oT_mm)
            pe.wait_ge(ld_cff, 16 * 7)
            for t in range(TILES):
                pe.wait_ge(oT_ready, 1 + t // 4)
                ins = T.matmul(bank[:, 2 + t // 4, (t % 4) * P:(t % 4 + 1) * P], vT[:, t, :], wo_c[:], start=True, stop=True)
            ins.then_inc(attn_mm, 1)
            pe.wait_ge(v_ready, 2)
            turn8(lambda t: v_tm[:, t, :], 0, v_turned)
            pe.wait_ge(vT_ready, 4)
            for f in range(FC):
                for k in range(2):
                    i = 2 * f + k
                    if i >= 2:
                        pe.wait_ge(f1_ready, i - 1)
                    T.matmul(bank[:, 2 + i % 2, :], wf1[:, f * P:(f + 1) * P], vT[:, 4 * k:4 * k + 4, :].rearrange("p t n -> p (t n)"),
                             start=True, stop=True).then_inc(f1_mm, 1)
                    t = i
                    if t >= 2:
                        pe.wait_ge(f1_norm, t - 1)
                    T.matmul(bank[:, 4 + t % 2, :], vT[:, t, :], wf1[:], start=True, stop=False)
                    T.matmul(bank[:, 4 + t % 2, :], ones[:], bf1_row[:], start=False, stop=True).then_inc(f1n_mm, 1)
            pe.wait_ge(f1_ready, 2 * FC)
            for t in range(TILES):
                for f in range(FC):
                    ins = T.matmul(bank[:, 6 + t // 4, (t % 4) * P:(t % 4 + 1) * P], f1_slot(f, t // 4)[:, (t % 4) * P:(t % 4 + 1) * P],
                                   wf2[:, f, :], start=(f == 0), stop=(f == FC - 1))
            ins.then_inc(f2_mm, 1)
            pe.wait_ge(cond_out, 1)
            turn8(lambda t: v_tm[:, t, :], 0, co_turned)
            pe.wait_ge(ld_mla, 16 * 6)
            for j in range(2):
                for k in range(2):
                    pe.wait_ge(co_ready, k + 1)
                    T.matmul(bank[0:32, 2 + 2 * j + k, :], wd[:, j, :], vT[:, 4 * k:4 * k + 4, :].rearrange("p t n -> p (t n)"),
                             start=True, stop=True).then_inc(c_mm, 1)
            pe.wait_ge(c_ready, 4)
            for j in range(2):
                for k in range(2):
                    T.matmul(bank[:, 2 * j + k, :], wu[:, j, :], cT[:, j, 512 * k:512 * k + 512], start=True, stop=True).then_inc(u_mm, 1)
            for t in range(TILES):
                if t >= 2:
                    pe.wait_ge(mv_ready, t - 1)
                T.matmul(bank[:, 4 + t % 2, 0:D], cT[:, 1, t * P:(t + 1) * P], wu[:, 2, :], start=True, stop=True).then_inc(mv_mm, 1)
            pe.wait_ge(mv_ready, TILES)
            pe.wait_ge(mq_ready, 4)
            pe.wait_ge(qz_ready, 32 * H)
            m = 0
            for half in range(HALVES):
                keys = P * (half + 1)
                for u in range(B * NG):
                    bb, g = divmod(u, NG)
                    if m >= 1:
                        pe.wait_ge(mp_ready, m)
                    per = 512 // keys
                    for j in range(GROUP):
                        if j % per == 0:
                            T.matmul(bank[:, j // per, :], identb[:], (mask0, mask1)[half][:], start=True, stop=False, skip_group_check=True)
                        ins = T.matmul(bank[:, j // per, (j % per) * keys:(j % per + 1) * keys],
                                       qz[:, GROUP * g + j, bb * S + half * P:bb * S + half * P + P],
                                       kT[:].rearrange("p t n -> p (t n)")[:, bb * S:bb * S + keys],
                                       start=False, stop=True, skip_group_check=True)
                    ins.then_inc(ms_mm, 1)
                    pe.wait_ge(mp_ready, m + 1)
                    if m >= 1:
                        pe.wait_ge(mt_ready, m)
                    for kc in range(half + 1):
                        for j in range(GROUP):
                            ins = T.transpose(bank[:, 2 + kc, j * P:(j + 1) * P], pT[:, m % 2, j * keys + kc * P:j * keys + kc * P + P], ident[:])
                    ins.then_inc(mt_mm, 1)
                    pe.wait_ge(mt_ready, m + 1)
                    if m >= 1:
                        pe.wait_ge(mo_copied, m)
                    for kc in range(half + 1):
                        for j in range(GROUP):
                            o = kc * GROUP * P + j * P
                            ins = T.matmul(bank[VP * j:VP * j + VP, 4, 0:P], vaug[:, HALVES * bb + kc, GROUP * g + j, :],
                                           q_sq[:].rearrange("p a t h d -> p (a t h d)")[:, o:o + P],
                                           start=(kc == 0), stop=(kc == half), tile_position=(0, VP * j))
                    ins.then_inc(mpv_mm, 1)
                    pe.wait_ge(mo_copied, m + 1)
                    if m >= 1:
                        pe.wait_ge(mo_normed, m)
                    T.transpose(bank[:, 5, 0:P], oTs[:, 0, 0:P], ident[:]).then_inc(mo_turned, 1)
                    m += 1
            pe.wait_ge(mo_normed, m)
            turn8(lambda t: o_tm[:, t, :], 0, moT_mm)
            for k in range(2):
                pe.wait_ge(moT_ready, 2)
                pe.wait_ge(ld_xtb, 64)
                T.matmul(bank[:, 2 + k, :], wo_m[:], oT[:, 512 * k:512 * k + 512], start=True, stop=True)
                for t in range(4):
                    ins = T.matmul(bank[:, 2 + k, t * P:(t + 1) * P], x_tb[:, 4 * k + t, :], ident[:], start=False, stop=True, skip_group_check=True)
                ins.then_inc(x1_mm, 1)
            pe.wait_ge(x1_ready, 2)
            pe.wait_ge(w_ready, 8)

            def inputs_of(c):
                acc = bank[:, 6 + c % 2, :].rearrange("p (t g b) -> p t g b", g=4, b=B)
                for g in range(4):
                    T.matmul(acc[:, :, g, :], bg[:, g, :], ones[:].rearrange("a (t b) -> a t b", b=B), start=(g == 0), stop=True,
                             skip_group_check=True)
                for g in range(4):
                    ins = T.matmul(acc[:, :, g, :], wx[:, g, :], x1T[:, c * P:(c + 1) * P], start=False, stop=True,
                                   skip_group_check=True)
                ins.then_inc(xw_ready, 1)

            def ffn_up(c):
                pe.wait_ge(hist_ready, STEPS * (c + 1))
                if c >= 2:
                    pe.wait_ge(gel_ready, c - 1)
                for f in range(FC):
                    ins = T.matmul(bank[:, 4 + c % 2, f * P:(f + 1) * P], w1s[:, f * P:(f + 1) * P],
                                   hist[:, c % 2].rearrange("p t b -> p (t b)"), start=True, stop=True)
                ins.then_inc(ff_mm, 1)

            def ffn_down(c):
                pe.wait_ge(gel_ready, c + 1)
                if c >= 2:
                    pe.wait_ge(y_ready, c - 1)
                y = bank[:, 2 + c % 2, 0:D]
                T.matmul(y, ones[:], b2s[:], start=True, stop=False)
                T.matmul(y, oT[:, c * P:(c + 1) * P], wo_m[:], start=False, stop=False)
                for f in range(FC):
                    ins = T.matmul(y, gel[:, c % 2, f, :], w2s[:, f, :], start=False, stop=(f == FC - 1))
                ins.then_inc(y_mm, 1)

            inputs_of(0)
            for t in range(S):
                k = (t + 1) % 2
                acc = bank[:, 6 + (t // STEPS) % 2, (t % STEPS) * GW:(t % STEPS + 1) * GW]
                pe.wait_ge(h_ready, t + 1)

                def add(w, h):
                    for g in range(4):
                        ins = T.matmul(acc[:, g * B:(g + 1) * B], w[:, g, :], h, start=False, stop=True, skip_group_check=True)
                    return ins

                if t == 0:
                    add(wh, h0[:]).then_inc(gates_mm, 1)
                else:
                    add(wha, ha[:, k, :])
                    add(whb, ha[:, k, :])
                    pe.wait_ge(hb_ready, t)
                    add(wha, hb[:, k, :]).then_inc(gates_mm, 1)
                if t % STEPS == 2 and t + STEPS < S:
                    inputs_of(t // STEPS + 1)
                if t % STEPS == 4 and t > STEPS:
                    ffn_up(t // STEPS - 1)
                if t % STEPS == 12 and t > STEPS:
                    ffn_down(t // STEPS - 1)
            ffn_up(CHUNKS - 1)
            ffn_down(CHUNKS - 1)


_INS = ['x', 'cond_1024', 'L0_cond_w_q', 'L0_cond_b_q', 'L0_cond_w_k', 'L0_cond_b_k', 'L0_cond_w_v', 'L0_cond_b_v',
        'L0_cond_w_o', 'L0_cond_b_o', 'L0_cond_w_f1', 'L0_cond_b_f1', 'L0_cond_w_f2', 'L0_cond_b_f2', 'L0_cond_w_ada',
        'L0_cond_b_ada', 'L0_attn_W_dq', 'L0_attn_W_uq', 'L0_attn_W_dkv', 'L0_attn_W_uk', 'L0_attn_W_uv', 'L0_attn_W_o',
        'L0_cond2_Wx', 'L0_cond2_Wh', 'L0_cond2_b', 'L0_ffn_w1', 'L0_ffn_b1', 'L0_ffn_w2', 'L0_ffn_b2']


def kernel(**inputs):
    import numpy as np
    import concourse.bacc as bacc
    from concourse.bass_utils import run_bass_kernel_spmd

    nc = bacc.Bacc("TRN2", target_bir_lowering=False, num_devices=1)
    arrays, args = {}, []
    for name in _INS:
        a = np.ascontiguousarray(inputs[name])
        arrays[f"in_{name}"] = a
        args.append(nc.dram_tensor(f"in_{name}", a.shape, mybir.dt.from_np(a.dtype), kind="ExternalInput").ap())
    args.append(nc.dram_tensor("out_y", (B, S, D), F32, kind="ExternalOutput").ap())
    adaln_attention_lstm_ffn(nc, *args)
    r = run_bass_kernel_spmd(nc, [arrays], core_ids=[0])
    return r.results[0]["out_y"]
```

```python
import math
from contextlib import ExitStack

import concourse.bass as bass
from concourse import mybir

ALU = mybir.AluOpType
ACT = mybir.ActivationFunctionType
AX = mybir.AxisListType
F32 = mybir.dt.float32
F16 = mybir.dt.float16
BF16 = mybir.dt.bfloat16

B, S, D, H = 4, 256, 128, 16
HD = D // H
FF = 512
P = 128
HALVES = S // P
TILES = B * HALVES
GROUP = 4
NG = H // GROUP
FC = FF // P
VP = 32

LN_EXP = "natural_log_exp_and_others"
TANH_EXP = "exp_and_others"

EPS = 1e-7
MAX_TANH_ARG = 1.0 - 1e-5
CLIP = math.atanh(0.9999899864196777)
LN_EPS = 1e-6
TINY = EPS * EPS
SERIES_TO = 0.25


def _beta(a, b):
    return math.exp(math.lgamma(a) + math.lgamma(b) - math.lgamma(a + b))


HEADS_UP = _beta(HD / 2, 0.5) / _beta(D / 2, 0.5)
SCALE = 1.0 / math.sqrt(HD)
MASKED = -1e30
QK_SCALE = 1024.0
SLOTS = 4

STEPS = 32
CHUNKS = S // STEPS
GW = 4 * B
H_SCALE = 4096.0
W_SCALE = 16.0
A_SCALE = H_SCALE * W_SCALE


def adaln_attention_lstm_ffn(nc, x, cond, w_q, b_q, w_k, b_k, w_v, b_v, w_o, b_o, w_f1, b_f1, w_f2, b_f2,
                             w_ada, b_ada, W_dq, W_uq, W_dkv, W_uk, W_uv, W_o, Wx, Wh, b_g, w1, b1, w2, b2, out):
    with ExitStack() as ctx:
        def sb(name, shape, dt=F32):
            return ctx.enter_context(nc.sbuf_tensor(name, shape, dt))

        def ps(name, shape, dt=F32):
            return ctx.enter_context(nc.psum_tensor(name, shape, dt))

        def sem(name):
            return ctx.enter_context(nc.semaphore(name))

        ident = sb("ident", [P, P])
        identb = sb("identb", [P, P], BF16)
        identh = sb("identh", [P, P], F16)
        mask0 = sb("mask0", [P, GROUP, P], BF16)
        mask1 = sb("mask1", [P, 2, S], BF16)
        ones = sb("ones", [1, P])
        cond4 = sb("cond4", [B, D])
        condT = sb("condT", [P, B])
        condB = sb("condB", [P, B, P])
        ada_w = sb("ada_w", [P, 6 * D])
        ada_b = sb("ada_b", [1, 6 * D])
        ada = sb("ada", [P, B, 6, D])
        wqkv = sb("wqkv", [P, 3, D])
        bqkv = sb("bqkv", [P, 3, D])
        wo_c = sb("wo_c", [P, D])
        bo_c = sb("bo_c", [P, D])
        wf1 = sb("wf1", [P, FF])
        bf1_col = sb("bf1_col", [P, FC])
        bf1_row = sb("bf1_row", [1, FF])
        wf2 = sb("wf2", [P, FC, D])
        bf2 = sb("bf2", [P, D])
        wd = sb("wd", [P, 2, 32])
        wu = sb("wu", [64, 2, D])
        wo_m = sb("wo_m", [P, D])
        wx = sb("wx", [P, 4, D])
        wh = sb("wh", [P, 4, D])
        bg = sb("bg", [1, 4, D])
        wha = sb("wha", [P, 4, D], F16)
        whb = sb("whb", [P, 4, D], F16)
        w1s = sb("w1s", [P, FF])
        b1s = sb("b1s", [P, FC])
        w2s = sb("w2s", [P, FC, D])
        b2s = sb("b2s", [1, D])
        x_tb = sb("x_tb", [P, CHUNKS, D])

        x_tm = sb("x_tm", [P, TILES, D])
        ta = sb("ta", [P, TILES, D])
        tb = sb("tb", [P, TILES, D])
        v_tm = sb("v_tm", [P, TILES, D])
        x1_tm = sb("x1_tm", [P, TILES, D])
        o_tm = sb("o_tm", [P, TILES, D])
        vT = sb("vT", [P, TILES, P])
        q_tm = sb("q_tm", [P, 3, TILES, H, HD])
        q_sq = sb("q_sq", [P, 3, TILES, H, HD])
        qT = sb("qT", [P, TILES, P])
        kT = sb("kT", [P, TILES, P])
        qz = sb("qz", [P, H, B * S])
        pairs = qz[:].rearrange("p h n -> p (h n)").bitcast(F16)
        kS, qS = (pairs[:, i * NG * B * S:(i + 1) * NG * B * S].rearrange("p (g n) -> p g n", g=NG) for i in range(2))
        k_pair, q_pair = (pairs[:, i * TILES * H * SLOTS * HD:(i + 1) * TILES * H * SLOTS * HD].rearrange(
            "p (t h s d) -> p (t h) s d", t=TILES, s=SLOTS, d=HD) for i in range(2, 4))
        q_slab = pairs[:, H * B * S:].rearrange("p (h n) -> p h n", h=H)
        vaug = sb("vaug", [P, TILES, H, VP])
        hn = sb("hn", [P, 3, TILES, H])
        pT = sb("pT", [P, 2, GROUP * S])
        p_cond = [pT[:, 0, :], pT[:, 1, :], qT[:].rearrange("p t n -> p (t n)"), kT[:].rearrange("p t n -> p (t n)")]
        p_mla = pT[:].rearrange("p a (c n) -> p (a c) n", n=512)
        oTs = sb("oTs", [P, 2, S])
        rd = sb("rd", [P, 2, HALVES, GROUP])
        rdm = sb("rdm", [P, 2, GROUP])
        sm = sb("sm", [P, 24, TILES])
        nq = sb("nq", [P, 3, 3 * TILES])
        hn_x = tb[:].rearrange("p t n -> p (t n)")[:, 0:3 * TILES * H]
        hn_t = tb[:].rearrange("p t n -> p (t n)")[:, 512:512 + 3 * TILES * H]
        cT = q_sq[:].rearrange("p a t h d -> p (a t h d)")[0:64, 0:B * S]
        mx = sb("mx", [P, 2, GROUP])
        pt_mla = q_sq[:].rearrange("p a t h d -> p (a t h d)")[:, 1024:2048].rearrange("p (a n) -> p a n", a=2)

        gates = sb("gates", [P, 2, 5 * B])
        so = sb("so", [P, 2, B])
        pr = sb("pr", [P, 2, 2 * B])
        th = sb("th", [P, 2, B])
        ha = sb("ha", [P, 2, B], F16)
        hb = sb("hb", [P, 2, B], F16)
        h0 = sb("h0", [P, B])
        hist = v_tm[:].rearrange("p t n -> p (t n)").rearrange("p (t b) -> p t b", b=B)
        gel = ta[:].rearrange("p (a f) n -> p a f n", a=2)
        o_sb = tb[:, 0:2, :]

        x1T = vT[:].rearrange("p t n -> p (t n)")
        oT = qT[:].rearrange("p t n -> p (t n)")

        bank = ps("bank", [P, 8, 512])

        ld_x = sem("ld_x")
        ld_ada = sem("ld_ada")
        ld_qkv = sem("ld_qkv")
        ld_cff = sem("ld_cff")
        ld_mla = sem("ld_mla")
        ld_rnn = sem("ld_rnn")
        ld_xtb = sem("ld_xtb")
        consts = sem("consts")
        zeros = sem("zeros")
        dve = sem("dve_chain")
        act_ch = sem("act_chain")
        squares = sem("squares")
        cond_t = sem("cond_t")
        cond_bc = sem("cond_bc")
        ada_mm = sem("ada_mm")
        ada_ready = sem("ada_ready")
        roots_in = sem("roots_in")
        roots_out = sem("roots_out")
        ratio_ready = sem("ratio_ready")
        ln_ready = sem("ln_ready")
        v_ready = sem("v_ready")
        v_turned = sem("v_turned")
        vT_ready = sem("vT_ready")
        qkv_mm = sem("qkv_mm")
        qkv_ready = sem("qkv_ready")
        qk_scaled = sem("qk_scaled")
        k_high = sem("k_high")
        q_high = sem("q_high")
        k_low = sem("k_low")
        q_low = sem("q_low")
        q_turned = sem("q_turned")
        qT_ready = sem("qT_ready")
        k_turned = sem("k_turned")
        kT_ready = sem("kT_ready")
        qz_group = [sem(f"qz_group{g}") for g in range(NG)]
        slab_group = [sem(f"slab_group{g}") for g in range(NG)]
        vaug_ready = sem("vaug_ready")
        score_mm = sem("score_mm")
        exp_done = sem("exp_done")
        pv_mm = sem("pv_mm")
        o_copied = sem("o_copied")
        o_turned = sem("o_turned")
        o_normed = sem("o_normed")
        oT_mm = sem("oT_mm")
        oT_ready = sem("oT_ready")
        attn_mm = sem("attn_mm")
        tanh_in = sem("tanh_in")
        tanh_out = sem("tanh_out")
        f1_mm = sem("f1_mm")
        f1n_mm = sem("f1n_mm")
        f1_ready = sem("f1_ready")
        f1_norm = sem("f1_norm")
        f2_mm = sem("f2_mm")
        cond_out = sem("cond_out")
        co_turned = sem("co_turned")
        co_ready = sem("co_ready")
        c_mm = sem("c_mm")
        c_ready = sem("c_ready")
        u_mm = sem("u_mm")
        mq_ready = sem("mq_ready")
        mk_ready = sem("mk_ready")
        mv_mm = sem("mv_mm")
        mv_ready = sem("mv_ready")
        ms_mm = sem("ms_mm")
        mx_ready = sem("mx_ready")
        mp_ready = sem("mp_ready")
        mt_mm = sem("mt_mm")
        mt_ready = sem("mt_ready")
        mpv_mm = sem("mpv_mm")
        mo_copied = sem("mo_copied")
        mo_turned = sem("mo_turned")
        mo_normed = sem("mo_normed")
        moT_mm = sem("moT_mm")
        moT_ready = sem("moT_ready")
        x1_mm = sem("x1_mm")
        x1_ready = sem("x1_ready")
        w_ready = sem("w_ready")
        h_ready = sem("h_ready")
        hb_ready = sem("hb_ready")
        hist_ready = sem("hist_ready")
        xw_ready = sem("xw_ready")
        gates_mm = sem("gates_mm")
        gates_act = sem("gates_act")
        c_new = sem("c_new")
        th_act = sem("th_act")
        p_ready = sem("p_ready")
        so_ready = sem("so_ready")
        ff_mm = sem("ff_mm")
        gel_ready = sem("gel_ready")
        y_mm = sem("y_mm")
        y_ready = sem("y_ready")
        stored = [sem("stored_even"), sem("stored_odd")]

        block = ctx.enter_context(nc.Block())

        qk_f = q_tm[:].rearrange("p a t h d -> p (a t h) d")

        def doubled(a):
            return a.unsqueeze(2).to_broadcast([P, TILES * H, 2, HD])

        x_tiles = x.rearrange("b (h p) d -> p (b h) d", p=P)
        x_steps = x.rearrange("b (c t) d -> b t c d", t=STEPS)
        out_steps = out.rearrange("b (c t) d -> c t b d", t=STEPS)

        def row(a):
            return a.rearrange("(a n) -> a n", a=1)

        def spread(a):
            return row(a).partition_broadcast(P).rearrange("p a n -> p (a n)") if len(row(a).partition_broadcast(P).shape) == 3 else row(a).partition_broadcast(P)

        def column(a, c):
            return a.rearrange("(c p) -> p c", c=c)

        def flat(a):
            return a.rearrange("p t n -> p (t n)")

        UNITS = [(0, g, b, 0) for g in range(NG) for b in range(B)]
        UNITS += [(1, g, b, i) for g in range(NG) for b in range(B) for i in range(2)]
        GROUPS = [(half, g, b) for half in range(HALVES) for g in range(NG) for b in range(B)]
        FIRST_UNITS = B * NG
        SECOND_UNITS = 2 * B * NG
        TAIL_FROM = 3 * SECOND_UNITS + 6
        FFN_FROM = S // 2
        FFN_EVERY = 16

        def group_of(m):
            return m if m < FIRST_UNITS else FIRST_UNITS + (m - FIRST_UNITS) // 2

        def last_unit(g):
            return g if g < FIRST_UNITS else FIRST_UNITS + 2 * (g - FIRST_UNITS) + 1

        def blocks(m):
            half, g, b, i = UNITS[m]
            if half == 0:
                return [(GROUP * g + j, j, 0) for j in range(GROUP)]
            return [(GROUP * g + 2 * i + j, 2 * i + j, kc) for j in range(2) for kc in range(2)]

        def f1_slot(f, k):
            base = (q_tm if f < 3 else q_sq)
            v = base[:].rearrange("p a t h d -> p (a t h d)")
            o = (f % 3) * B * S + 512 * k + (FF if f == 3 else 0)
            return v[:, o:o + 512]

        @block.sync
        def _(sp):
            sp.dma_start(cond4[:], cond).then_inc(ld_ada, 16)
            sp.dma_start(ada_w[:], w_ada).then_inc(ld_ada, 16)
            sp.dma_start(ada_b[:], row(b_ada)).then_inc(ld_ada, 16)
            sp.dma_start(wqkv[:, 0, :], w_q).then_inc(ld_qkv, 16)
            sp.dma_start(wqkv[:, 1, :], w_k).then_inc(ld_qkv, 16)
            sp.dma_start(wqkv[:, 2, :], w_v).then_inc(ld_qkv, 16)
            sp.dma_start(bqkv[:, 0, :], spread(b_q)).then_inc(ld_qkv, 16)
            sp.dma_start(bqkv[:, 1, :], spread(b_k)).then_inc(ld_qkv, 16)
            sp.dma_start(bqkv[:, 2, :], spread(b_v)).then_inc(ld_qkv, 16)
            sp.dma_start(wo_c[:], w_o).then_inc(ld_cff, 16)
            sp.dma_start(bo_c[:], spread(b_o)).then_inc(ld_cff, 16)
            sp.dma_start(wf1[:], w_f1).then_inc(ld_cff, 16)
            sp.dma_start(bf1_row[:], row(b_f1)).then_inc(ld_cff, 16)
            sp.dma_start(bf1_col[:], column(b_f1, FC), allow_slow_non_contiguous=True).then_inc(ld_cff, 16)
            sp.dma_start(wf2[:], w_f2.rearrange("(c p) d -> p c d", p=P)).then_inc(ld_cff, 16)
            sp.dma_start(bf2[:], spread(b_f2)).then_inc(ld_cff, 16)
            sp.dma_start(wd[:, 0, :], W_dq).then_inc(ld_mla, 16)
            sp.dma_start(wd[:, 1, :], W_dkv).then_inc(ld_mla, 16)
            sp.dma_start(wu[0:32, 0, :], W_uq).then_inc(ld_mla, 16)
            sp.dma_start(wu[32:64, 0, :], W_uk).then_inc(ld_mla, 16)
            sp.dma_start(wu[32:64, 1, :], W_uv).then_inc(ld_mla, 16)
            sp.dma_start(wo_m[:], W_o).then_inc(ld_mla, 16)
            for w_s, w_d in ((wx, Wx), (wh, Wh)):
                src = w_d.rearrange("k (g n) -> k g n", g=4)
                sp.dma_start(w_s[:, 0, :], src[:, 2, :]).then_inc(ld_rnn, 16)
                sp.dma_start(w_s[:, 1:3, :], src[:, 0:2, :]).then_inc(ld_rnn, 16)
                sp.dma_start(w_s[:, 3, :], src[:, 3, :]).then_inc(ld_rnn, 16)
            bsrc = row(b_g).rearrange("a (g n) -> a g n", g=4)
            sp.dma_start(bg[:, 0, :], bsrc[:, 2, :]).then_inc(ld_rnn, 16)
            sp.dma_start(bg[:, 1:3, :], bsrc[:, 0:2, :]).then_inc(ld_rnn, 16)
            sp.dma_start(bg[:, 3, :], bsrc[:, 3, :]).then_inc(ld_rnn, 16)
            sp.dma_start(w1s[:], w1).then_inc(ld_rnn, 16)
            sp.dma_start(b1s[:], column(b1, FC), allow_slow_non_contiguous=True).then_inc(ld_rnn, 16)
            sp.dma_start(w2s[:], w2.rearrange("(c p) d -> p c d", p=P)).then_inc(ld_rnn, 16)
            sp.dma_start(b2s[:], row(b2)).then_inc(ld_rnn, 16)
            for bb in range(B):
                sp.dma_start(x_tb[bb:P:B, :, :], x_steps[bb]).then_inc(ld_xtb, 16)

            sp.wait_ge(zeros, 2)
            for g in range(NG):
                sp.wait_ge(qT_ready, g + 1)
                for j in range(GROUP):
                    rows = slice(SLOTS * HD * j, SLOTS * HD * (j + 1))
                    sp.dma_start(q_slab[rows, GROUP * g + j, :], qS[rows, g, :]).then_inc(slab_group[g], 16)

            sp.wait_ge(zeros, 3)
            sp.wait_ge(mq_ready, 2)
            for h in range(H):
                sp.dma_start(qz[h * HD:(h + 1) * HD, h, :], flat(qT[h * HD:(h + 1) * HD])).then_inc(qz_group[h // GROUP], 16)
            for c in range(CHUNKS):
                sp.wait_ge(y_ready, c + 1)
                sp.dma_start(out_steps[c], o_sb[:, c % 2, :]).then_inc(stored[c % 2], 16)
            for k in range(2):
                sp.wait_ge(stored[k], 8 * CHUNKS)

        @block.gpsimd
        def _(pool):
            nc.gpsimd.memset(ident[:], 0.0).then_inc(consts, 1)
            nc.gpsimd.memset(mask0[:], 0.0).then_inc(consts, 1)
            nc.gpsimd.memset(mask1[:], 0.0).then_inc(consts, 1)
            nc.gpsimd.memset(ones[:], 1.0).then_inc(consts, 1)
            pool.wait_ge(consts, 4)
            nc.gpsimd.affine_select(out=ident[:], in_=ident[:], compare_op=ALU.not_equal, fill=1.0, base=0,
                                    pattern=[[-1, P]], channel_multiplier=1).then_inc(consts, 1)
            nc.gpsimd.affine_select(out=mask0[:], in_=mask0[:], compare_op=ALU.is_ge, fill=MASKED, base=0,
                                    pattern=[[0, GROUP], [-1, P]], channel_multiplier=1).then_inc(consts, 1)
            nc.gpsimd.affine_select(out=mask1[:], in_=mask1[:], compare_op=ALU.is_ge, fill=MASKED, base=P,
                                    pattern=[[0, 2], [-1, S]], channel_multiplier=1).then_inc(consts, 1)
            pool.wait_ge(consts, 7)
            nc.gpsimd.tensor_copy(identb[:], ident[:]).then_inc(consts, 1)
            nc.gpsimd.tensor_copy(identh[:], ident[:]).then_inc(consts, 1)
            nc.gpsimd.memset(vaug[:], 0.0).then_inc(zeros, 1)
            nc.gpsimd.memset(q_slab, 0.0).then_inc(zeros, 1)
            pool.wait_ge(score_mm, 2 * B * NG)
            nc.gpsimd.memset(qz[:], 0.0).then_inc(zeros, 1)

        @block.scalar
        def _(act):
            act.dma_start(x_tm[:], x_tiles).then_inc(ld_x, 16)

            taken = [0, 0]

            def col(k):
                return sm[:, k, :]

            def root(a, y):
                taken[0] += 1
                act.wait_ge(roots_in, taken[0])
                nc.scalar.activation(y, a, ACT.Ln).then_inc(act_ch, 1)
                taken[1] += 1
                act.wait_ge(act_ch, taken[1])
                nc.scalar.activation(y, y, ACT.Exp, scale=-0.5).then_inc(roots_out, 1)

            def front_roots(k):
                root(col(4), col(21))
                act.wait_ge(ratio_ready, k)
                nc.scalar.activation(col(7), col(6), ACT.Ln).then_inc(ln_ready, 1)
                root(col(4), col(21))

            def join_roots(k):
                root(col(23), col(11))
                root(col(23), col(15))
                nc.scalar.preload_act_table_set(TANH_EXP)
                act.wait_ge(tanh_in, k)
                nc.scalar.activation(col(14), col(12), ACT.Tanh).then_inc(tanh_out, 1)

            nc.scalar.preload_act_table_set(LN_EXP)
            front_roots(1)
            for bb in range(B):
                act.wait_ge(ada_mm, bb + 1)
                nc.scalar.activation(ada[:, bb].rearrange("p s d -> p (s d)"),
                                     bank[:, 2 * bb:2 * bb + 2, :].rearrange("p k n -> p (k n)")[:, 0:6 * D], ACT.Copy).then_inc(ada_ready, 1)
            root(col(23), col(10))
            for k in range(2):
                act.wait_ge(v_turned, k + 1)
                nc.scalar.activation(vT[:, 4 * k:4 * k + 4, :].rearrange("p t n -> p (t n)"), bank[:, k, :], ACT.Copy).then_inc(vT_ready, 1)
            act.wait_ge(qkv_ready, TILES)
            nc.scalar.activation(q_sq[:].rearrange("p a t h d -> p (a t h d)"),
                                 q_tm[:].rearrange("p a t h d -> p (a t h d)"), ACT.Square).then_inc(squares, 1)
            root(nq[:, 1, :], nq[:, 0, :])
            root(hn_x, hn[:].rearrange("p a t h -> p (a t h)"))
            act.wait_ge(qk_scaled, 1)
            nc.scalar.activation(k_pair[:, :, 0:SLOTS:2, :], doubled(qk_f[:, TILES * H:2 * TILES * H, :]), ACT.Copy).then_inc(k_high, 1)
            act.wait_ge(qk_scaled, 2)
            nc.scalar.activation(q_pair[:, :, 0:2, :], doubled(qk_f[:, 0:TILES * H, :]), ACT.Copy).then_inc(q_high, 1)
            for g in range(NG):
                act.wait_ge(q_turned, g + 1)
                nc.scalar.activation(qS[:, g, :], bank[:, NG + g, :].bitcast(F16), ACT.Copy).then_inc(qT_ready, 1)
            act.wait_ge(ld_rnn, 16 * 13)
            for w in (wx, bg):
                for g0, g1, f in ((0, 3, .5), (3, 4, 1.)):
                    nc.scalar.mul(w[:, g0:g1, :], w[:, g0:g1, :], A_SCALE * f).then_inc(w_ready, 1)
            for g0, g1, f in ((0, 3, .5), (3, 4, 1.)):
                nc.scalar.mul(wh[:, g0:g1, :], wh[:, g0:g1, :], W_SCALE * f).then_inc(w_ready, 1)
            act.wait_ge(w_ready, 6)
            nc.scalar.activation(wha[:].rearrange("p g n -> p (g n)"), wh[:].rearrange("p g n -> p (g n)"), ACT.Copy).then_inc(w_ready, 1)
            nc.scalar.mul(h0[:], condT[:], H_SCALE).then_inc(w_ready, 1)
            for w in range(2 * B * NG):
                act.wait_ge(score_mm, w + 1)
                if w >= 4:
                    act.wait_ge(pv_mm, w // 2 - 1)
                pair = w % 2
                nc.scalar.activation(p_cond[w % 4], bank[:, 2 * pair:2 * pair + 2, :].rearrange("p k n -> p (k n)"),
                                     ACT.Exp, scale=SCALE / QK_SCALE ** 2).then_inc(exp_done, 1)
            for k in range(2):
                act.wait_ge(oT_mm, k + 1)
                nc.scalar.activation(vT[:, 4 * k:4 * k + 4, :].rearrange("p t n -> p (t n)"), bank[:, k, :], ACT.Copy).then_inc(oT_ready, 1)
            join_roots(1)
            nc.scalar.preload_act_table_set(LN_EXP)
            front_roots(2)
            root(col(23), col(10))
            for k in range(2):
                act.wait_ge(v_turned, 3 + k)
                nc.scalar.activation(vT[:, 4 * k:4 * k + 4, :].rearrange("p t n -> p (t n)"), bank[:, k, :], ACT.Copy).then_inc(vT_ready, 1)
            for t in range(TILES):
                act.wait_ge(f1n_mm, t + 1)
                nc.scalar.activation(q_sq[:].rearrange("p a t h d -> p (a t h d)")[:, 0:FF], bank[:, 4 + t % 2, :], ACT.Square,
                                     accum_out=sm[:, 20, t:t + 1]).then_inc(f1_norm, 1)
                act.wait_ge(f1_norm, t + 1)
            root(col(23), col(20))
            join_roots(2)
            for k in range(2):
                act.wait_ge(co_turned, k + 1)
                nc.scalar.activation(vT[:, 4 * k:4 * k + 4, :].rearrange("p t n -> p (t n)"), bank[:, k, :], ACT.Copy).then_inc(co_ready, 1)
            for k in range(2):
                act.wait_ge(c_mm, k + 1)
                nc.scalar.activation(cT[:, 512 * k:512 * k + 512], bank[0:64, 2 + k, :], ACT.Copy).then_inc(c_ready, 1)
            for k in range(2):
                act.wait_ge(u_mm, k + 1)
                nc.scalar.mul(flat(qT[:, 4 * k:4 * k + 4, :]), bank[:, k, :], SCALE).then_inc(mq_ready, 1)

            def m_exp(m):
                act.wait_ge(mx_ready, m + 1)
                if m >= 2:
                    act.wait_ge(mt_mm, m - 1)
                n = P * (UNITS[m][0] + 1)
                for j in range(512 // n):
                    ins = nc.scalar.activation(p_mla[:, m % 2, j * n:(j + 1) * n], bank[:, m % 2, j * n:(j + 1) * n],
                                               ACT.Exp, bias=mx[:, m % 2, j:j + 1])
                ins.then_inc(mp_ready, 1)

            for m in range(FIRST_UNITS):
                m_exp(m)

            def gelu(c):
                act.wait_ge(ff_mm, c + 1)
                if c >= 2:
                    act.wait_ge(y_mm, c - 1)
                for f in range(FC):
                    ins = nc.scalar.activation(gel[:, c % 2, f, :], bank[:, c % 2, f * P:(f + 1) * P], ACT.Gelu,
                                               scale=1.0 / H_SCALE, bias=b1s[:, f:f + 1])
                ins.then_inc(gel_ready, 1)

            def act_jobs(t):
                m, w = divmod(t, 3)
                if w == 0 and 1 <= m <= SECOND_UNITS:
                    yield lambda: m_exp(FIRST_UNITS + m - 1)
                if t >= FFN_FROM and (t - FFN_FROM) % FFN_EVERY == 3 and (t - FFN_FROM) // FFN_EVERY < CHUNKS - 1:
                    yield lambda: gelu((t - FFN_FROM) // FFN_EVERY)

            for t in range(S):
                k = t % 2
                src = bank[:, 6 + (t // STEPS) % 2, (t % STEPS) * GW:(t % STEPS + 1) * GW]
                if t == 0:
                    act.wait_ge(c_new, 1)
                act.wait_ge(gates_mm, t + 1)
                nc.scalar.activation(gates[:, k, 0:GW], src, ACT.Tanh, scale=1.0 / A_SCALE).then_inc(gates_act, 1)
                act.wait_ge(c_new, t + 2)
                nc.scalar.activation(th[:, k, :], gates[:, 1 - k, 4 * B:5 * B], ACT.Tanh, scale=0.5).then_inc(th_act, 1)
                for job in act_jobs(t):
                    job()
            gelu(CHUNKS - 1)

        @block.vector
        def _(vec):
            counts = {}

            def step(ins, signal=None):
                s = dve if signal is None else signal
                ins.then_inc(s, 1)
                counts[id(s)] = counts.get(id(s), 0) + 1
                vec.wait_ge(s, counts[id(s)])

            V = nc.vector

            def wide(a):
                return a.unsqueeze(2).to_broadcast([P, TILES, D])

            vec.wait_ge(ld_ada, 48)
            step(V.tensor_scalar(ada_b[:, D:2 * D], ada_b[:, D:2 * D], 1.0, None, ALU.add))
            step(V.tensor_scalar(ada_b[:, 4 * D:5 * D], ada_b[:, 4 * D:5 * D], 1.0, None, ALU.add))
            vec.wait_ge(cond_t, 1)
            step(V.tensor_copy(condT[:], bank[:, 0, 0:B]))
            step(V.tensor_copy(condB[:], condT[:].unsqueeze(2).to_broadcast([P, B, P])), cond_bc)

            def col(k):
                return sm[:, k, :]

            def rsqrt(a, y, t):
                vec.wait_ge(roots_out, counts[id(roots_in)])
                step(V.tensor_tensor(t, y, y, ALU.mult))
                step(V.scalar_tensor_tensor(t, t, -0.5, a, ALU.mult, ALU.mult))
                step(V.scalar_tensor_tensor(y, t, 1.5, y, ALU.add, ALU.mult))

            def front(src, part):
                step(V.tensor_reduce(col(0), src[:], AX.X, ALU.add))
                step(V.tensor_scalar(col(2), col(0), 1.0 / D, None, ALU.mult))
                step(V.tensor_tensor(ta[:], src[:], wide(col(2)), ALU.subtract))
                step(V.tensor_tensor(tb[:], ta[:], ta[:], ALU.mult))
                step(V.tensor_reduce(col(3), tb[:], AX.X, ALU.add))
                step(V.tensor_tensor(col(4), col(2), col(0), ALU.mult))
                step(V.tensor_tensor(col(1), col(4), col(3), ALU.add))
                step(V.tensor_scalar(col(4), col(1), TINY, None, ALU.max), roots_in)
                rsqrt(col(4), col(21), col(22))
                step(V.tensor_tensor(col(4), col(4), col(21), ALU.mult))
                step(V.tensor_scalar(col(4), col(4), MAX_TANH_ARG, None, ALU.min))
                step(V.tensor_scalar(col(5), col(4), -1.0, 1.0, ALU.mult, ALU.add))
                step(V.reciprocal(col(6), col(5)))
                step(V.scalar_tensor_tensor(col(6), col(4), 1.0, col(6), ALU.add, ALU.mult), ratio_ready)
                step(V.tensor_tensor(col(8), col(4), col(4), ALU.mult))
                step(V.tensor_scalar(col(9), col(8), 1.0 / 13, None, ALU.mult))
                for k in (11, 9, 7, 5, 3):
                    step(V.scalar_tensor_tensor(col(9), col(9), 1.0 / k, col(8), ALU.add, ALU.mult))
                step(V.tensor_scalar(col(9), col(9), 1.0, None, ALU.add))
                step(V.tensor_scalar(col(5), col(4), SERIES_TO, None, ALU.is_lt))
                vec.wait_ge(ln_ready, counts[id(ratio_ready)])
                step(V.scalar_tensor_tensor(col(7), col(7), 0.5, col(21), ALU.mult, ALU.mult))
                step(V.tensor_tensor(col(9), col(9), col(7), ALU.subtract))
                step(V.tensor_tensor(col(9), col(9), col(5), ALU.mult))
                step(V.tensor_tensor(col(9), col(9), col(7), ALU.add))
                step(V.tensor_tensor(col(4), col(9), col(9), ALU.mult))
                step(V.scalar_tensor_tensor(col(4), col(4), 1.0 / D, col(3), ALU.mult, ALU.mult))
                step(V.tensor_scalar(col(4), col(4), LN_EPS, None, ALU.add), roots_in)
                rsqrt(col(4), col(21), col(22))
                step(V.tensor_tensor(col(4), col(21), col(9), ALU.mult))
                vec.wait_ge(ada_ready, B)
                step(V.tensor_tensor(ta[:], ta[:], wide(col(4)), ALU.mult))
                step(V.tensor_tensor(ta[:].rearrange("p (b h) d -> p b h d", b=B), ta[:].rearrange("p (b h) d -> p b h d", b=B),
                                     ada[:, :, part + 1, :].unsqueeze(2).to_broadcast([P, B, HALVES, D]), ALU.mult))
                step(V.tensor_tensor(v_tm[:].rearrange("p (b h) d -> p b h d", b=B), ta[:].rearrange("p (b h) d -> p b h d", b=B),
                                     ada[:, :, part, :].unsqueeze(2).to_broadcast([P, B, HALVES, D]), ALU.add))
                step(V.tensor_tensor(tb[:], v_tm[:], v_tm[:], ALU.mult))
                step(V.tensor_reduce(col(10), tb[:], AX.X, ALU.add))
                step(V.tensor_scalar(col(23), col(10), TINY, None, ALU.max), roots_in)
                rsqrt(col(23), col(10), col(22))
                step(V.tensor_scalar(col(10), col(10), CLIP, 1.0, ALU.mult, ALU.min))

            def join(src, part, dst, signal):
                step(V.tensor_tensor(tb[:], ta[:], ta[:], ALU.mult))
                step(V.tensor_reduce(col(11), tb[:], AX.X, ALU.add))
                step(V.tensor_scalar(col(23), col(11), TINY, None, ALU.max), roots_in)
                rsqrt(col(23), col(11), col(22))
                step(V.tensor_scalar(col(11), col(11), CLIP, 1.0, ALU.mult, ALU.min))
                step(V.tensor_tensor(ta[:], ta[:], wide(col(11)), ALU.mult))
                step(V.tensor_tensor(ta[:].rearrange("p (b h) d -> p b h d", b=B), ta[:].rearrange("p (b h) d -> p b h d", b=B),
                                     ada[:, :, part, :].unsqueeze(2).to_broadcast([P, B, HALVES, D]), ALU.mult))
                step(V.tensor_tensor(tb[:], ta[:], ta[:], ALU.mult))
                step(V.tensor_reduce(col(11), tb[:], AX.X, ALU.add))
                step(V.tensor_scalar(col(23), col(11), TINY, None, ALU.max), roots_in)
                rsqrt(col(23), col(15), col(22))
                step(V.tensor_tensor(col(12), col(23), col(15), ALU.mult), tanh_in)
                step(V.tensor_tensor(tb[:], ta[:], src[:], ALU.mult))
                step(V.tensor_reduce(col(13), tb[:], AX.X, ALU.add))
                vec.wait_ge(tanh_out, counts[id(tanh_in)])
                step(V.tensor_tensor(col(15), col(15), col(14), ALU.mult))
                step(V.tensor_tensor(col(13), col(13), col(15), ALU.mult))
                step(V.tensor_scalar(col(13), col(13), 2.0, 1.0, ALU.mult, ALU.add))
                step(V.tensor_tensor(col(16), col(15), col(15), ALU.mult))
                step(V.tensor_tensor(col(16), col(16), col(11), ALU.mult))
                step(V.tensor_tensor(col(17), col(13), col(16), ALU.add))
                step(V.tensor_tensor(col(16), col(16), col(1), ALU.mult))
                step(V.tensor_tensor(col(16), col(16), col(13), ALU.add))
                step(V.tensor_scalar(col(16), col(16), EPS, None, ALU.max))
                step(V.reciprocal(col(16), col(16)))
                step(V.tensor_scalar(col(18), col(1), -1.0, 1.0, ALU.mult, ALU.add))
                step(V.tensor_tensor(col(18), col(18), col(15), ALU.mult))
                step(V.tensor_tensor(col(18), col(18), col(16), ALU.mult))
                step(V.tensor_tensor(col(17), col(17), col(16), ALU.mult))
                step(V.tensor_tensor(ta[:], ta[:], wide(col(18)), ALU.mult))
                step(V.tensor_tensor(tb[:], src[:], wide(col(17)), ALU.mult))
                step(V.tensor_tensor(dst[:], ta[:], tb[:], ALU.add), signal)

            vec.wait_ge(ld_x, 16)
            front(x_tm, 0)
            step(V.tensor_copy(col(19), col(10)), v_ready)
            vec.wait_ge(ld_qkv, 96)
            for t in range(TILES):
                vec.wait_ge(qkv_mm, t + 1)
                V.scalar_tensor_tensor(q_tm[:, :, t].rearrange("p a h d -> p a (h d)"),
                                       bank[:, 2 + t % 4, 0:3 * D].rearrange("p (a n) -> p a n", a=3), sm[:, 10, t:t + 1],
                                       bqkv[:], ALU.mult, ALU.add).then_inc(qkv_ready, 1)
            vec.wait_ge(squares, 1)
            hn_f = hn[:].rearrange("p a t h -> p (a t) h")
            hn_g = hn[:].rearrange("p a t h -> p (a t h)")
            q_f = q_tm[:].rearrange("p a t h d -> p (a t h) d")
            step(V.tensor_reduce(hn_g, q_sq[:].rearrange("p a t h d -> p (a t h) d"), AX.X, ALU.add))
            step(V.tensor_reduce(nq[:, 0, :], hn_f, AX.X, ALU.add))
            step(V.tensor_scalar(nq[:, 1, :], nq[:, 0, :], TINY, None, ALU.max), roots_in)
            rsqrt(nq[:, 1, :], nq[:, 0, :], nq[:, 2, :])
            step(V.tensor_scalar(nq[:, 0, :], nq[:, 0, :], CLIP, 1.0, ALU.mult, ALU.min))
            step(V.tensor_scalar(nq[:, 0, :], nq[:, 0, :], HEADS_UP, None, ALU.mult))
            step(V.tensor_scalar(hn_x, hn_g, TINY, None, ALU.max), roots_in)
            rsqrt(hn_x, hn_g, hn_t)
            step(V.tensor_scalar(hn_g, hn_g, CLIP, None, ALU.mult))
            step(V.tensor_tensor(hn_f, hn_f, nq[:, 0, :].unsqueeze(2).to_broadcast([P, 3 * TILES, H]), ALU.min))
            n = TILES * H
            for a in (1, 0):
                V.scalar_tensor_tensor(q_f[:, a * n:a * n + n, :], q_f[:, a * n:a * n + n, :], QK_SCALE,
                                       hn_g[:, a * n:a * n + n].unsqueeze(2).to_broadcast([P, n, HD]), ALU.mult, ALU.mult).then_inc(qk_scaled, 1)
            vec.wait_ge(qk_scaled, 2)
            vec.wait_ge(k_high, 1)
            V.tensor_tensor(k_pair[:, :, 1:SLOTS:2, :], doubled(q_f[:, n:2 * n, :]), k_pair[:, :, 0:SLOTS:2, :], ALU.subtract).then_inc(k_low, 1)
            vec.wait_ge(q_high, 1)
            V.tensor_tensor(q_pair[:, :, 2:SLOTS, :], doubled(q_f[:, 0:n, :]), q_pair[:, :, 0:2, :], ALU.subtract).then_inc(q_low, 1)
            vec.wait_ge(zeros, 1)
            step(V.tensor_tensor(vaug[:].rearrange("p t h v -> p (t h) v")[:, :, 0:HD], q_f[:, 2 * n:3 * n, :],
                                 hn_g[:, 2 * n:3 * n].unsqueeze(2).to_broadcast([P, TILES * H, HD]), ALU.mult))
            step(V.memset(vaug[:, :, :, HD:HD + 1], HEADS_UP), vaug_ready)
            vec.wait_ge(w_ready, 8)
            step(V.tensor_tensor(whb[:], wh[:], wha[:], ALU.subtract), h_ready)
            for g in range(NG):
                vec.wait_ge(k_turned, g + 1)
                V.tensor_copy(kS[:, g, :], bank[:, g, :].bitcast(F16)).then_inc(kT_ready, 1)

            def o_copy(u):
                vec.wait_ge(pv_mm, u + 1)
                if u >= 2:
                    vec.wait_ge(o_turned, u - 1)
                V.tensor_copy(oTs[:, u % 2, :], bank[:, 4 + u % 2, 0:S]).then_inc(o_copied, 1)

            def o_norm(u):
                vec.wait_ge(o_turned, u + 1)
                g, bb = divmod(u, B)
                tr = bank[:, 6 + u % 2, 0:S].rearrange("p (h j v) -> p h j v", h=HALVES, j=GROUP)
                step(V.reciprocal(rd[:, u % 2], tr[:, :, :, HD]))
                o4 = o_tm[:].rearrange("p t (g j d) -> p t g j d", g=NG, d=HD)
                V.tensor_tensor(o4[:, HALVES * bb:HALVES * bb + HALVES, g], tr[:, :, :, 0:HD],
                                rd[:, u % 2].unsqueeze(3).to_broadcast([P, HALVES, GROUP, HD]), ALU.mult).then_inc(o_normed, 1)

            for u in range(B * NG):
                o_copy(u)
                if u:
                    o_norm(u - 1)
            o_norm(B * NG - 1)
            vec.wait_ge(ld_cff, 16 * 7)
            vec.wait_ge(attn_mm, 1)
            step(V.tensor_tensor(ta[:], bank[:, 2:4, :].rearrange("p k (t n) -> p (k t) n", n=D),
                                 bo_c[:].unsqueeze(1).to_broadcast([P, TILES, D]), ALU.add))
            join(x_tm, 2, x1_tm, dve)
            front(x1_tm, 3)
            step(V.tensor_tensor(v_tm[:], v_tm[:], wide(col(10)), ALU.mult), v_ready)
            for f in range(FC):
                for k in range(2):
                    i = 2 * f + k
                    vec.wait_ge(f1_mm, i + 1)
                    V.tensor_scalar(f1_slot(f, k),
                                    bank[:, 2 + i % 2, :], bf1_col[:, f:f + 1], None, ALU.add).then_inc(f1_ready, 1)
            vec.wait_ge(f1_norm, TILES)
            step(V.tensor_scalar(col(23), col(20), TINY, None, ALU.max), roots_in)
            rsqrt(col(23), col(20), col(22))
            step(V.tensor_scalar(col(20), col(20), CLIP, 1.0, ALU.mult, ALU.min))
            vec.wait_ge(f2_mm, 1)
            step(V.tensor_tensor(ta[:], bank[:, 6:8, :].rearrange("p k (t n) -> p (k t) n", n=D), wide(col(20)), ALU.mult))
            step(V.tensor_tensor(ta[:], ta[:], bf2[:].unsqueeze(1).to_broadcast([P, TILES, D]), ALU.add))
            join(x1_tm, 5, v_tm, cond_out)

            step(V.memset(vaug[:, :, :, HD:HD + 1], 1.0))
            for k in range(2):
                vec.wait_ge(u_mm, 3 + k)
                V.tensor_copy(flat(kT[:, 4 * k:4 * k + 4, :]), bank[:, 2 + k, :]).then_inc(mk_ready, 1)
            for k in range(2):
                vec.wait_ge(mv_mm, k + 1)
                V.tensor_copy(vaug[:, 4 * k:4 * k + 4, :, 0:HD], bank[:, 4 + k, :].rearrange("p (t h d) -> p t h d", t=4, h=H)).then_inc(mv_ready, 1)

            def m_max(m):
                half = UNITS[m][0]
                n = P * (half + 1)
                vec.wait_ge(ms_mm, m + 1)
                if m >= 2:
                    vec.wait_ge(mp_ready, m - 1)
                V.tensor_reduce(mx[:, m % 2, 0:512 // n], bank[:, m % 2, :].rearrange("p (j n) -> p j n", n=n), AX.X, ALU.max,
                                negate=True).then_inc(mx_ready, 1)

            def m_weights(m):
                vec.wait_ge(mt_mm, m + 1)
                if m >= 2:
                    vec.wait_ge(mpv_mm, m - 1)
                V.tensor_copy(pt_mla[:, m % 2, :], bank[:, 2 + m % 2, :]).then_inc(mt_ready, 1)

            def m_out(g):
                vec.wait_ge(mpv_mm, last_unit(g) + 1)
                if g >= 2:
                    vec.wait_ge(mo_turned, g - 1)
                V.tensor_copy(oTs[:, g % 2, 0:P], bank[:, 4, 0:P]).then_inc(mo_copied, 1)

            def m_norm(g):
                half, hg, b = GROUPS[g]
                vec.wait_ge(mo_turned, g + 1)
                tr = bank[:, 5, 0:P].rearrange("p (j v) -> p j v", j=GROUP)
                step(V.reciprocal(rdm[:, g % 2], tr[:, :, HD]))
                o4 = o_tm[:].rearrange("p t (g j d) -> p t g j d", g=NG, d=HD)
                V.tensor_tensor(o4[:, HALVES * b + half, hg], tr[:, :, 0:HD],
                                rdm[:, g % 2].unsqueeze(2).to_broadcast([P, GROUP, HD]), ALU.mult).then_inc(mo_normed, 1)

            def m_oT(half):
                vec.wait_ge(moT_mm, half + 1)
                V.tensor_copy(oT[:, half * 512:half * 512 + 512].rearrange("p (t b) -> p t b", b=B),
                              bank[:, 0, :].rearrange("p (b t) -> p t b", b=B)).then_inc(moT_ready, 1)

            def m_x1(half):
                vec.wait_ge(x1_mm, half + 1)
                V.tensor_copy(x1T[:, half * 512:half * 512 + 512], bank[:, 1, :]).then_inc(x1_ready, 1)

            m_max(0)
            for m in range(FIRST_UNITS):
                if m + 1 < FIRST_UNITS:
                    m_max(m + 1)
                m_weights(m)
                if m >= 1:
                    m_out(m - 1)
                if m >= 2:
                    m_norm(m - 2)
            m_out(FIRST_UNITS - 1)
            m_norm(FIRST_UNITS - 2)
            m_norm(FIRST_UNITS - 1)
            m_oT(0)
            m_x1(0)

            step(V.memset(gates[:], 0.0), c_new)

            def result(c):
                vec.wait_ge(y_mm, c + 1)
                vec.wait_ge(ld_xtb, 64)
                if c >= 2:
                    vec.wait_ge(stored[c % 2], 16 * (c // 2))
                V.tensor_tensor(o_sb[:, c % 2, :], bank[:, 2 + c % 2, 0:D], x_tb[:, c, :], ALU.add).then_inc(y_ready, 1)

            def vec_jobs(t):
                m, w = divmod(t, 3)
                if w == 2 and m < SECOND_UNITS:
                    yield lambda: m_max(FIRST_UNITS + m)
                if w == 1 and 1 <= m <= SECOND_UNITS:
                    yield lambda: m_weights(FIRST_UNITS + m - 1)
                if w == 0 and m >= 3 and m % 2 == 1 and m <= SECOND_UNITS + 1:
                    yield lambda: m_out(FIRST_UNITS + (m - 3) // 2)
                if w == 0 and m >= 4 and m % 2 == 0 and m <= SECOND_UNITS + 2:
                    yield lambda: m_norm(FIRST_UNITS + (m - 4) // 2)
                if t == TAIL_FROM + 4:
                    yield lambda: m_oT(1)
                if t == TAIL_FROM + 10:
                    yield lambda: m_x1(1)
                if t >= FFN_FROM and (t - FFN_FROM) % FFN_EVERY == 12 and (t - FFN_FROM) // FFN_EVERY < CHUNKS - 1:
                    yield lambda: result((t - FFN_FROM) // FFN_EVERY)

            for t in range(S):
                k = t % 2
                vec.wait_ge(gates_act, t + 1)
                V.scalar_tensor_tensor(pr[:, k, :], gates[:, k, B:3 * B], 1.0, gates[:, k, 3 * B:5 * B], ALU.add, ALU.mult).then_inc(p_ready, 1)
                V.tensor_scalar(so[:, k, :], gates[:, k, 0:B], 1.0, 0.5 * H_SCALE, ALU.add, ALU.mult).then_inc(so_ready, 1)
                vec.wait_ge(p_ready, t + 1)
                V.scalar_tensor_tensor(gates[:, 1 - k, 4 * B:5 * B], pr[:, k, B:2 * B], 0.5, pr[:, k, 0:B], ALU.mult, ALU.add).then_inc(c_new, 1)
                vec.wait_ge(th_act, t + 1)
                V.tensor_tensor(ha[:, k, :], so[:, k, :], th[:, k, :], ALU.mult).then_inc(h_ready, 1)
                hs = hist[:, t, :]
                V.tensor_tensor(hs, so[:, k, :], th[:, k, :], ALU.mult).then_inc(hist_ready, 1)
                vec.wait_ge(hist_ready, t + 1)
                V.tensor_tensor(hb[:, k, :], hs, ha[:, k, :], ALU.subtract).then_inc(hb_ready, 1)
                for job in vec_jobs(t):
                    job()
            result(CHUNKS - 1)

        @block.tensor
        def _(pe):
            T = nc.tensor
            pe.wait_ge(consts, 9)
            pe.wait_ge(ld_ada, 48)
            T.transpose(bank[:, 0, 0:B], cond4[:], ident[0:B, 0:B]).then_inc(cond_t, 1)
            pe.wait_ge(cond_bc, 1)
            pe.wait_ge(dve, 2)
            for bb in range(B):
                for k, (a, z) in enumerate(((0, 512), (512, 6 * D))):
                    T.matmul(bank[:, 2 * bb + k, 0:z - a], condB[:, bb, :], ada_w[:, a:z], start=True, stop=False)
                    ins = T.matmul(bank[:, 2 * bb + k, 0:z - a], ones[:], ada_b[:, a:z], start=False, stop=True)
                ins.then_inc(ada_mm, 1)

            def turn8(src, base, signal):
                for k in range(2):
                    for t in range(4):
                        ins = T.transpose(bank[:, base + k, t * P:(t + 1) * P], src(4 * k + t), ident[:])
                    ins.then_inc(signal, 1)

            pe.wait_ge(v_ready, 1)
            pe.wait_ge(ada_ready, B)
            turn8(lambda t: v_tm[:, t, :], 0, v_turned)
            pe.wait_ge(ld_qkv, 96)
            for t in range(TILES):
                pe.wait_ge(vT_ready, 1 + t // 4)
                if t >= 4:
                    pe.wait_ge(qkv_ready, t - 3)
                T.matmul(bank[:, 2 + t % 4, 0:3 * D], vT[:, t, :], wqkv[:].rearrange("p a n -> p (a n)"), start=True, stop=True).then_inc(qkv_mm, 1)
            for pair, low, base, signal in ((k_pair, k_low, 0, k_turned), (q_pair, q_low, NG, q_turned)):
                pe.wait_ge(low, 1)
                stacks = pair.rearrange("p (t g j) s d -> p t g (j s d)", t=TILES, g=NG)
                for g in range(NG):
                    for t in range(TILES):
                        ins = T.transpose(bank[:, base + g, :].bitcast(F16)[:, t * P:(t + 1) * P], stacks[:, t, g], identh[:])
                    ins.then_inc(signal, 1)

            def scores(w):
                u, pair = divmod(w, 2)
                g, bb = divmod(u, B)
                if w >= 2:
                    pe.wait_ge(exp_done, w - 1)
                if w % (2 * B) == 0:
                    pe.wait_ge(slab_group[g], 16 * GROUP)
                h = GROUP * g + 2 * pair
                for kc in range(HALVES):
                    ins = T.matmul(bank[:, 2 * (w % 2) + kc, :], kS[:, g, bb * S + kc * P:bb * S + (kc + 1) * P],
                                   q_slab[:, h:h + 2, bb * S:(bb + 1) * S], start=True, stop=True)
                ins.then_inc(score_mm, 1)

            def values(u):
                g, bb = divmod(u, B)
                pe.wait_ge(exp_done, 2 * u + 2)
                if u >= 2:
                    pe.wait_ge(o_copied, u - 1)
                for kc in range(HALVES):
                    for j in range(GROUP):
                        ins = T.matmul(bank[VP * j:VP * j + VP, 4 + u % 2, 0:S], vaug[:, HALVES * bb + kc, GROUP * g + j, :],
                                       p_cond[(2 * u + j // 2) % 4][:, (2 * kc + j % 2) * S:(2 * kc + j % 2 + 1) * S],
                                       start=(kc == 0), stop=(kc == 1), tile_position=(0, VP * j))
                ins.then_inc(pv_mm, 1)

            def o_turn(u):
                pe.wait_ge(o_copied, u + 1)
                if u >= 2:
                    pe.wait_ge(o_normed, u - 1)
                for half in range(HALVES):
                    ins = T.transpose(bank[:, 6 + u % 2, half * P:(half + 1) * P], oTs[:, u % 2, half * P:(half + 1) * P], ident[:])
                ins.then_inc(o_turned, 1)

            pe.wait_ge(qT_ready, NG)
            pe.wait_ge(kT_ready, NG)
            pe.wait_ge(vaug_ready, 1)
            N = 2 * B * NG
            for w in range(2):
                scores(w)
            for u in range(B * NG):
                for w in (2 * u + 2, 2 * u + 3):
                    if w < N:
                        scores(w)
                values(u)
                if u:
                    o_turn(u - 1)
            o_turn(B * NG - 1)
            pe.wait_ge(o_normed, B * NG)
            turn8(lambda t: o_tm[:, t, :], 0, oT_mm)
            pe.wait_ge(ld_cff, 16 * 7)
            for t in range(TILES):
                pe.wait_ge(oT_ready, 1 + t // 4)
                ins = T.matmul(bank[:, 2 + t // 4, (t % 4) * P:(t % 4 + 1) * P], vT[:, t, :], wo_c[:], start=True, stop=True)
            ins.then_inc(attn_mm, 1)
            pe.wait_ge(v_ready, 2)
            turn8(lambda t: v_tm[:, t, :], 0, v_turned)
            pe.wait_ge(vT_ready, 4)
            for f in range(FC):
                for k in range(2):
                    i = 2 * f + k
                    if i >= 2:
                        pe.wait_ge(f1_ready, i - 1)
                    T.matmul(bank[:, 2 + i % 2, :], wf1[:, f * P:(f + 1) * P], vT[:, 4 * k:4 * k + 4, :].rearrange("p t n -> p (t n)"),
                             start=True, stop=True).then_inc(f1_mm, 1)
                    t = i
                    if t >= 2:
                        pe.wait_ge(f1_norm, t - 1)
                    T.matmul(bank[:, 4 + t % 2, :], vT[:, t, :], wf1[:], start=True, stop=False)
                    T.matmul(bank[:, 4 + t % 2, :], ones[:], bf1_row[:], start=False, stop=True).then_inc(f1n_mm, 1)
            pe.wait_ge(f1_ready, 2 * FC)
            for t in range(TILES):
                for f in range(FC):
                    ins = T.matmul(bank[:, 6 + t // 4, (t % 4) * P:(t % 4 + 1) * P], f1_slot(f, t // 4)[:, (t % 4) * P:(t % 4 + 1) * P],
                                   wf2[:, f, :], start=(f == 0), stop=(f == FC - 1))
            ins.then_inc(f2_mm, 1)
            pe.wait_ge(cond_out, 1)
            turn8(lambda t: v_tm[:, t, :], 0, co_turned)
            pe.wait_ge(ld_mla, 16 * 6)
            for k in range(2):
                pe.wait_ge(co_ready, k + 1)
                T.matmul(bank[0:64, 2 + k, :], wd[:].rearrange("p a n -> p (a n)"), flat(vT[:, 4 * k:4 * k + 4, :]),
                         start=True, stop=True).then_inc(c_mm, 1)
            pe.wait_ge(c_ready, 2)
            for j in range(2):
                for k in range(2):
                    T.matmul(bank[:, 2 * j + k, :], wu[32 * j:32 * j + 32, 0, :], cT[32 * j:32 * j + 32, 512 * k:512 * k + 512],
                             start=True, stop=True).then_inc(u_mm, 1)
            for k in range(2):
                for t in range(4):
                    ins = T.matmul(bank[:, 4 + k, t * P:(t + 1) * P], cT[32:64, (4 * k + t) * P:(4 * k + t + 1) * P], wu[32:64, 1, :],
                                   start=True, stop=True)
                ins.then_inc(mv_mm, 1)
            kT_flat = flat(kT[:])

            def m_scores(m, part=None):
                half, g, b, i = UNITS[m]
                n = P * (half + 1)
                per = 512 // n
                if part in (None, 0):
                    if m >= 2:
                        pe.wait_ge(mp_ready, m - 1)
                    T.matmul(bank[:, m % 2, :], identb[:], (mask0, mask1)[half][:], start=True, stop=True)
                js = range(per) if part is None else [part]
                for j in js:
                    h = GROUP * g + 2 * i + j
                    ins = T.matmul(bank[:, m % 2, j * n:(j + 1) * n], qz[:, h, b * S + half * P:b * S + half * P + P],
                                   kT_flat[:, b * S:b * S + n], start=False, stop=True, skip_group_check=True)
                if js[-1] == per - 1:
                    ins.then_inc(ms_mm, 1)

            def m_turn(m):
                pe.wait_ge(mp_ready, m + 1)
                if m >= 2:
                    pe.wait_ge(mt_ready, m - 1)
                for i in range(4):
                    ins = T.transpose(bank[:, 2 + m % 2, i * P:(i + 1) * P], p_mla[:, m % 2, i * P:(i + 1) * P], ident[:])
                ins.then_inc(mt_mm, 1)

            def m_values(m):
                half, _, b, _ = UNITS[m]
                g = group_of(m)
                pe.wait_ge(mt_ready, m + 1)
                if g >= 1:
                    pe.wait_ge(mo_copied, g)
                for i, (h, j, kc) in enumerate(blocks(m)):
                    ins = T.matmul(bank[VP * j:VP * j + VP, 4, 0:P], vaug[:, HALVES * b + kc, h, :], pt_mla[:, m % 2, i * P:(i + 1) * P],
                                   start=(kc == 0), stop=(kc == half), tile_position=(0, VP * j))
                ins.then_inc(mpv_mm, 1)

            def m_back(g):
                pe.wait_ge(mo_copied, g + 1)
                if g >= 1:
                    pe.wait_ge(mo_normed, g)
                T.transpose(bank[:, 5, 0:P], oTs[:, g % 2, 0:P], ident[:]).then_inc(mo_turned, 1)

            def m_turn_out(half):
                pe.wait_ge(mo_normed, (half + 1) * FIRST_UNITS)
                for b in range(B):
                    ins = T.transpose(bank[:, 0, b * P:(b + 1) * P], o_tm[:, HALVES * b + half, :], ident[:])
                ins.then_inc(moT_mm, 1)

            def m_x1(half, c):
                if c == 0:
                    pe.wait_ge(moT_ready, half + 1)
                i = half * 4 + c
                T.matmul(bank[:, 1, c * P:(c + 1) * P], wo_m[:], oT[:, i * P:(i + 1) * P], start=True, stop=False)
                ins = T.matmul(bank[:, 1, c * P:(c + 1) * P], x_tb[:, i, :], ident[:], start=False, stop=True)
                if c == 3:
                    ins.then_inc(x1_mm, 1)

            pe.wait_ge(mv_ready, 2)
            pe.wait_ge(mq_ready, 2)
            pe.wait_ge(mk_ready, 2)
            pe.wait_ge(qz_group[0], 16 * GROUP)
            m_scores(0)
            for m in range(FIRST_UNITS):
                if m + 1 < FIRST_UNITS:
                    if (m + 1) % B == 0:
                        pe.wait_ge(qz_group[(m + 1) // B], 16 * GROUP)
                    m_scores(m + 1)
                if m >= 1:
                    m_values(m - 1)
                m_turn(m)
                if m >= 2:
                    m_back(m - 2)
            m_values(FIRST_UNITS - 1)
            m_back(FIRST_UNITS - 2)
            m_back(FIRST_UNITS - 1)
            pe.wait_ge(ld_xtb, 64)
            m_turn_out(0)
            for c in range(4):
                m_x1(0, c)
            pe.wait_ge(x1_ready, 1)
            pe.wait_ge(w_ready, 8)

            def inputs_of(c, g):
                acc = bank[:, 6 + c % 2, :].rearrange("p (t g b) -> p t g b", g=4, b=B)
                if g == 0 and c == 4:
                    pe.wait_ge(x1_ready, 2)
                T.matmul(acc[:, :, g, :], bg[:, g, :], ones[:].rearrange("a (t b) -> a t b", b=B), start=(g == 0), stop=True,
                         skip_group_check=True)
                T.matmul(acc[:, :, g, :], wx[:, g, :], x1T[:, c * P:(c + 1) * P], start=False, stop=True, skip_group_check=True)

            def ffn_up(c, fs=range(FC)):
                pe.wait_ge(hist_ready, STEPS * (c + 1))
                if c >= 2:
                    pe.wait_ge(gel_ready, c - 1)
                for f in fs:
                    ins = T.matmul(bank[:, c % 2, f * P:(f + 1) * P], w1s[:, f * P:(f + 1) * P],
                                   hist[:, c * STEPS:(c + 1) * STEPS, :].rearrange("p t b -> p (t b)"), start=True, stop=True)
                if fs[-1] == FC - 1:
                    ins.then_inc(ff_mm, 1)

            def ffn_down(c, part=(0, 1, 2)):
                pe.wait_ge(gel_ready, c + 1)
                if c >= 2:
                    pe.wait_ge(y_ready, c - 1)
                y = bank[:, 2 + c % 2, 0:D]
                if 0 in part:
                    T.matmul(y, ones[:], b2s[:], start=True, stop=False)
                    T.matmul(y, oT[:, c * P:(c + 1) * P], wo_m[:], start=False, stop=False)
                for f in (f for p in part if p for f in (2 * p - 2, 2 * p - 1)):
                    ins = T.matmul(y, gel[:, c % 2, f, :], w2s[:, f, :], start=False, stop=(f == FC - 1))
                if 2 in part:
                    ins.then_inc(y_mm, 1)

            for g in range(4):
                inputs_of(0, g)

            def pe_jobs(t):
                m, w = divmod(t, 3)
                if w == 0 and m < SECOND_UNITS:
                    yield lambda: m_scores(FIRST_UNITS + m, 0)
                if w == 1 and m < SECOND_UNITS:
                    yield lambda: m_scores(FIRST_UNITS + m, 1)
                if w == 1 and 1 <= m <= SECOND_UNITS:
                    yield lambda: m_turn(FIRST_UNITS + m - 1)
                if w == 2 and 1 <= m <= SECOND_UNITS:
                    yield lambda: m_values(FIRST_UNITS + m - 1)
                if w == 2 and m >= 3 and m % 2 == 1 and m <= SECOND_UNITS + 1:
                    yield lambda: m_back(FIRST_UNITS + (m - 3) // 2)
                if t == TAIL_FROM + 4:
                    yield lambda: m_turn_out(1)
                if TAIL_FROM + 6 <= t < TAIL_FROM + 10:
                    yield lambda: m_x1(1, t - TAIL_FROM - 6)
                if t % STEPS >= STEPS - 6 and t % STEPS < STEPS - 2 and t < S - STEPS:
                    yield lambda: inputs_of(t // STEPS + 1, t % STEPS - STEPS + 6)
                if t >= FFN_FROM and (t - FFN_FROM) // FFN_EVERY < CHUNKS - 1:
                    c, i = divmod(t - FFN_FROM, FFN_EVERY)
                    if i in (0, 2):
                        yield lambda: ffn_up(c, range(i, i + 2))
                    if i in (5, 7, 9):
                        yield lambda: ffn_down(c, ((i - 5) // 2,))

            for t in range(S):
                k = (t + 1) % 2
                acc = bank[:, 6 + (t // STEPS) % 2, (t % STEPS) * GW:(t % STEPS + 1) * GW]
                pe.wait_ge(h_ready, t + 1)

                def add(w, h):
                    for g in range(4):
                        ins = T.matmul(acc[:, g * B:(g + 1) * B], w[:, g, :], h, start=False, stop=True, skip_group_check=True)
                    return ins

                if t == 0:
                    add(wh, h0[:]).then_inc(gates_mm, 1)
                else:
                    add(wha, ha[:, k, :])
                    add(whb, ha[:, k, :])
                    pe.wait_ge(hb_ready, t)
                    add(wha, hb[:, k, :]).then_inc(gates_mm, 1)
                for job in pe_jobs(t):
                    job()
            ffn_up(CHUNKS - 1)
            ffn_down(CHUNKS - 1)


_INS = ['x', 'cond_1024', 'L0_cond_w_q', 'L0_cond_b_q', 'L0_cond_w_k', 'L0_cond_b_k', 'L0_cond_w_v', 'L0_cond_b_v',
        'L0_cond_w_o', 'L0_cond_b_o', 'L0_cond_w_f1', 'L0_cond_b_f1', 'L0_cond_w_f2', 'L0_cond_b_f2', 'L0_cond_w_ada',
        'L0_cond_b_ada', 'L0_attn_W_dq', 'L0_attn_W_uq', 'L0_attn_W_dkv', 'L0_attn_W_uk', 'L0_attn_W_uv', 'L0_attn_W_o',
        'L0_cond2_Wx', 'L0_cond2_Wh', 'L0_cond2_b', 'L0_ffn_w1', 'L0_ffn_b1', 'L0_ffn_w2', 'L0_ffn_b2']


def kernel(**inputs):
    import numpy as np
    import concourse.bacc as bacc
    from concourse.bass_utils import run_bass_kernel_spmd

    nc = bacc.Bacc("TRN2", target_bir_lowering=False, num_devices=1)
    arrays, args = {}, []
    for name in _INS:
        a = np.ascontiguousarray(inputs[name])
        arrays[f"in_{name}"] = a
        args.append(nc.dram_tensor(f"in_{name}", a.shape, mybir.dt.from_np(a.dtype), kind="ExternalInput").ap())
    args.append(nc.dram_tensor("out_y", (B, S, D), F32, kind="ExternalOutput").ap())
    adaln_attention_lstm_ffn(nc, *args)
    r = run_bass_kernel_spmd(nc, [arrays], core_ids=[0])
    return r.results[0]["out_y"]
```

```python
import math
from contextlib import ExitStack

import concourse.bass as bass
from concourse import mybir

ALU = mybir.AluOpType
ACT = mybir.ActivationFunctionType
AX = mybir.AxisListType
F32 = mybir.dt.float32
F16 = mybir.dt.float16
BF16 = mybir.dt.bfloat16

B, S, D, H = 4, 256, 128, 16
HD = D // H
FF = 512
P = 128
HALVES = S // P
TILES = B * HALVES
GROUP = 4
NG = H // GROUP
FC = FF // P
VP = 32

LN_EXP = "natural_log_exp_and_others"
TANH_EXP = "exp_and_others"

EPS = 1e-7
MAX_TANH_ARG = 1.0 - 1e-5
CLIP = math.atanh(0.9999899864196777)
LN_EPS = 1e-6
TINY = EPS * EPS
SERIES_TO = 0.25


def _beta(a, b):
    return math.exp(math.lgamma(a) + math.lgamma(b) - math.lgamma(a + b))


HEADS_UP = _beta(HD / 2, 0.5) / _beta(D / 2, 0.5)
SCALE = 1.0 / math.sqrt(HD)
MASKED = -1e30
QK_SCALE = 1024.0
SLOTS = 4

(X_SQ, ARG, IS_SMALL, LN_MINUS, LN_PLUS, N_SQ, ALPHA, V_FACTOR, NORM_SQ, U_NORM,
 XY, TANH_N, Y_FACTOR, Y_SQ, X_WEIGHT, U_WEIGHT, DENOM, F1_FACTOR, ROOT, NEWTON, GUARDED) = range(21)
SMALL_COLS = 21

STEPS = 32
CHUNKS = S // STEPS
GW = 4 * B
H_SCALE = 4096.0
W_SCALE = 16.0
A_SCALE = H_SCALE * W_SCALE
BF16_PARTS = 3
BIAS_ROWS = BF16_PARTS * 4


def adaln_attention_lstm_ffn(nc, x, cond, w_q, b_q, w_k, b_k, w_v, b_v, w_o, b_o, w_f1, b_f1, w_f2, b_f2,
                             w_ada, b_ada, W_dq, W_uq, W_dkv, W_uk, W_uv, W_o, Wx, Wh, b_g, w1, b1, w2, b2, out):
    with ExitStack() as ctx:
        def sb(name, shape, dt=F32):
            return ctx.enter_context(nc.sbuf_tensor(name, shape, dt))

        def ps(name, shape, dt=F32):
            return ctx.enter_context(nc.psum_tensor(name, shape, dt))

        def sem(name):
            return ctx.enter_context(nc.semaphore(name))

        ident = sb("ident", [P, P])
        identb = sb("identb", [P, P], BF16)
        identh = sb("identh", [P, P], F16)
        mask = sb("mask", [P, GROUP, P], BF16)
        ones = sb("ones", [1, P])
        cond4 = sb("cond4", [B, D])
        condT = sb("condT", [P, B])
        ada_w = sb("ada_w", [P, 6 * D])
        ada_b = sb("ada_b", [B, 6 * D])
        ada4 = sb("ada4", [B, 6 * D])
        ada = sb("ada", [P, B, 6, D])
        wqkv = sb("wqkv", [P, 3, D])
        bqkv = sb("bqkv", [P, 3, D])
        wo_c = sb("wo_c", [P, D])
        bo_c = sb("bo_c", [P, D])
        wf1 = sb("wf1", [P, FF])
        bf1_all = sb("bf1_all", [P, FF])
        wf2 = sb("wf2", [P, FC, D])
        bf2 = sb("bf2", [P, D])
        wd = sb("wd", [P, 2, 32])
        wu = sb("wu", [64, 2, D])
        w_mla = sb("w_mla", [P, 3, D])
        wo_m = sb("wo_m", [P, D])
        wx = sb("wx", [P, 4, D])
        wh = sb("wh", [P, 4, D])
        bg = sb("bg", [1, 4, D])
        bg_rows = sb("bg_rows", [BIAS_ROWS, D], BF16)
        gate_cols = sb("gate_cols", [BIAS_ROWS, STEPS * GW], BF16)
        wox = sb("wox", [P, 4, D])
        wha = sb("wha", [P, 4, D], F16)
        whb = sb("whb", [P, 4, D], F16)
        w1s = sb("w1s", [P, FF])
        b1s = sb("b1s", [P, FC])
        w2s = sb("w2s", [P, FC, D])
        b2s = sb("b2s", [1, D])
        x_tb = sb("x_tb", [P, CHUNKS, D])

        x_tm = sb("x_tm", [P, TILES, D])
        ta = sb("ta", [P, TILES, D])
        tb = sb("tb", [P, TILES, D])
        v_tm = sb("v_tm", [P, TILES, D])
        x1_tm = sb("x1_tm", [P, TILES, D])
        o_tm = sb("o_tm", [P, TILES, D])
        vT = sb("vT", [P, TILES, P])
        q_tm = sb("q_tm", [P, 3, TILES, H, HD])
        q_sq = sb("q_sq", [P, 3, TILES, H, HD])
        qT = sb("qT", [P, TILES, P])
        kT = sb("kT", [P, TILES, P])
        qz = sb("qz", [P, H, B * S])
        pairs = qz[:].rearrange("p h n -> p (h n)").bitcast(F16)
        kS, qS = (pairs[:, i * NG * B * S:(i + 1) * NG * B * S].rearrange("p (g n) -> p g n", g=NG) for i in range(2))
        k_pair, q_pair = (pairs[:, i * TILES * H * SLOTS * HD:(i + 1) * TILES * H * SLOTS * HD].rearrange(
            "p (t h s d) -> p (t h) s d", t=TILES, s=SLOTS, d=HD) for i in range(2, 4))
        q_slab = pairs[:, H * B * S:].rearrange("p (h n) -> p h n", h=H)
        vaug = sb("vaug", [P, TILES, H, VP])
        hn = sb("hn", [P, 3, TILES, H])
        p_mla = sb("p_mla", [P, 2, 512])
        p_cond = [a[:].rearrange("p a t h d -> p a (t h d)")[:, i, :] for a in (q_sq, q_tm) for i in range(3)]
        oTs = sb("oTs", [P, 2, S])
        rd = sb("rd", [P, 2, HALVES, GROUP])
        rdm = sb("rdm", [P, 2, GROUP])
        small = sb("small", [P, SMALL_COLS, TILES])
        st6 = sb("st6", [P, TILES, 6])
        mv = sb("mv", [P, TILES, 2])
        nq = sb("nq", [P, 3, 3 * TILES])
        hn_x = tb[:].rearrange("p t n -> p (t n)")[:, 0:3 * TILES * H]
        hn_t = tb[:].rearrange("p t n -> p (t n)")[:, 512:512 + 3 * TILES * H]
        mx = sb("mx", [P, 2, GROUP])
        pt_mla = q_sq[:].rearrange("p a t h d -> p (a t h d)")[:, 1024:2048].rearrange("p (a n) -> p a n", a=2)

        q_tm_flat = q_tm[:].rearrange("p a t h d -> p (a t h d)")
        wdT = q_tm_flat[0:64, 0:P]
        woT = q_tm_flat[:, 0:P]
        bg_parts = p_mla[0:1].rearrange("p a n -> p (a n)").bitcast(BF16)[:, 0:BIAS_ROWS * D].rearrange("p (r n) -> p r n", n=D)

        gates = sb("gates", [P, 2, 5 * B])
        so = sb("so", [P, 2, B])
        pr = sb("pr", [P, 2, 2 * B])
        th = sb("th", [P, 2, B])
        ha = sb("ha", [P, 2, B], F16)
        hb = sb("hb", [P, 2, B], F16)
        h0 = sb("h0", [P, B])
        hist = v_tm[:].rearrange("p t n -> p (t n)").rearrange("p (t b) -> p t b", b=B)
        gel = ta[:].rearrange("p (a f) n -> p a f n", a=2)
        o_sb = tb[:, 0:2, :]

        xT = x1_tm[:].rearrange("p t n -> p (t n)")
        oT = qT[:].rearrange("p t n -> p (t n)")

        bank = ps("bank", [P, 8, 512])

        ld_x = sem("ld_x")
        ld_ada = sem("ld_ada")
        ld_qkv = sem("ld_qkv")
        ld_cff = sem("ld_cff")
        ld_mla = sem("ld_mla")
        ld_rnn = sem("ld_rnn")
        ld_xtb = sem("ld_xtb")
        consts = sem("consts")
        zeros = sem("zeros")
        dve = sem("dve_chain")
        act_ch = sem("act_chain")
        squares = sem("squares")
        cond_t = sem("cond_t")
        cond_ready = sem("cond_ready")
        ada_mm = sem("ada_mm")
        ada_rows = sem("ada_rows")
        ada_ready = [sem("ada_msa_ready"), sem("ada_rest_ready")]
        roots_in = sem("roots_in")
        roots_out = sem("roots_out")
        ratio_ready = sem("ratio_ready")
        ln_ready = sem("ln_ready")
        v_ready = sem("v_ready")
        v_turned = sem("v_turned")
        vT_ready = sem("vT_ready")
        qkv_mm = sem("qkv_mm")
        qkv_ready = sem("qkv_ready")
        qk_scaled = sem("qk_scaled")
        k_high = sem("k_high")
        q_high = sem("q_high")
        k_low = sem("k_low")
        q_low = sem("q_low")
        q_turned = sem("q_turned")
        qT_ready = sem("qT_ready")
        k_turned = sem("k_turned")
        kT_ready = sem("kT_ready")
        qz_group = [sem(f"qz_group{g}") for g in range(NG)]
        slab_group = [sem(f"slab_group{g}") for g in range(NG)]
        vaug_zero = sem("vaug_zero")
        vaug_ready = sem("vaug_ready")
        score_mm = sem("score_mm")
        exp_done = sem("exp_done")
        pv_mm = sem("pv_mm")
        o_copied = sem("o_copied")
        o_turned = sem("o_turned")
        o_normed = sem("o_normed")
        oT_mm = sem("oT_mm")
        oT_ready = sem("oT_ready")
        attn_mm = sem("attn_mm")
        tanh_in = sem("tanh_in")
        tanh_out = sem("tanh_out")
        f1_mm = sem("f1_mm")
        f1_turned = sem("f1_turned")
        f1T_ready = sem("f1T_ready")
        f2_tile = sem("f2_tile")
        f1_norm = sem("f1_norm")
        f1_biased = sem("f1_biased")
        sq_in = sem("sq_in")
        sq_out = sem("sq_out")
        cond_out = sem("cond_out")
        co_turned = sem("co_turned")
        co_ready = sem("co_ready")
        wd_turned = sem("wd_turned")
        wdT_ready = sem("wdT_ready")
        w_mla_mm = sem("w_mla_mm")
        w_mla_ready = sem("w_mla_ready")
        mq_mm = sem("mq_mm")
        mk_mm = sem("mk_mm")
        mq_ready = sem("mq_ready")
        mk_ready = sem("mk_ready")
        mv_mm = sem("mv_mm")
        mv_ready = sem("mv_ready")
        ms_mm = sem("ms_mm")
        mx_ready = sem("mx_ready")
        mp_ready = sem("mp_ready")
        mt_mm = sem("mt_mm")
        mt_ready = sem("mt_ready")
        mpv_mm = sem("mpv_mm")
        mo_copied = sem("mo_copied")
        mo_turned = sem("mo_turned")
        mo_normed = sem("mo_normed")
        moT_mm = sem("moT_mm")
        moT_ready = sem("moT_ready")
        bias_part = sem("bias_part")
        bias_ready = sem("bias_ready")
        wo_turned = sem("wo_turned")
        woT_ready = sem("woT_ready")
        wox_mm = sem("wox_mm")
        wox_ready = sem("wox_ready")
        x_turned = sem("x_turned")
        xT_ready = sem("xT_ready")
        w_ready = sem("w_ready")
        h_ready = sem("h_ready")
        hb_ready = sem("hb_ready")
        hist_ready = sem("hist_ready")
        gates_mm = sem("gates_mm")
        gates_act = sem("gates_act")
        c_new = sem("c_new")
        th_act = sem("th_act")
        p_ready = sem("p_ready")
        ff_mm = sem("ff_mm")
        gel_ready = sem("gel_ready")
        y_mm = sem("y_mm")
        y_ready = sem("y_ready")
        stored = [sem("stored_even"), sem("stored_odd")]

        block = ctx.enter_context(nc.Block())

        qk_f = q_tm[:].rearrange("p a t h d -> p (a t h) d")

        def doubled(a):
            return a.unsqueeze(2).to_broadcast([P, TILES * H, 2, HD])

        x_tiles = x.rearrange("b (h p) d -> p (b h) d", p=P)
        x_steps = x.rearrange("b (c t) d -> b t c d", t=STEPS)
        out_steps = out.rearrange("b (c t) d -> c t b d", t=STEPS)

        def row(a):
            return a.rearrange("(a n) -> a n", a=1)

        def spread(a, n=P):
            return row(a).partition_broadcast(n).rearrange("p a n -> p (a n)")

        def column(a, c):
            return a.rearrange("(c p) -> p c", c=c)

        def flat(a):
            return a.rearrange("p t n -> p (t n)")

        UNITS = [(0, g, b, 0) for g in range(NG) for b in range(B)]
        UNITS += [(1, g, b, i) for g in range(NG) for b in range(B) for i in range(2)]
        GROUPS = [(half, g, b) for half in range(HALVES) for g in range(NG) for b in range(B)]
        FIRST_UNITS = B * NG
        SECOND_UNITS = 2 * B * NG
        ADA_PARTS = ((0, 2 * D), (2 * D, 6 * D))
        INPUTS_AT = {STEPS - 4: (0, 3), STEPS - 3: (3, 6), STEPS - 2: (6, 9)}
        free_steps = [t for t in range(S) if t % STEPS not in INPUTS_AT]
        slot_of = {t: divmod(i, 3) for i, t in enumerate(free_steps)}
        NO_SLOT = (S, 0)
        TAIL_FROM = free_steps[3 * (SECOND_UNITS + 3) + 2]
        FFN_FROM = S // 2
        FFN_EVERY = 16
        PIECES = [(c, 0, P) for c in range(CHUNKS - 1)] + [(CHUNKS - 1, 0, P - VP), (CHUNKS - 1, P - VP, P)]
        LAST = len(PIECES) - 1
        FFN_STEPS = [FFN_FROM + FFN_EVERY * c for c in range(CHUNKS - 1)] + [S - VP // B]
        ffn_of = {t0 + i: (p, i) for p, t0 in enumerate(FFN_STEPS) for i in range(min(FFN_EVERY, S - t0))}
        NO_PIECE = (LAST, S)

        def group_of(m):
            return m if m < FIRST_UNITS else FIRST_UNITS + (m - FIRST_UNITS) // 2

        def last_unit(g):
            return g if g < FIRST_UNITS else FIRST_UNITS + 2 * (g - FIRST_UNITS) + 1

        def blocks(m):
            half, g, b, i = UNITS[m]
            if half == 0:
                return [(GROUP * g + j, j, 0) for j in range(GROUP)]
            return [(GROUP * g + 2 * i + j, 2 * i + j, kc) for j in range(2) for kc in range(2)]

        f1_tm, f1T, f1_sq = (
            [q_sq[:].rearrange("p a t h d -> p (a t h d)")[:, (2 * i + k) * FF:(2 * i + k + 1) * FF] for k in range(2)] for i in range(3))

        @block.sync
        def _(sp):
            sp.dma_start(cond4[:], cond).then_inc(ld_ada, 16)
            sp.dma_start(ada_w[:], w_ada).then_inc(ld_ada, 16)
            sp.dma_start(ada_b[:], spread(b_ada, B)).then_inc(ld_ada, 16)
            sp.dma_start(wqkv[:, 0, :], w_q).then_inc(ld_qkv, 16)
            sp.dma_start(wqkv[:, 1, :], w_k).then_inc(ld_qkv, 16)
            sp.dma_start(wqkv[:, 2, :], w_v).then_inc(ld_qkv, 16)
            sp.dma_start(bqkv[:, 0, :], spread(b_q)).then_inc(ld_qkv, 16)
            sp.dma_start(bqkv[:, 1, :], spread(b_k)).then_inc(ld_qkv, 16)
            sp.dma_start(bqkv[:, 2, :], spread(b_v)).then_inc(ld_qkv, 16)
            for k, (a, z) in enumerate(ADA_PARTS):
                sp.wait_ge(ada_rows, k + 1)
                for bb in range(B):
                    sp.dma_start(ada[:, bb].rearrange("p s d -> p (s d)")[:, a:z],
                                 ada4[bb:bb + 1, a:z].unsqueeze(1).to_broadcast([1, P, z - a])).then_inc(ada_ready[k], 16)
            sp.dma_start(wo_c[:], w_o).then_inc(ld_cff, 16)
            sp.dma_start(bo_c[:], spread(b_o)).then_inc(ld_cff, 16)
            sp.dma_start(wf1[:], w_f1).then_inc(ld_cff, 16)
            sp.dma_start(bf1_all[:], spread(b_f1)).then_inc(ld_cff, 16)
            sp.dma_start(wf2[:], w_f2.rearrange("(c p) d -> p c d", p=P)).then_inc(ld_cff, 16)
            sp.dma_start(bf2[:], spread(b_f2)).then_inc(ld_cff, 16)
            sp.dma_start(wd[:, 0, :], W_dq).then_inc(ld_mla, 16)
            sp.dma_start(wd[:, 1, :], W_dkv).then_inc(ld_mla, 16)
            sp.dma_start(wu[0:32, 0, :], W_uq).then_inc(ld_mla, 16)
            sp.dma_start(wu[32:64, 0, :], W_uk).then_inc(ld_mla, 16)
            sp.dma_start(wu[32:64, 1, :], W_uv).then_inc(ld_mla, 16)
            sp.dma_start(wo_m[:], W_o).then_inc(ld_mla, 16)
            for w_s, w_d in ((wx, Wx), (wh, Wh)):
                src = w_d.rearrange("k (g n) -> k g n", g=4)
                sp.dma_start(w_s[:, 0, :], src[:, 2, :]).then_inc(ld_rnn, 16)
                sp.dma_start(w_s[:, 1:3, :], src[:, 0:2, :]).then_inc(ld_rnn, 16)
                sp.dma_start(w_s[:, 3, :], src[:, 3, :]).then_inc(ld_rnn, 16)
            bsrc = row(b_g).rearrange("a (g n) -> a g n", g=4)
            sp.dma_start(bg[:, 0, :], bsrc[:, 2, :]).then_inc(ld_rnn, 16)
            sp.dma_start(bg[:, 1:3, :], bsrc[:, 0:2, :]).then_inc(ld_rnn, 16)
            sp.dma_start(bg[:, 3, :], bsrc[:, 3, :]).then_inc(ld_rnn, 16)
            sp.dma_start(w1s[:], w1).then_inc(ld_rnn, 16)
            sp.dma_start(b1s[:], column(b1, FC), allow_slow_non_contiguous=True).then_inc(ld_rnn, 16)
            sp.dma_start(w2s[:], w2.rearrange("(c p) d -> p c d", p=P)).then_inc(ld_rnn, 16)
            sp.dma_start(b2s[:], row(b2)).then_inc(ld_rnn, 16)
            for bb in range(B):
                sp.dma_start(x_tb[bb:P:B, :, :], x_steps[bb]).then_inc(ld_xtb, 16)

            sp.wait_ge(zeros, 2)
            for g in range(NG):
                sp.wait_ge(qT_ready, g + 1)
                for j in range(GROUP):
                    rows = slice(SLOTS * HD * j, SLOTS * HD * (j + 1))
                    sp.dma_start(q_slab[rows, GROUP * g + j, :], qS[rows, g, :]).then_inc(slab_group[g], 16)

            sp.wait_ge(bias_part, 2 * BF16_PARTS - 1)
            sp.dma_start(bg_rows[:], bg_parts).then_inc(bias_ready, 16)
            sp.wait_ge(zeros, 3)
            sp.wait_ge(mq_ready, 2)
            for h in range(H):
                sp.dma_start(qz[h * HD:(h + 1) * HD, h, :], flat(qT[h * HD:(h + 1) * HD])).then_inc(qz_group[h // GROUP], 16)
            for p, (c, a, z) in enumerate(PIECES):
                sp.wait_ge(y_ready, p + 1)
                sp.dma_start(out_steps[c, a // B:z // B], o_sb[a:z, c % 2, :]).then_inc(stored[c % 2], 16)
            for k in range(2):
                sp.wait_ge(stored[k], 16 * sum(c % 2 == k for c, _, _ in PIECES))

        @block.gpsimd
        def _(pool):
            nc.gpsimd.memset(ident[:], 0.0).then_inc(consts, 1)
            nc.gpsimd.memset(mask[:], 0.0).then_inc(consts, 1)
            nc.gpsimd.memset(gate_cols[:], 0.0).then_inc(consts, 1)
            nc.gpsimd.memset(ones[:], 1.0).then_inc(consts, 1)
            pool.wait_ge(consts, 4)
            nc.gpsimd.affine_select(out=ident[:], in_=ident[:], compare_op=ALU.not_equal, fill=1.0, base=0,
                                    pattern=[[-1, P]], channel_multiplier=1).then_inc(consts, 1)
            nc.gpsimd.affine_select(out=mask[:], in_=mask[:], compare_op=ALU.is_ge, fill=MASKED, base=0,
                                    pattern=[[0, GROUP], [-1, P]], channel_multiplier=1).then_inc(consts, 1)
            pool.wait_ge(consts, 5)
            nc.gpsimd.tensor_copy(identb[:], ident[:]).then_inc(consts, 1)
            nc.gpsimd.tensor_copy(identh[:], ident[:]).then_inc(consts, 1)
            nc.gpsimd.memset(vaug[:], 0.0).then_inc(vaug_zero, 1)
            pool.wait_ge(vaug_zero, 1)
            nc.gpsimd.memset(vaug[:, :, :, HD:HD + 1], HEADS_UP).then_inc(zeros, 1)
            nc.gpsimd.memset(q_slab, 0.0).then_inc(zeros, 1)
            for i in range(BF16_PARTS):
                nc.gpsimd.affine_select(out=gate_cols[:], in_=gate_cols[:], compare_op=ALU.not_equal, fill=1.0, base=-4 * i,
                                        pattern=[[0, STEPS], [-1, 4], [0, B]], channel_multiplier=1).then_inc(consts, 1)
                pool.wait_ge(consts, 9 + i)
            pool.wait_ge(score_mm, 2 * B * NG)
            nc.gpsimd.memset(qz[:], 0.0).then_inc(zeros, 1)
            pool.wait_ge(pv_mm, B * NG)
            nc.gpsimd.memset(vaug[:, :, :, HD:HD + 1], 1.0).then_inc(zeros, 1)
            pool.wait_ge(w_ready, 4)
            bias = bg[:].rearrange("a g n -> a (g n)")
            for i in range(BF16_PARTS):
                part = bg_parts[:, 4 * i:4 * i + 4, :].rearrange("a g n -> a (g n)")
                nc.gpsimd.tensor_copy(part, bias).then_inc(bias_part, 1)
                pool.wait_ge(bias_part, 2 * i + 1)
                if i < BF16_PARTS - 1:
                    nc.gpsimd.tensor_tensor(bias, bias, part, ALU.subtract).then_inc(bias_part, 1)
                    pool.wait_ge(bias_part, 2 * i + 2)
            pool.wait_ge(w_ready, 7)
            nc.gpsimd.tensor_tensor(whb[:], wh[:], wha[:], ALU.subtract).then_inc(w_ready, 1)

        @block.scalar
        def _(act):
            act.dma_start(x_tm[:], x_tiles).then_inc(ld_x, 16)

            taken = [0, 0, 0]

            def col(k):
                return small[:, k, :]

            def root(a, y):
                taken[0] += 1
                act.wait_ge(roots_in, taken[0])
                nc.scalar.activation(y, a, ACT.Ln).then_inc(act_ch, 1)
                taken[1] += 1
                act.wait_ge(act_ch, taken[1])
                nc.scalar.activation(y, y, ACT.Exp, scale=-0.5).then_inc(roots_out, 1)

            def squared(src):
                for k in range(2):
                    taken[2] += 1
                    act.wait_ge(sq_in, taken[2])
                    ts = slice(TILES // 2 * k, TILES // 2 * (k + 1))
                    nc.scalar.activation(flat(tb[:, ts]), flat(src[:, ts]), ACT.Square).then_inc(sq_out, 1)

            def front_roots(k):
                root(col(ARG), col(ROOT))
                act.wait_ge(ratio_ready, k)
                nc.scalar.activation(col(LN_PLUS), col(ARG), ACT.Ln, bias=1.0)
                nc.scalar.activation(col(LN_MINUS), col(ARG), ACT.Ln, bias=1.0, scale=-1.0).then_inc(ln_ready, 1)
                root(col(ARG), col(ROOT))

            def join_roots(k):
                squared(ta)
                root(col(GUARDED), col(NORM_SQ))
                squared(ta)
                root(col(GUARDED), col(Y_FACTOR))
                nc.scalar.preload_act_table_set(TANH_EXP)
                act.wait_ge(tanh_in, k)
                nc.scalar.activation(col(TANH_N), col(U_NORM), ACT.Tanh).then_inc(tanh_out, 1)

            nc.scalar.preload_act_table_set(LN_EXP)
            front_roots(1)
            squared(v_tm)
            for k in range(2):
                act.wait_ge(v_turned, k + 1)
                nc.scalar.activation(vT[:, 4 * k:4 * k + 4, :].rearrange("p t n -> p (t n)"), bank[:, k, :], ACT.Copy).then_inc(vT_ready, 1)
            root(col(GUARDED), col(V_FACTOR))
            for t in range(TILES):
                act.wait_ge(qkv_ready, t + 1)
                nc.scalar.activation(q_sq[:, :, t].rearrange("p a h d -> p a (h d)"),
                                     q_tm[:, :, t].rearrange("p a h d -> p a (h d)"), ACT.Square).then_inc(squares, 1)
            root(hn_x, hn[:].rearrange("p a t h -> p (a t h)"))
            root(nq[:, 1, :], nq[:, 0, :])
            act.wait_ge(qk_scaled, 1)
            nc.scalar.activation(q_pair[:, :, 0:2, :], doubled(qk_f[:, 0:TILES * H, :]), ACT.Copy).then_inc(q_high, 1)
            act.wait_ge(qk_scaled, 2)
            nc.scalar.activation(k_pair[:, :, 0:SLOTS:2, :], doubled(qk_f[:, TILES * H:2 * TILES * H, :]), ACT.Copy).then_inc(k_high, 1)
            for g in range(NG):
                act.wait_ge(q_turned, g + 1)
                nc.scalar.activation(qS[:, g, :], bank[:, NG + g, :].bitcast(F16), ACT.Copy).then_inc(qT_ready, 1)
            for w in range(2 * B * NG):
                act.wait_ge(score_mm, w + 1)
                if w >= 6:
                    act.wait_ge(pv_mm, w // 2 - 2)
                pair = w % 2
                nc.scalar.activation(p_cond[w % 6], bank[:, 2 * pair:2 * pair + 2, :].rearrange("p k n -> p (k n)"),
                                     ACT.Exp, scale=SCALE / QK_SCALE ** 2).then_inc(exp_done, 1)
            for k in range(2):
                act.wait_ge(oT_mm, k + 1)
                nc.scalar.activation(vT[:, 4 * k:4 * k + 4, :].rearrange("p t n -> p (t n)"), bank[:, 4 * (1 - k), :], ACT.Copy).then_inc(oT_ready, 1)
            join_roots(1)
            act.wait_ge(wd_turned, 1)
            nc.scalar.activation(wdT[:], bank[0:64, 4, 0:P], ACT.Copy).then_inc(wdT_ready, 1)
            act.wait_ge(w_mla_mm, 1)
            nc.scalar.activation(w_mla[:, 0, :], bank[:, 5, 0:D], ACT.Copy).then_inc(w_mla_ready, 1)
            nc.scalar.activation(w_mla[:, 1:3, :].rearrange("p a n -> p (a n)"), bank[:, 6, D:3 * D], ACT.Copy).then_inc(w_mla_ready, 1)
            act.wait_ge(ld_rnn, 16 * 13)
            for w in (wx, bg):
                for g0, g1, f in ((0, 3, .5), (3, 4, 1.)):
                    nc.scalar.mul(w[:, g0:g1, :], w[:, g0:g1, :], A_SCALE * f).then_inc(w_ready, 1)
            for g0, g1, f in ((0, 3, .5), (3, 4, 1.)):
                nc.scalar.mul(wh[:, g0:g1, :], wh[:, g0:g1, :], W_SCALE * f).then_inc(w_ready, 1)
            act.wait_ge(w_ready, 6)
            nc.scalar.activation(wha[:].rearrange("p g n -> p (g n)"), wh[:].rearrange("p g n -> p (g n)"), ACT.Copy).then_inc(w_ready, 1)
            nc.scalar.mul(h0[:], condT[:], H_SCALE).then_inc(w_ready, 1)
            nc.scalar.preload_act_table_set(LN_EXP)
            front_roots(2)
            squared(v_tm)
            root(col(GUARDED), col(V_FACTOR))
            for k in range(2):
                act.wait_ge(v_turned, 3 + k)
                nc.scalar.activation(vT[:, 4 * k:4 * k + 4, :].rearrange("p t n -> p (t n)"), bank[:, k, :], ACT.Copy).then_inc(vT_ready, 1)
            for t in range(TILES):
                act.wait_ge(f1_biased, t + 1)
                nc.scalar.activation(f1_sq[t % 2], f1_tm[t % 2], ACT.Square, accum_out=small[:, F1_FACTOR, t:t + 1]).then_inc(f1_norm, 1)
            root(col(GUARDED), col(F1_FACTOR))
            join_roots(2)
            act.wait_ge(wo_turned, 1)
            nc.scalar.activation(woT, bank[:, 4, 0:P], ACT.Copy).then_inc(woT_ready, 1)
            act.wait_ge(wox_mm, 1)
            nc.scalar.activation(wox[:].rearrange("p g n -> p (g n)"), bank[:, 5, :], ACT.Copy).then_inc(wox_ready, 1)
            for k in range(2):
                act.wait_ge(co_turned, k + 1)
                nc.scalar.activation(vT[:, 4 * k:4 * k + 4, :].rearrange("p t n -> p (t n)"), bank[:, k, :], ACT.Copy).then_inc(co_ready, 1)
            for k in range(2):
                act.wait_ge(mq_mm, k + 1)
                nc.scalar.mul(flat(qT[:, 4 * k:4 * k + 4, :]), bank[:, 2 + k, :], SCALE).then_inc(mq_ready, 1)

            for k in range(2):
                act.wait_ge(x_turned, k + 1)
                nc.scalar.activation(xT[:, 512 * k:512 * k + 512], bank[:, k, :], ACT.Copy).then_inc(xT_ready, 1)

            def m_exp(m):
                act.wait_ge(mx_ready, m + 1)
                if m >= 2:
                    act.wait_ge(mt_mm, m - 1)
                n = P * (UNITS[m][0] + 1)
                for j in range(512 // n):
                    ins = nc.scalar.activation(p_mla[:, m % 2, j * n:(j + 1) * n], bank[:, m % 2, j * n:(j + 1) * n],
                                               ACT.Exp, bias=mx[:, m % 2, j:j + 1])
                ins.then_inc(mp_ready, 1)

            for m in range(FIRST_UNITS):
                m_exp(m)

            def gelu(p):
                c, a, z = PIECES[p]
                act.wait_ge(ff_mm, p + 1)
                if 2 <= p < LAST:
                    act.wait_ge(y_mm, p - 1)
                for f in range(FC):
                    nc.scalar.activation(gel[:, c % 2, f, a:z], bank[:, c % 2, f * P + a:f * P + z], ACT.Gelu,
                                         scale=1.0 / H_SCALE, bias=b1s[:, f:f + 1]).then_inc(gel_ready, 1)

            def act_jobs(t):
                m, w = slot_of.get(t, NO_SLOT)
                if w == 0 and 1 <= m <= SECOND_UNITS:
                    yield lambda: m_exp(FIRST_UNITS + m - 1)
                p, i = ffn_of.get(t, NO_PIECE)
                if i == 2:
                    yield lambda: gelu(p)

            for t in range(S):
                k = t % 2
                src = bank[:, 6 + (t // STEPS) % 2, (t % STEPS) * GW:(t % STEPS + 1) * GW]
                if t == 0:
                    act.wait_ge(c_new, 1)
                act.wait_ge(gates_mm, t + 1)
                nc.scalar.activation(gates[:, k, 0:GW], src, ACT.Tanh, scale=1.0 / A_SCALE).then_inc(gates_act, 1)
                act.wait_ge(c_new, t + 2)
                nc.scalar.activation(th[:, k, :], gates[:, 1 - k, 4 * B:5 * B], ACT.Tanh, scale=0.5).then_inc(th_act, 1)
                for job in act_jobs(t):
                    job()
            gelu(LAST)

        @block.vector
        def _(vec):
            counts = {}

            def go(ins, signal=None):
                s = dve if signal is None else signal
                ins.then_inc(s, 1)
                counts[id(s)] = counts.get(id(s), 0) + 1
                return s

            def done(s=dve):
                vec.wait_ge(s, counts[id(s)])

            def step(ins, signal=None):
                done(go(ins, signal))

            V = nc.vector

            def wide(a):
                return a.unsqueeze(2).to_broadcast([P, TILES, D])

            def statistics(src):
                for t in range(TILES):
                    go(V.bn_stats(st6[:, t, :], src[:, t, :]))
                done()
                for t in range(TILES):
                    go(V.bn_aggr(mv[:, t, :], st6[:, t, :]))
                done()

            vec.wait_ge(ld_x, 16)
            statistics(x_tm)
            vec.wait_ge(ld_ada, 48)
            step(V.tensor_scalar(ada_b[:, D:2 * D], ada_b[:, D:2 * D], 1.0, None, ALU.add))
            step(V.tensor_scalar(ada_b[:, 4 * D:5 * D], ada_b[:, 4 * D:5 * D], 1.0, None, ALU.add))
            vec.wait_ge(cond_t, 1)
            step(V.tensor_copy(condT[:], bank[:, 0, 0:B]), cond_ready)
            for k, (a, z) in enumerate(ADA_PARTS):
                vec.wait_ge(ada_mm, k + 1)
                V.tensor_tensor(ada4[:, a:z], bank[0:B, 1 + k, 0:z - a], ada_b[:, a:z], ALU.add).then_inc(ada_rows, 1)

            def col(k):
                return small[:, k, :]

            def rsqrt(a, y, t, asked_since=0):
                vec.wait_ge(roots_out, counts[id(roots_in)] - asked_since)
                step(V.tensor_tensor(t, y, y, ALU.mult))
                step(V.scalar_tensor_tensor(t, t, -0.5, a, ALU.mult, ALU.mult))
                step(V.scalar_tensor_tensor(y, t, 1.5, y, ALU.add, ALU.mult))

            def half(a, k):
                n = a.shape[1] // 2
                return a[:, n * k:n * (k + 1)]

            def norms(dst):
                for k in range(2):
                    vec.wait_ge(sq_out, counts[id(sq_in)] - 1 + k)
                    go(V.tensor_reduce(half(dst, k), half(tb, k), AX.X, ALU.add))
                done()

            def front(src, part):
                first = part == 0
                mean, var = mv[:, :, 0], mv[:, :, 1]

                def scaled(tiles):
                    for t in tiles:
                        go(V.scalar_tensor_tensor(ta[:, t, :], src[:, t, :], mv[:, t, 0:1], ada[:, t // HALVES, part + 1, :], ALU.subtract, ALU.mult))

                step(V.scalar_tensor_tensor(col(ARG), mean, float(D), mean, ALU.mult, ALU.mult))
                step(V.scalar_tensor_tensor(col(X_SQ), var, float(D), col(ARG), ALU.mult, ALU.add))
                step(V.tensor_scalar(col(ARG), col(X_SQ), TINY, None, ALU.max), roots_in)
                if not first:
                    scaled(range(0, 4))
                rsqrt(col(ARG), col(ROOT), col(NEWTON))
                step(V.tensor_tensor(col(ARG), col(ARG), col(ROOT), ALU.mult))
                step(V.tensor_scalar(col(ARG), col(ARG), MAX_TANH_ARG, None, ALU.min), ratio_ready)
                step(V.tensor_tensor(col(N_SQ), col(ARG), col(ARG), ALU.mult))
                go(V.tensor_scalar(col(IS_SMALL), col(ARG), SERIES_TO, None, ALU.is_lt))
                step(V.tensor_scalar(col(ALPHA), col(N_SQ), 1.0 / 13, None, ALU.mult))
                for k in (11, 9, 7, 5, 3):
                    step(V.scalar_tensor_tensor(col(ALPHA), col(ALPHA), 1.0 / k, col(N_SQ), ALU.add, ALU.mult))
                vec.wait_ge(ln_ready, counts[id(ratio_ready)])
                step(V.tensor_tensor(col(LN_PLUS), col(LN_PLUS), col(LN_MINUS), ALU.subtract))
                step(V.scalar_tensor_tensor(col(LN_PLUS), col(LN_PLUS), 0.5, col(ROOT), ALU.mult, ALU.mult))
                step(V.scalar_tensor_tensor(col(ALPHA), col(ALPHA), 1.0, col(LN_PLUS), ALU.add, ALU.subtract))
                step(V.tensor_tensor(col(ALPHA), col(ALPHA), col(IS_SMALL), ALU.mult))
                step(V.tensor_tensor(col(ALPHA), col(ALPHA), col(LN_PLUS), ALU.add))
                step(V.tensor_tensor(col(ARG), col(ALPHA), col(ALPHA), ALU.mult))
                step(V.tensor_tensor(col(ARG), col(ARG), var, ALU.mult))
                step(V.tensor_scalar(col(ARG), col(ARG), LN_EPS, None, ALU.add), roots_in)
                if first:
                    vec.wait_ge(ada_ready[0], 16 * B)
                scaled(range(0 if first else 4, TILES))
                rsqrt(col(ARG), col(ROOT), col(NEWTON))
                step(V.tensor_tensor(col(ARG), col(ROOT), col(ALPHA), ALU.mult))
                for t in range(TILES):
                    go(V.scalar_tensor_tensor(v_tm[:, t, :], ta[:, t, :], small[:, ARG, t:t + 1], ada[:, t // HALVES, part, :], ALU.mult, ALU.add),
                       sq_in if t % 4 == 3 else None)
                norms(col(V_FACTOR))
                step(V.tensor_scalar(col(GUARDED), col(V_FACTOR), TINY, None, ALU.max), roots_in)
                rsqrt(col(GUARDED), col(V_FACTOR), col(NEWTON))
                step(V.tensor_scalar(col(V_FACTOR), col(V_FACTOR), CLIP, 1.0, ALU.mult, ALU.min))

            def join(src, part, dst, signal):
                norms(col(NORM_SQ))
                step(V.tensor_scalar(col(GUARDED), col(NORM_SQ), TINY, None, ALU.max), roots_in)
                rsqrt(col(GUARDED), col(NORM_SQ), col(NEWTON))
                step(V.tensor_scalar(col(NORM_SQ), col(NORM_SQ), CLIP, 1.0, ALU.mult, ALU.min))
                for t in range(TILES):
                    go(V.scalar_tensor_tensor(ta[:, t, :], ta[:, t, :], small[:, NORM_SQ, t:t + 1], ada[:, t // HALVES, part, :], ALU.mult, ALU.mult),
                       sq_in if t % 4 == 3 else None)
                vec.wait_ge(sq_in, counts[id(sq_in)])
                go(V.tensor_tensor(v_tm[:], ta[:], src[:], ALU.mult))
                norms(col(NORM_SQ))
                step(V.tensor_scalar(col(GUARDED), col(NORM_SQ), TINY, None, ALU.max), roots_in)
                go(V.tensor_reduce(col(XY), v_tm[:], AX.X, ALU.add))
                go(V.tensor_scalar(col(U_WEIGHT), col(X_SQ), 1.0, None, ALU.subtract))
                rsqrt(col(GUARDED), col(Y_FACTOR), col(NEWTON))
                step(V.tensor_tensor(col(U_NORM), col(GUARDED), col(Y_FACTOR), ALU.mult), tanh_in)
                vec.wait_ge(tanh_out, counts[id(tanh_in)])
                go(V.tensor_tensor(col(Y_SQ), col(TANH_N), col(TANH_N), ALU.mult))
                step(V.tensor_tensor(col(Y_FACTOR), col(Y_FACTOR), col(TANH_N), ALU.mult))
                go(V.tensor_tensor(col(DENOM), col(Y_SQ), col(X_SQ), ALU.mult))
                go(V.tensor_tensor(col(U_WEIGHT), col(U_WEIGHT), col(Y_FACTOR), ALU.mult))
                step(V.scalar_tensor_tensor(col(XY), col(XY), 2.0, col(Y_FACTOR), ALU.mult, ALU.mult))
                go(V.scalar_tensor_tensor(col(X_WEIGHT), col(XY), 1.0, col(Y_SQ), ALU.add, ALU.add))
                step(V.scalar_tensor_tensor(col(DENOM), col(XY), 1.0, col(DENOM), ALU.add, ALU.add))
                step(V.tensor_scalar(col(DENOM), col(DENOM), EPS, None, ALU.max))
                step(V.reciprocal(col(DENOM), col(DENOM)))
                go(V.tensor_tensor(col(X_WEIGHT), col(X_WEIGHT), col(DENOM), ALU.mult))
                step(V.scalar_tensor_tensor(col(U_WEIGHT), col(U_WEIGHT), -1.0, col(DENOM), ALU.mult, ALU.mult))
                for k in range(2):
                    ts = range(TILES // 2 * k, TILES // 2 * (k + 1))
                    for t in ts:
                        go(V.tensor_scalar(tb[:, t, :], src[:, t, :], small[:, X_WEIGHT, t:t + 1], None, ALU.mult))
                    done()
                    for t in ts:
                        go(V.scalar_tensor_tensor(dst[:, t, :], ta[:, t, :], small[:, U_WEIGHT, t:t + 1], tb[:, t, :], ALU.mult, ALU.add),
                           signal if t == ts[-1] else None)
                done(signal)

            front(x_tm, 0)
            vec.wait_ge(ld_qkv, 96)

            def head_sums(t):
                vec.wait_ge(squares, t + 1)
                go(V.tensor_reduce(hn[:, :, t, :], q_sq[:, :, t], AX.X, ALU.add))

            for t in range(TILES):
                vec.wait_ge(qkv_mm, t + 1)
                V.scalar_tensor_tensor(q_tm[:, :, t].rearrange("p a h d -> p a (h d)"),
                                       bank[:, 2 + t % 4, 0:3 * D].rearrange("p (a n) -> p a n", a=3), small[:, V_FACTOR, t:t + 1],
                                       bqkv[:], ALU.mult, ALU.add).then_inc(qkv_ready, 1)
                if t:
                    head_sums(t - 1)
            head_sums(TILES - 1)
            done()
            hn_f = hn[:].rearrange("p a t h -> p (a t) h")
            hn_g = hn[:].rearrange("p a t h -> p (a t h)")
            q_f = q_tm[:].rearrange("p a t h d -> p (a t h) d")
            step(V.tensor_reduce(nq[:, 0, :], hn_f, AX.X, ALU.add))
            go(V.tensor_scalar(hn_x, hn_g, TINY, None, ALU.max), roots_in)
            go(V.tensor_scalar(nq[:, 1, :], nq[:, 0, :], TINY, None, ALU.max), roots_in)
            rsqrt(hn_x, hn_g, hn_t, 1)
            rsqrt(nq[:, 1, :], nq[:, 0, :], nq[:, 2, :])
            step(V.tensor_scalar(nq[:, 0, :], nq[:, 0, :], CLIP * HEADS_UP, HEADS_UP, ALU.mult, ALU.min))
            step(V.scalar_tensor_tensor(hn_f, hn_f, CLIP, nq[:, 0, :].unsqueeze(2).to_broadcast([P, 3 * TILES, H]), ALU.mult, ALU.min))
            n = TILES * H
            for a in (0, 1):
                V.scalar_tensor_tensor(q_f[:, a * n:a * n + n, :], q_f[:, a * n:a * n + n, :], QK_SCALE,
                                       hn_g[:, a * n:a * n + n].unsqueeze(2).to_broadcast([P, n, HD]), ALU.mult, ALU.mult).then_inc(qk_scaled, 1)
            vec.wait_ge(zeros, 1)
            V.tensor_tensor(vaug[:].rearrange("p t h v -> p (t h) v")[:, :, 0:HD], q_f[:, 2 * n:3 * n, :],
                            hn_g[:, 2 * n:3 * n].unsqueeze(2).to_broadcast([P, TILES * H, HD]), ALU.mult).then_inc(vaug_ready, 1)
            vec.wait_ge(qk_scaled, 2)
            vec.wait_ge(q_high, 1)
            V.tensor_tensor(q_pair[:, :, 2:SLOTS, :], doubled(q_f[:, 0:n, :]), q_pair[:, :, 0:2, :], ALU.subtract).then_inc(q_low, 1)
            vec.wait_ge(k_high, 1)
            V.tensor_tensor(k_pair[:, :, 1:SLOTS:2, :], doubled(q_f[:, n:2 * n, :]), k_pair[:, :, 0:SLOTS:2, :], ALU.subtract).then_inc(k_low, 1)
            for g in range(NG):
                vec.wait_ge(k_turned, g + 1)
                V.tensor_copy(kS[:, g, :], bank[:, g, :].bitcast(F16)).then_inc(kT_ready, 1)

            def o_copy(u):
                vec.wait_ge(pv_mm, u + 1)
                if u >= 2:
                    vec.wait_ge(o_turned, u - 1)
                V.tensor_copy(oTs[:, u % 2, :], bank[:, 4 + u % 2, 0:S]).then_inc(o_copied, 1)

            def o_norm(u):
                vec.wait_ge(o_turned, u + 1)
                g, bb = divmod(u, B)
                tr = bank[:, 6 + u % 2, 0:S].rearrange("p (h j v) -> p h j v", h=HALVES, j=GROUP)
                step(V.reciprocal(rd[:, u % 2], tr[:, :, :, HD]))
                o4 = o_tm[:].rearrange("p t (g j d) -> p t g j d", g=NG, d=HD)
                V.tensor_tensor(o4[:, HALVES * bb:HALVES * bb + HALVES, g], tr[:, :, :, 0:HD],
                                rd[:, u % 2].unsqueeze(3).to_broadcast([P, HALVES, GROUP, HD]), ALU.mult).then_inc(o_normed, 1)

            for u in range(B * NG):
                o_copy(u)
                if u:
                    o_norm(u - 1)
            o_norm(B * NG - 1)
            vec.wait_ge(ld_cff, 16 * 6)
            for k in range(2):
                vec.wait_ge(attn_mm, k + 1)
                go(V.tensor_tensor(half(ta, k), bank[:, 2 + k, :].rearrange("p (t n) -> p t n", n=D),
                                   bo_c[:].unsqueeze(1).to_broadcast([P, TILES // 2, D]), ALU.add), sq_in)
            vec.wait_ge(ada_ready[1], 16 * B)
            join(x_tm, 2, x1_tm, dve)
            statistics(x1_tm)
            front(x1_tm, 3)
            for k in range(2):
                go(V.tensor_tensor(half(v_tm, k), half(v_tm, k), half(wide(col(V_FACTOR)), k), ALU.mult), v_ready)

            def f1_copy(t):
                vec.wait_ge(f1_turned, t + 1)
                if t >= 2:
                    vec.wait_ge(f2_tile, t - 1)
                V.tensor_copy(f1T[t % 2], bank[:, 4 + t % 2, :]).then_inc(f1T_ready, 1)

            for t in range(TILES):
                vec.wait_ge(f1_mm, t + 1)
                if t >= 2:
                    vec.wait_ge(f1_norm, t - 1)
                    vec.wait_ge(f1_turned, t - 1)
                V.tensor_tensor(f1_tm[t % 2], bank[:, 2 + t % 2, :], bf1_all[:], ALU.add).then_inc(f1_biased, 1)
                if t:
                    f1_copy(t - 1)
            f1_copy(TILES - 1)
            vec.wait_ge(f1_norm, TILES)
            step(V.tensor_scalar(col(GUARDED), col(F1_FACTOR), TINY, None, ALU.max), roots_in)
            rsqrt(col(GUARDED), col(F1_FACTOR), col(NEWTON))
            step(V.tensor_scalar(col(F1_FACTOR), col(F1_FACTOR), CLIP, 1.0, ALU.mult, ALU.min))
            vec.wait_ge(f2_tile, TILES)
            for t in range(TILES):
                go(V.scalar_tensor_tensor(ta[:, t, :], bank[:, 6 + t // 4, (t % 4) * P:(t % 4 + 1) * P], small[:, F1_FACTOR, t:t + 1], bf2[:], ALU.mult, ALU.add),
                   sq_in if t % 4 == 3 else None)
            join(x1_tm, 5, v_tm, cond_out)

            for k in range(2):
                vec.wait_ge(mk_mm, k + 1)
                V.tensor_copy(flat(kT[:, 4 * k:4 * k + 4, :]), bank[:, 4 + k, :]).then_inc(mk_ready, 1)
            for k in range(2):
                vec.wait_ge(mv_mm, k + 1)
                V.tensor_copy(vaug[:, 4 * k:4 * k + 4, :, 0:HD], bank[:, 6 + k, :].rearrange("p (t h d) -> p t h d", t=4, h=H)).then_inc(mv_ready, 1)

            def m_max(m):
                half = UNITS[m][0]
                n = P * (half + 1)
                vec.wait_ge(ms_mm, m + 1)
                if m >= 2:
                    vec.wait_ge(mp_ready, m - 1)
                V.tensor_reduce(mx[:, m % 2, 0:512 // n], bank[:, m % 2, :].rearrange("p (j n) -> p j n", n=n), AX.X, ALU.max,
                                negate=True).then_inc(mx_ready, 1)

            def m_weights(m):
                vec.wait_ge(mt_mm, m + 1)
                if m >= 2:
                    vec.wait_ge(mpv_mm, m - 1)
                V.tensor_copy(pt_mla[:, m % 2, :], bank[:, 2 + m % 2, :]).then_inc(mt_ready, 1)

            def m_out(g):
                vec.wait_ge(mpv_mm, last_unit(g) + 1)
                if g >= 2:
                    vec.wait_ge(mo_turned, g - 1)
                V.tensor_copy(oTs[:, g % 2, 0:P], bank[:, 4, 0:P]).then_inc(mo_copied, 1)

            def m_norm(g):
                half, hg, b = GROUPS[g]
                vec.wait_ge(mo_turned, g + 1)
                tr = bank[:, 5, 0:P].rearrange("p (j v) -> p j v", j=GROUP)
                step(V.reciprocal(rdm[:, g % 2], tr[:, :, HD]))
                o4 = o_tm[:].rearrange("p t (g j d) -> p t g j d", g=NG, d=HD)
                V.tensor_tensor(o4[:, HALVES * b + half, hg], tr[:, :, 0:HD],
                                rdm[:, g % 2].unsqueeze(2).to_broadcast([P, GROUP, HD]), ALU.mult).then_inc(mo_normed, 1)

            def m_oT(half):
                vec.wait_ge(moT_mm, half + 1)
                for a, z in ((0, STEPS), (STEPS, P)):
                    V.tensor_copy(oT[:, half * 512 + a * B:half * 512 + z * B].rearrange("p (t b) -> p t b", b=B),
                                  bank[:, 0, :].rearrange("p (b t) -> p t b", b=B)[:, a:z, :]).then_inc(moT_ready, 1)

            m_max(0)
            for m in range(FIRST_UNITS):
                if m + 1 < FIRST_UNITS:
                    m_max(m + 1)
                m_weights(m)
                if m >= 1:
                    m_out(m - 1)
                if m >= 2:
                    m_norm(m - 2)
            m_out(FIRST_UNITS - 1)
            m_norm(FIRST_UNITS - 2)
            m_norm(FIRST_UNITS - 1)
            step(V.memset(gates[:], 0.0), c_new)
            m_oT(0)

            def result(p):
                c, a, z = PIECES[p]
                vec.wait_ge(y_mm, p + 1)
                vec.wait_ge(ld_xtb, 64)
                if 2 <= p < LAST:
                    vec.wait_ge(stored[c % 2], 16 * (c // 2))
                V.tensor_tensor(o_sb[a:z, c % 2, :], bank[a:z, 2 + c % 2, 0:D], x_tb[a:z, c, :], ALU.add).then_inc(y_ready, 1)

            def vec_jobs(t):
                m, w = slot_of.get(t, NO_SLOT)
                if w == 2 and m < SECOND_UNITS:
                    yield lambda: m_max(FIRST_UNITS + m)
                if w == 0 and 2 <= m <= SECOND_UNITS + 1:
                    yield lambda: m_weights(FIRST_UNITS + m - 2)
                if w == 1 and m >= 4 and m % 2 == 0 and m <= SECOND_UNITS + 2:
                    yield lambda: m_out(FIRST_UNITS + (m - 4) // 2)
                if w == 1 and m >= 5 and m % 2 == 1 and m <= SECOND_UNITS + 3:
                    yield lambda: m_norm(FIRST_UNITS + (m - 5) // 2)
                if t == TAIL_FROM + 1:
                    yield lambda: m_oT(1)
                p, i = ffn_of.get(t, NO_PIECE)
                if i == 7:
                    yield lambda: result(p)

            for t in range(S):
                k = t % 2
                vec.wait_ge(gates_act, t + 1)
                V.scalar_tensor_tensor(pr[:, k, :], gates[:, k, B:3 * B], 1.0, gates[:, k, 3 * B:5 * B], ALU.add, ALU.mult).then_inc(p_ready, 1)
                V.tensor_scalar(so[:, k, :], gates[:, k, 0:B], 1.0, 0.5 * H_SCALE, ALU.add, ALU.mult)
                vec.wait_ge(p_ready, t + 1)
                V.scalar_tensor_tensor(gates[:, 1 - k, 4 * B:5 * B], pr[:, k, B:2 * B], 0.5, pr[:, k, 0:B], ALU.mult, ALU.add).then_inc(c_new, 1)
                vec.wait_ge(th_act, t + 1)
                V.tensor_tensor(ha[:, k, :], so[:, k, :], th[:, k, :], ALU.mult).then_inc(h_ready, 1)
                hs = hist[:, t, :]
                V.tensor_tensor(hs, so[:, k, :], th[:, k, :], ALU.mult).then_inc(hist_ready, 1)
                vec.wait_ge(hist_ready, t + 1)
                V.tensor_tensor(hb[:, k, :], hs, ha[:, k, :], ALU.subtract).then_inc(hb_ready, 1)
                for job in vec_jobs(t):
                    job()
            result(LAST)

        @block.tensor
        def _(pe):
            T = nc.tensor
            pe.wait_ge(consts, 5)
            pe.wait_ge(ld_ada, 48)
            T.transpose(bank[:, 0, 0:B], cond4[:], ident[0:B, 0:B]).then_inc(cond_t, 1)
            pe.wait_ge(cond_ready, 1)
            for k, (a, z) in enumerate(ADA_PARTS):
                T.matmul(bank[0:B, 1 + k, 0:z - a], condT[:], ada_w[:, a:z], start=True, stop=True).then_inc(ada_mm, 1)

            def turn8(src, base, signal, ready=None, count=0):
                for k in range(2):
                    if ready is not None:
                        pe.wait_ge(ready, count + k + 1)
                    for t in range(4):
                        ins = T.transpose(bank[:, base + k, t * P:(t + 1) * P], src(4 * k + t), ident[:])
                    ins.then_inc(signal, 1)

            pe.wait_ge(ada_rows, 2)
            turn8(lambda t: v_tm[:, t, :], 0, v_turned, sq_in)
            pe.wait_ge(ld_qkv, 96)
            for t in range(TILES):
                pe.wait_ge(vT_ready, 1 + t // 4)
                if t >= 4:
                    pe.wait_ge(qkv_ready, t - 3)
                T.matmul(bank[:, 2 + t % 4, 0:3 * D], vT[:, t, :], wqkv[:].rearrange("p a n -> p (a n)"), start=True, stop=True).then_inc(qkv_mm, 1)
            pe.wait_ge(consts, 8)
            for pair, low, base, signal in ((q_pair, q_low, NG, q_turned), (k_pair, k_low, 0, k_turned)):
                pe.wait_ge(low, 1)
                stacks = pair.rearrange("p (t g j) s d -> p t g (j s d)", t=TILES, g=NG)
                for g in range(NG):
                    for t in range(TILES):
                        ins = T.transpose(bank[:, base + g, :].bitcast(F16)[:, t * P:(t + 1) * P], stacks[:, t, g], identh[:])
                    ins.then_inc(signal, 1)

            def scores(w):
                u, pair = divmod(w, 2)
                g, bb = divmod(u, B)
                if w >= 2:
                    pe.wait_ge(exp_done, w - 1)
                if w % (2 * B) == 0:
                    pe.wait_ge(slab_group[g], 16 * GROUP)
                if w == 1:
                    pe.wait_ge(kT_ready, NG)
                h = GROUP * g + 2 * pair
                for kc in range(HALVES):
                    ins = T.matmul(bank[:, 2 * (w % 2) + kc, :], kS[:, g, bb * S + kc * P:bb * S + (kc + 1) * P],
                                   q_slab[:, h:h + 2, bb * S:(bb + 1) * S], start=True, stop=True)
                ins.then_inc(score_mm, 1)

            def values(u, kc):
                g, bb = divmod(u, B)
                if kc == 0:
                    pe.wait_ge(exp_done, 2 * u + 2)
                    if u >= 2:
                        pe.wait_ge(o_copied, u - 1)
                for j in range(GROUP):
                    ins = T.matmul(bank[VP * j:VP * j + VP, 4 + u % 2, 0:S], vaug[:, HALVES * bb + kc, GROUP * g + j, :],
                                   p_cond[(2 * u + j // 2) % 6][:, (2 * kc + j % 2) * S:(2 * kc + j % 2 + 1) * S],
                                   start=(kc == 0), stop=(kc == 1), tile_position=(0, VP * j))
                if kc == 1:
                    ins.then_inc(pv_mm, 1)

            def o_turn(u):
                pe.wait_ge(o_copied, u + 1)
                if u >= 2:
                    pe.wait_ge(o_normed, u - 1)
                for half in range(HALVES):
                    ins = T.transpose(bank[:, 6 + u % 2, half * P:(half + 1) * P], oTs[:, u % 2, half * P:(half + 1) * P], ident[:])
                ins.then_inc(o_turned, 1)

            pe.wait_ge(kT_ready, 2)
            pe.wait_ge(vaug_ready, 1)
            N = 2 * B * NG
            for w in range(3):
                scores(w)
            for u in range(B * NG):
                for kc in range(HALVES):
                    if 2 * u + 3 + kc < N:
                        scores(2 * u + 3 + kc)
                    values(u, kc)
                if u:
                    o_turn(u - 1)

            def o_project(k):
                pe.wait_ge(oT_ready, k + 1)
                for t in range(4 * k, 4 * k + 4):
                    ins = T.matmul(bank[:, 2 + k, (t % 4) * P:(t % 4 + 1) * P], vT[:, t, :], wo_c[:], start=True, stop=True)
                ins.then_inc(attn_mm, 1)

            def oT_half(k):
                pe.wait_ge(o_normed, B * NG - (B // 2) * (1 - k))
                for t in range(4):
                    ins = T.transpose(bank[:, 4 * (1 - k), t * P:(t + 1) * P], o_tm[:, 4 * k + t, :], ident[:])
                ins.then_inc(oT_mm, 1)

            pe.wait_ge(o_copied, B * NG - 1)
            oT_half(0)
            o_turn(B * NG - 1)
            pe.wait_ge(ld_cff, 16 * 6)
            oT_half(1)
            o_project(0)
            o_project(1)
            pe.wait_ge(ld_mla, 16 * 6)
            T.transpose(bank[0:64, 4, 0:P], wd[:].rearrange("p a n -> p (a n)"), ident[:]).then_inc(wd_turned, 1)
            pe.wait_ge(wdT_ready, 1)
            for i, (rows, w) in enumerate(((slice(0, 32), wu[0:32, 0, :]), (slice(32, 64), wu[32:64, 0, :]), (slice(32, 64), wu[32:64, 1, :]))):
                ins = T.matmul(bank[:, 5 + min(i, 1), i * D:(i + 1) * D], wdT[rows, :], w, start=True, stop=True)
            ins.then_inc(w_mla_mm, 1)
            turn8(lambda t: v_tm[:, t, :], 0, v_turned, v_ready)
            pe.wait_ge(vT_ready, 4)

            def f1_product(t):
                if t >= 2:
                    pe.wait_ge(f1_biased, t - 1)
                T.matmul(bank[:, 2 + t % 2, :], vT[:, t, :], wf1[:], start=True, stop=True).then_inc(f1_mm, 1)

            def f1_turn(t):
                pe.wait_ge(f1_biased, t + 1)
                if t >= 2:
                    pe.wait_ge(f1T_ready, t - 1)
                for f in range(FC):
                    ins = T.transpose(bank[:, 4 + t % 2, f * P:(f + 1) * P], f1_tm[t % 2][:, f * P:(f + 1) * P], ident[:])
                ins.then_inc(f1_turned, 1)

            def f2_product(t):
                pe.wait_ge(f1T_ready, t + 1)
                for f in range(FC):
                    ins = T.matmul(bank[:, 6 + t // 4, (t % 4) * P:(t % 4 + 1) * P], f1T[t % 2][:, f * P:(f + 1) * P],
                                   wf2[:, f, :], start=(f == 0), stop=(f == FC - 1))
                ins.then_inc(f2_tile, 1)

            f1_product(0)
            for t in range(TILES):
                if t + 1 < TILES:
                    f1_product(t + 1)
                f1_turn(t)
                if t:
                    f2_product(t - 1)
            f2_product(TILES - 1)
            pe.wait_ge(f1_norm, TILES)
            T.transpose(bank[:, 4, 0:P], wo_m[:], ident[:]).then_inc(wo_turned, 1)
            pe.wait_ge(woT_ready, 1)
            T.matmul(bank[:, 5, :], woT, wx[:].rearrange("p g n -> p (g n)"), start=True, stop=True).then_inc(wox_mm, 1)
            turn8(lambda t: v_tm[:, t, :], 0, co_turned, cond_out)
            pe.wait_ge(w_mla_ready, 2)
            for j, signal in ((0, mq_mm), (1, mk_mm)):
                for k in range(2):
                    pe.wait_ge(co_ready, k + 1)
                    T.matmul(bank[:, 2 + 2 * j + k, :], w_mla[:, j, :], flat(vT[:, 4 * k:4 * k + 4, :]), start=True, stop=True).then_inc(signal, 1)
            for k in range(2):
                for t in range(4):
                    ins = T.matmul(bank[:, 6 + k, t * P:(t + 1) * P], vT[:, 4 * k + t, :], w_mla[:, 2, :], start=True, stop=True)
                ins.then_inc(mv_mm, 1)
            kT_flat = flat(kT[:])

            def m_scores(m, part=None):
                half, g, b, i = UNITS[m]
                n = P * (half + 1)
                per = 512 // n
                if m == FIRST_UNITS and part == 0:
                    pe.wait_ge(moT_ready, 2)
                if part in (None, 0) and m >= 2:
                    pe.wait_ge(mp_ready, m - 1)
                js = range(per) if part is None else [part]
                for j in js:
                    h = GROUP * g + 2 * i + j
                    T.matmul(bank[:, m % 2, j * n:(j + 1) * n], qz[:, h, b * S + half * P:b * S + half * P + P],
                             kT_flat[:, b * S:b * S + n], start=(j == 0), stop=True, skip_group_check=True)
                    if half == 1:
                        ins = T.matmul(bank[:, m % 2, (j + 1) * n - P:(j + 1) * n], identb[:], mask[:, 0, :], start=False, stop=True,
                                       skip_group_check=True)
                if half == 0:
                    ins = T.matmul(bank[:, m % 2, :], identb[:], mask[:], start=False, stop=True, skip_group_check=True)
                if js[-1] == per - 1:
                    ins.then_inc(ms_mm, 1)

            def m_turn(m, blocks=range(4)):
                if blocks[0] == 0:
                    pe.wait_ge(mp_ready, m + 1)
                    if m >= 2:
                        pe.wait_ge(mt_ready, m - 1)
                for i in blocks:
                    ins = T.transpose(bank[:, 2 + m % 2, i * P:(i + 1) * P], p_mla[:, m % 2, i * P:(i + 1) * P], ident[:])
                if blocks[-1] == 3:
                    ins.then_inc(mt_mm, 1)

            def m_values(m, parts=range(4)):
                half, _, b, _ = UNITS[m]
                g = group_of(m)
                if parts[0] == 0:
                    pe.wait_ge(mt_ready, m + 1)
                    if g >= 1:
                        pe.wait_ge(mo_copied, g)
                for i in parts:
                    h, j, kc = blocks(m)[i]
                    ins = T.matmul(bank[VP * j:VP * j + VP, 4, 0:P], vaug[:, HALVES * b + kc, h, :], pt_mla[:, m % 2, i * P:(i + 1) * P],
                                   start=(kc == 0), stop=(kc == half), tile_position=(0, VP * j))
                if parts[-1] == 3:
                    ins.then_inc(mpv_mm, 1)

            def m_back(g):
                pe.wait_ge(mo_copied, g + 1)
                if g >= 1:
                    pe.wait_ge(mo_normed, g)
                T.transpose(bank[:, 5, 0:P], oTs[:, g % 2, 0:P], ident[:]).then_inc(mo_turned, 1)

            def m_turn_out(half):
                pe.wait_ge(mo_normed, (half + 1) * FIRST_UNITS)
                for b in range(B):
                    ins = T.transpose(bank[:, 0, b * P:(b + 1) * P], o_tm[:, HALVES * b + half, :], ident[:])
                ins.then_inc(moT_mm, 1)

            def inputs_of(c, parts):
                acc = bank[:, 6 + c % 2, :]
                by_gate = acc.rearrange("p (t g b) -> p t g b", g=4, b=B)
                cols = slice(c * P, (c + 1) * P)
                for i in parts:
                    if i == 0:
                        T.matmul(acc, bg_rows[:], gate_cols[:], start=True, stop=True, skip_group_check=True)
                    elif i <= 4:
                        T.matmul(by_gate[:, :, i - 1, :], wx[:, i - 1, :], xT[:, cols], start=False, stop=True, skip_group_check=True)
                    else:
                        if i == 5 and c in (0, 1, 4):
                            pe.wait_ge(moT_ready, (1, 2, None, None, 4)[c])
                        T.matmul(by_gate[:, :, i - 5, :], wox[:, i - 5, :], oT[:, cols], start=False, stop=True, skip_group_check=True)

            pe.wait_ge(ld_xtb, 64)
            for k in range(2):
                pe.wait_ge(co_ready, k + 1)
                for t in range(4):
                    ins = T.transpose(bank[:, k, t * P:(t + 1) * P], x_tb[:, 4 * k + t, :], ident[:])
                ins.then_inc(x_turned, 1)
            pe.wait_ge(mv_ready, 1)
            pe.wait_ge(bias_ready, 16)
            pe.wait_ge(consts, 11)
            pe.wait_ge(xT_ready, 2)
            inputs_of(0, range(0, 5))

            pe.wait_ge(mk_ready, 2)
            pe.wait_ge(qz_group[0], 16 * GROUP)
            pe.wait_ge(zeros, 4)
            m_scores(0)
            for m in range(FIRST_UNITS):
                if m + 1 < FIRST_UNITS:
                    if (m + 1) % B == 0:
                        pe.wait_ge(qz_group[(m + 1) // B], 16 * GROUP)
                    m_scores(m + 1)
                if m >= 1:
                    m_values(m - 1)
                m_turn(m)
                if m >= 2:
                    m_back(m - 2)
            m_values(FIRST_UNITS - 1)
            m_back(FIRST_UNITS - 2)
            m_back(FIRST_UNITS - 1)
            m_turn_out(0)
            pe.wait_ge(wox_ready, 1)
            inputs_of(0, range(5, 9))
            pe.wait_ge(w_ready, 9)

            def ffn_up(p, fs=range(FC)):
                c, a, z = PIECES[p]
                if fs[0] == 0:
                    pe.wait_ge(hist_ready, STEPS * c + z // B)
                    if p >= 2:
                        pe.wait_ge(gel_ready, FC * (p if p == LAST else p - 1))
                for f in fs:
                    ins = T.matmul(bank[:, c % 2, f * P + a:f * P + z], w1s[:, f * P:(f + 1) * P],
                                   hist[:, c * STEPS + a // B:c * STEPS + z // B, :].rearrange("p t b -> p (t b)"), start=True, stop=True)
                if fs[-1] == FC - 1:
                    ins.then_inc(ff_mm, 1)

            def ffn_down(p, parts):
                c, a, z = PIECES[p]
                y = bank[a:z, 2 + c % 2, 0:D]
                at = dict(tile_position=(0, a)) if z - a <= VP else {}
                for i in parts:
                    if i == 0:
                        if 2 <= p < LAST:
                            pe.wait_ge(y_ready, p - 1)
                        T.matmul(y, ones[:, a:z], b2s[:], start=True, stop=False, **at)
                        T.matmul(y, oT[:, c * P + a:c * P + z], wo_m[:], start=False, stop=False, **at)
                    else:
                        pe.wait_ge(gel_ready, FC * p + i)
                        ins = T.matmul(y, gel[:, c % 2, i - 1, a:z], w2s[:, i - 1, :], start=False, stop=(i == FC), **at)
                if parts[-1] == FC:
                    ins.then_inc(y_mm, 1)

            def pe_jobs(t):
                m, w = slot_of.get(t, NO_SLOT)
                if w == 0 and 3 <= m <= SECOND_UNITS + 2:
                    yield lambda: m_values(FIRST_UNITS + m - 3, range(3, 4))
                if w == 0 and m < SECOND_UNITS:
                    yield lambda: m_scores(FIRST_UNITS + m, 0)
                if w == 0 and m >= 5 and m % 2 == 1 and m <= SECOND_UNITS + 3:
                    yield lambda: m_back(FIRST_UNITS + (m - 5) // 2)
                if w == 1 and m < SECOND_UNITS:
                    yield lambda: m_scores(FIRST_UNITS + m, 1)
                if w == 1 and 1 <= m <= SECOND_UNITS:
                    yield lambda: m_turn(FIRST_UNITS + m - 1, range(0, 1))
                if w == 2 and 1 <= m <= SECOND_UNITS:
                    yield lambda: m_turn(FIRST_UNITS + m - 1, range(1, 4))
                if w == 2 and 2 <= m <= SECOND_UNITS + 1:
                    yield lambda: m_values(FIRST_UNITS + m - 2, range(0, 3))
                if t == TAIL_FROM:
                    yield lambda: m_turn_out(1)
                if t % STEPS in INPUTS_AT and t < S - STEPS:
                    yield lambda: inputs_of(t // STEPS + 1, range(*INPUTS_AT[t % STEPS]))
                p, i = ffn_of.get(t, NO_PIECE)
                if i in (0, 1):
                    yield lambda: ffn_up(p, range(2 * i, 2 * i + 2))
                if i in (2, 3, 4):
                    yield lambda: ffn_down(p, (range(0, 1), range(1, 3), range(3, 5))[i - 2])

            for t in range(S):
                k = (t + 1) % 2
                acc = bank[:, 6 + (t // STEPS) % 2, (t % STEPS) * GW:(t % STEPS + 1) * GW]
                if t:
                    pe.wait_ge(h_ready, t)

                def add(w, h):
                    for g in range(4):
                        ins = T.matmul(acc[:, g * B:(g + 1) * B], w[:, g, :], h, start=False, stop=True, skip_group_check=True)
                    return ins

                if t == 0:
                    add(wh, h0[:]).then_inc(gates_mm, 1)
                else:
                    add(wha, ha[:, k, :])
                    add(whb, ha[:, k, :])
                    pe.wait_ge(hb_ready, t)
                    add(wha, hb[:, k, :]).then_inc(gates_mm, 1)
                for job in pe_jobs(t):
                    job()
            ffn_down(LAST, range(0, 1))
            ffn_up(LAST)
            ffn_down(LAST, range(1, FC + 1))


_INS = ['x', 'cond_1024', 'L0_cond_w_q', 'L0_cond_b_q', 'L0_cond_w_k', 'L0_cond_b_k', 'L0_cond_w_v', 'L0_cond_b_v',
        'L0_cond_w_o', 'L0_cond_b_o', 'L0_cond_w_f1', 'L0_cond_b_f1', 'L0_cond_w_f2', 'L0_cond_b_f2', 'L0_cond_w_ada',
        'L0_cond_b_ada', 'L0_attn_W_dq', 'L0_attn_W_uq', 'L0_attn_W_dkv', 'L0_attn_W_uk', 'L0_attn_W_uv', 'L0_attn_W_o',
        'L0_cond2_Wx', 'L0_cond2_Wh', 'L0_cond2_b', 'L0_ffn_w1', 'L0_ffn_b1', 'L0_ffn_w2', 'L0_ffn_b2']


def kernel(**inputs):
    import numpy as np
    import concourse.bacc as bacc
    from concourse.bass_utils import run_bass_kernel_spmd

    nc = bacc.Bacc("TRN2", target_bir_lowering=False, num_devices=1)
    arrays, args = {}, []
    for name in _INS:
        a = np.ascontiguousarray(inputs[name])
        arrays[f"in_{name}"] = a
        args.append(nc.dram_tensor(f"in_{name}", a.shape, mybir.dt.from_np(a.dtype), kind="ExternalInput").ap())
    args.append(nc.dram_tensor("out_y", (B, S, D), F32, kind="ExternalOutput").ap())
    adaln_attention_lstm_ffn(nc, *args)
    r = run_bass_kernel_spmd(nc, [arrays], core_ids=[0])
    return r.results[0]["out_y"]
```
